# Optimizing a Trainium2 kernel written in Bass

```python
import numpy as np
import jax
import jax.numpy as jnp

def _softmax(x, axis=-1):
    return jax.nn.softmax(x, axis=axis)

def _gelu(x):
    return jax.nn.gelu(x, approximate=True)

def _silu(x):
    return jax.nn.silu(x)

def _sigmoid(x):
    return jax.nn.sigmoid(x)

def _layernorm(x, axis=-1, eps=1e-05):
    m = jnp.mean(x, axis=axis, keepdims=True)
    v = jnp.var(x, axis=axis, keepdims=True)
    return (x - m) / jnp.sqrt(v + eps)

def _scatter_add(tgt, idx, src, axis=0):
    return tgt.at[idx].add(src)

def _segment_sum(src, seg, n):
    return jax.ops.segment_sum(src, seg, n)
kernel_name = 'mk_gnn_preln_d4_gnn_r16_dd00a3'

def setup_inputs(seed: int=0):
    np.random.seed(seed)
    _w = jnp.asarray

    def _rec_inputs():
        import jax
        import jax.numpy as jnp
        _gk = jax.random.key(seed)
        x = -0.0009044 + 1 * jax.random.normal(jax.random.fold_in(_gk, 1), (3125, 160), jnp.float32)
        src = jax.random.randint(jax.random.fold_in(_gk, 2), (100000,), 0, 3125, jnp.int32)
        dst = jnp.minimum((3125 * jax.random.uniform(jax.random.fold_in(_gk, 3), (100000,)) ** 2.0).astype(jnp.int32), 49999)
        _o = jnp.argsort(dst, stable=True)
        src = src[_o]
        dst = dst[_o]
        edge_attr_16 = -0.000191324 + 0.999809 * jax.random.normal(jax.random.fold_in(_gk, 12), (100000, 16), jnp.float32)
        edge_attr_3 = 0.00047201 + 1.00023 * jax.random.normal(jax.random.fold_in(_gk, 13), (100000, 3), jnp.float32)
        edge_attr_4 = -0.000414295 + 0.999828 * jax.random.normal(jax.random.fold_in(_gk, 14), (100000, 4), jnp.float32)
        edge_attr_64 = 0.000279952 + 1.00013 * jax.random.normal(jax.random.fold_in(_gk, 15), (100000, 64), jnp.float32)
        edge_attr_8 = jax.random.uniform(jax.random.fold_in(_gk, 16), (100000, 8), jnp.float32, 0.0, 1)
        node_vec1 = jax.random.uniform(jax.random.fold_in(_gk, 18), (3125, 1), jnp.float32, 0.0, 1)
        return (x, src, dst, edge_attr_16, edge_attr_3, edge_attr_4, edge_attr_64, edge_attr_8, node_vec1)
    x, src, dst, edge_attr_16, edge_attr_3, edge_attr_4, edge_attr_64, edge_attr_8, node_vec1 = _rec_inputs()

    def _L0_gnn_setup():
        import jax, jax.numpy as jnp
        import numpy as np
        N_NODES = 625
        N_EDGES = 20000
        MUL0, MUL1 = (64, 32)
        EDGE_DIM = 64
        W_NUMEL = 224
        DENOM = 32.0
        SQRT3 = 3.0 ** 0.5
        INV_SQRT3 = 1.0 / SQRT3
        INV_SQRT2 = 2.0 ** (-0.5)

        def _forward(node_feature, edge_attr, edge_feature, W_skip0, W_skip1, W_nl0, W_nl1, W_fc1, W_fc2, W_out_s, W_out_v, edge_index):
            N = node_feature.shape[0]
            E = edge_attr.shape[0]
            s = node_feature[:, :MUL0]
            v = node_feature[:, MUL0:].reshape(N, MUL1, 3)
            skip_s = s @ W_skip0
            skip_v = jnp.einsum('nmi,mk->nki', v, W_skip1)
            s = s @ W_nl0
            v = jnp.einsum('nmi,mk->nki', v, W_nl1)
            rhat = edge_attr / jnp.linalg.norm(edge_attr, axis=-1, keepdims=True)
            sh1 = SQRT3 * rhat
            w = jax.nn.relu(edge_feature @ W_fc1) @ W_fc2
            w0, w1, w2, w3, w4 = jnp.split(w, [64, 128, 160, 192], axis=-1)
            src, dst = (edge_index[0], edge_index[1])
            xs = s[dst]
            xv = v[dst]
            out0a = w0 * xs
            out0b = w3 * (jnp.einsum('emi,ei->em', xv, sh1) * INV_SQRT3)
            out1a = (w1 * xs)[:, :, None] * sh1[:, None, :]
            out1b = w2[:, :, None] * xv
            out1c = w4[:, :, None] * (jnp.cross(xv, sh1[:, None, :]) * INV_SQRT2)
            tp = jnp.concatenate([out0a, out0b, out1a.reshape(E, -1), out1b.reshape(E, -1), out1c.reshape(E, -1)], axis=-1)
            agg = jax.ops.segment_sum(tp, src, num_segments=N) / DENOM
            agg_s = agg[:, :96]
            agg_v = agg[:, 96:].reshape(N, 128, 3)
            out_s = agg_s @ W_out_s + skip_s
            out_v = jnp.einsum('nmi,mk->nki', agg_v, W_out_v) + skip_v
            fs = jax.nn.silu(out_s[:, :MUL0])
            gate = jax.nn.sigmoid(out_s[:, MUL0:MUL0 + 32])
            gv = gate[:, :, None] * out_v
            return jnp.concatenate([fs, gv.reshape(N, -1)], axis=-1)
        key = jax.random.key(seed)
        ks = jax.random.split(key, 12)

        def lin(k, fi, fo):
            return jax.random.normal(k, (fi, fo), jnp.float32) / np.float32(np.sqrt(fi))
        return {'node_feature': jax.random.normal(ks[0], (N_NODES, MUL0 + 3 * MUL1), jnp.float32), 'edge_attr': jax.random.normal(ks[1], (N_EDGES, 3), jnp.float32), 'edge_feature': jax.random.normal(ks[2], (N_EDGES, EDGE_DIM), jnp.float32), 'W_skip0': lin(ks[3], MUL0, 96), 'W_skip1': lin(ks[4], MUL1, 32), 'W_nl0': lin(ks[5], MUL0, MUL0), 'W_nl1': lin(ks[6], MUL1, MUL1), 'W_fc1': lin(ks[7], EDGE_DIM, 64), 'W_fc2': lin(ks[8], 64, W_NUMEL), 'W_out_s': lin(ks[9], 96, 96), 'W_out_v': lin(ks[10], 128, 32), 'edge_index': jax.random.randint(ks[11], (2, N_EDGES), 0, N_NODES)}
    _L0_gnn_all = _L0_gnn_setup()
    _L0_gnn_in = {k: v for k, v in _L0_gnn_all.items() if k in ('W_skip0', 'W_skip1', 'W_nl0', 'W_nl1', 'W_fc1', 'W_fc2', 'W_out_s', 'W_out_v')}
    del _L0_gnn_all

    def _L1_gnn_setup():
        import jax, jax.numpy as jnp
        import numpy as np
        N = 2500
        E = 25000
        MUL0, MUL1 = (64, 32)
        RAD, HID = (8, 64)
        WNUM = 192
        NUM_NEIGHBORS = 10.0
        INV3 = 1.0 / np.sqrt(3.0)

        def _lin(s, v, Ws, Wv, attr):
            out_s = s @ Ws * attr * (1.0 / np.sqrt(Ws.shape[0]))
            out_v = jnp.einsum('nud,uv->nvd', v, Wv) * attr[..., None] * (1.0 / np.sqrt(Wv.shape[0]))
            return (out_s, out_v)
        key = jax.random.key(seed)
        ks = jax.random.split(key, 16)
        return {'node_input': jax.random.normal(ks[0], (N, MUL0 + 3 * MUL1), jnp.float32), 'node_attr': jnp.ones((N, 1), jnp.float32), 'edge_attr': jax.random.normal(ks[1], (E, 4), jnp.float32), 'edge_scalars': jax.random.uniform(ks[2], (E, RAD), jnp.float32), 'W_sc_s': jax.random.normal(ks[3], (MUL0, MUL0), jnp.float32), 'W_sc_v': jax.random.normal(ks[4], (MUL1, MUL1), jnp.float32), 'W1_s': jax.random.normal(ks[5], (MUL0, MUL0), jnp.float32), 'W1_v': jax.random.normal(ks[6], (MUL1, MUL1), jnp.float32), 'W2_s': jax.random.normal(ks[7], (MUL0 + MUL1, MUL0), jnp.float32), 'W2_v': jax.random.normal(ks[8], (MUL0 + MUL1, MUL1), jnp.float32), 'W3': jax.random.normal(ks[9], (MUL0 + MUL1, 1), jnp.float32), 'fcW1': jax.random.normal(ks[10], (RAD, HID), jnp.float32), 'fcW2': jax.random.normal(ks[11], (HID, WNUM), jnp.float32), 'edge_src': jax.random.randint(ks[12], (E,), 0, N, jnp.int32), 'edge_dst': jax.random.randint(ks[13], (E,), 0, N, jnp.int32)}
    _L1_gnn_all = _L1_gnn_setup()
    _L1_gnn_in = {k: v for k, v in _L1_gnn_all.items() if k in ('W_sc_s', 'W_sc_v', 'W1_s', 'W1_v', 'W2_s', 'W2_v', 'W3', 'fcW1', 'fcW2')}
    del _L1_gnn_all

    def _L2_gnn_setup():
        import jax, jax.numpy as jnp
        import numpy as np
        N = 1250
        E = 20000
        MUL0 = 64
        MUL1 = 32
        FC_IN = 16
        FC_H = 64
        WNUM = 192
        key = jax.random.key(seed)
        ks = jax.random.split(key, 16)
        return {'x': jax.random.normal(ks[0], (N, MUL0 + 3 * MUL1), jnp.float32), 'node_attr': jnp.ones((N, 1), jnp.float32), 'edge_scalars': jax.random.normal(ks[1], (E, FC_IN), jnp.float32), 'edge_attr_sh': jax.random.normal(ks[2], (E, 4), jnp.float32), 'edge_src': jax.random.randint(ks[3], (E,), 0, N), 'edge_dst': jax.random.randint(ks[4], (E,), 0, N), 'Wfc1': jax.random.normal(ks[5], (FC_IN, FC_H), jnp.float32), 'Wfc2': jax.random.normal(ks[6], (FC_H, WNUM), jnp.float32), 'Wsc0': jax.random.normal(ks[7], (MUL0, MUL0), jnp.float32), 'Wsc1': jax.random.normal(ks[8], (MUL1, MUL1), jnp.float32), 'Wl1_0': jax.random.normal(ks[9], (MUL0, MUL0), jnp.float32), 'Wl1_1': jax.random.normal(ks[10], (MUL1, MUL1), jnp.float32), 'Wl2_s': jax.random.normal(ks[11], (MUL0 + MUL1, MUL0), jnp.float32), 'Wl2_v': jax.random.normal(ks[12], (MUL0 + MUL1, MUL1), jnp.float32), 'Wa': 0.1 * jax.random.normal(ks[13], (MUL0 + MUL1, 1), jnp.float32)}
    _L2_gnn_all = _L2_gnn_setup()
    _L2_gnn_in = {k: v for k, v in _L2_gnn_all.items() if k in ('Wfc1', 'Wfc2', 'Wsc0', 'Wsc1', 'Wl1_0', 'Wl1_1', 'Wl2_s', 'Wl2_v', 'Wa')}
    del _L2_gnn_all

    def _L3_gnn_setup():
        import jax, jax.numpy as jnp
        import numpy as np
        N, E = (1250, 20000)
        CS, CV = (64, 32)
        AS_, AV, H = (16, 8, 4)
        NB = 16
        SQRT3 = 1.7320508075688772
        SQRT2 = 1.4142135623730951
        EPS = 1e-05

        def _cg_tp(s, v, y0, y1, w_ss, w_sv, w_vs, w_vv0, w_vv1):
            out_s = jnp.concatenate([w_ss * s * y0[:, None], w_vv0 * (jnp.einsum('eci,ei->ec', v, y1) / SQRT3)], axis=-1)
            out_v = jnp.concatenate([(w_sv * s)[:, :, None] * y1[:, None, :], (w_vs * jnp.ones_like(v[..., 0]))[..., None] * v * y0[:, None, None], (w_vv1 * jnp.ones_like(v[..., 0]))[..., None] * (jnp.cross(v, y1[:, None, :]) / SQRT2)], axis=1)
            return (out_s, out_v)

        def _equiv_layernorm(s, v, gamma_s, beta_s, gamma_v):
            mu = jnp.mean(s, axis=-1, keepdims=True)
            var = jnp.var(s, axis=-1, keepdims=True)
            s_n = (s - mu) * jax.lax.rsqrt(var + EPS) * gamma_s + beta_s
            rms = jnp.sqrt(jnp.mean(jnp.sum(v * v, axis=-1), axis=-1, keepdims=True) + EPS)
            v_n = v / rms[..., None] * gamma_v[None, :, None]
            return (s_n, v_n)
        key = jax.random.key(seed)
        ks = jax.random.split(key, 26)

        def rn(k, shape, fan):
            return jax.random.normal(k, shape, jnp.float32) / np.sqrt(fan)
        D1S, D1V = (CS + CV, CS + 2 * CV)
        WN = 2 * CS + 3 * CV
        inp = {'node': jax.random.normal(ks[0], (N, CS + 3 * CV), jnp.float32), 'edge_index': jax.random.randint(ks[1], (2, E), 0, N, jnp.int64 if jax.config.jax_enable_x64 else jnp.int32), 'rbf': jax.random.uniform(ks[2], (E, NB), jnp.float32), 'rsh': jax.random.normal(ks[3], (E, 4), jnp.float32), 'gamma_s': jnp.ones((CS,), jnp.float32), 'beta_s': jnp.zeros((CS,), jnp.float32), 'gamma_v': jnp.ones((CV,), jnp.float32), 'Ws_src': rn(ks[4], (CS, CS), CS), 'Wv_src': rn(ks[5], (CV, CV), CV), 'Ws_dst': rn(ks[6], (CS, CS), CS), 'Wv_dst': rn(ks[7], (CV, CV), CV), 'W_rbf': rn(ks[8], (NB, WN), NB), 'W_alpha': rn(ks[9], (D1S, H * AS_), D1S), 'alpha_dot': rn(ks[10], (1, H, AS_), AS_), 'Ws_val': rn(ks[11], (D1S, CS), D1S), 'Wv_val': rn(ks[12], (D1V, CV), D1V), 'Wg': rn(ks[13], (CS, CV), CS), 'w2_ss': rn(ks[14], (CS,), 1), 'w2_sv': rn(ks[15], (CS,), 1), 'w2_vs': rn(ks[16], (CV,), 1), 'w2_vv0': rn(ks[17], (CV,), 1), 'w2_vv1': rn(ks[18], (CV,), 1), 'Ws_vlin': rn(ks[19], (D1S, H * AS_), D1S), 'Wv_vlin': rn(ks[20], (D1V, H * AV), D1V), 'Wps': rn(ks[21], (H * AS_, CS), H * AS_), 'Wpv': rn(ks[22], (H * AV, CV), H * AV)}
        return inp
    _L3_gnn_all = _L3_gnn_setup()
    _L3_gnn_in = {k: v for k, v in _L3_gnn_all.items() if k in ('gamma_s', 'beta_s', 'gamma_v', 'Ws_src', 'Wv_src', 'Ws_dst', 'Wv_dst', 'W_rbf', 'W_alpha', 'alpha_dot', 'Ws_val', 'Wv_val', 'Wg', 'w2_ss', 'w2_sv', 'w2_vs', 'w2_vv0', 'w2_vv1', 'Ws_vlin', 'Wv_vlin', 'Wps', 'Wpv')}
    del _L3_gnn_all
    return {'x': x, 'src': src, 'dst': dst, 'edge_attr_16': edge_attr_16, 'edge_attr_3': edge_attr_3, 'edge_attr_4': edge_attr_4, 'edge_attr_64': edge_attr_64, 'edge_attr_8': edge_attr_8, 'node_vec1': node_vec1, 'L0_gnn_W_skip0': _L0_gnn_in['W_skip0'], 'L0_gnn_W_skip1': _L0_gnn_in['W_skip1'], 'L0_gnn_W_nl0': _L0_gnn_in['W_nl0'], 'L0_gnn_W_nl1': _L0_gnn_in['W_nl1'], 'L0_gnn_W_fc1': _L0_gnn_in['W_fc1'], 'L0_gnn_W_fc2': _L0_gnn_in['W_fc2'], 'L0_gnn_W_out_s': _L0_gnn_in['W_out_s'], 'L0_gnn_W_out_v': _L0_gnn_in['W_out_v'], 'L1_gnn_W_sc_s': _L1_gnn_in['W_sc_s'], 'L1_gnn_W_sc_v': _L1_gnn_in['W_sc_v'], 'L1_gnn_W1_s': _L1_gnn_in['W1_s'], 'L1_gnn_W1_v': _L1_gnn_in['W1_v'], 'L1_gnn_W2_s': _L1_gnn_in['W2_s'], 'L1_gnn_W2_v': _L1_gnn_in['W2_v'], 'L1_gnn_W3': _L1_gnn_in['W3'], 'L1_gnn_fcW1': _L1_gnn_in['fcW1'], 'L1_gnn_fcW2': _L1_gnn_in['fcW2'], 'L2_gnn_Wfc1': _L2_gnn_in['Wfc1'], 'L2_gnn_Wfc2': _L2_gnn_in['Wfc2'], 'L2_gnn_Wsc0': _L2_gnn_in['Wsc0'], 'L2_gnn_Wsc1': _L2_gnn_in['Wsc1'], 'L2_gnn_Wl1_0': _L2_gnn_in['Wl1_0'], 'L2_gnn_Wl1_1': _L2_gnn_in['Wl1_1'], 'L2_gnn_Wl2_s': _L2_gnn_in['Wl2_s'], 'L2_gnn_Wl2_v': _L2_gnn_in['Wl2_v'], 'L2_gnn_Wa': _L2_gnn_in['Wa'], 'L3_gnn_gamma_s': _L3_gnn_in['gamma_s'], 'L3_gnn_beta_s': _L3_gnn_in['beta_s'], 'L3_gnn_gamma_v': _L3_gnn_in['gamma_v'], 'L3_gnn_Ws_src': _L3_gnn_in['Ws_src'], 'L3_gnn_Wv_src': _L3_gnn_in['Wv_src'], 'L3_gnn_Ws_dst': _L3_gnn_in['Ws_dst'], 'L3_gnn_Wv_dst': _L3_gnn_in['Wv_dst'], 'L3_gnn_W_rbf': _L3_gnn_in['W_rbf'], 'L3_gnn_W_alpha': _L3_gnn_in['W_alpha'], 'L3_gnn_alpha_dot': _L3_gnn_in['alpha_dot'], 'L3_gnn_Ws_val': _L3_gnn_in['Ws_val'], 'L3_gnn_Wv_val': _L3_gnn_in['Wv_val'], 'L3_gnn_Wg': _L3_gnn_in['Wg'], 'L3_gnn_w2_ss': _L3_gnn_in['w2_ss'], 'L3_gnn_w2_sv': _L3_gnn_in['w2_sv'], 'L3_gnn_w2_vs': _L3_gnn_in['w2_vs'], 'L3_gnn_w2_vv0': _L3_gnn_in['w2_vv0'], 'L3_gnn_w2_vv1': _L3_gnn_in['w2_vv1'], 'L3_gnn_Ws_vlin': _L3_gnn_in['Ws_vlin'], 'L3_gnn_Wv_vlin': _L3_gnn_in['Wv_vlin'], 'L3_gnn_Wps': _L3_gnn_in['Wps'], 'L3_gnn_Wpv': _L3_gnn_in['Wpv']}

def reference(x, src, dst, edge_attr_16, edge_attr_3, edge_attr_4, edge_attr_64, edge_attr_8, node_vec1, L0_gnn_W_skip0, L0_gnn_W_skip1, L0_gnn_W_nl0, L0_gnn_W_nl1, L0_gnn_W_fc1, L0_gnn_W_fc2, L0_gnn_W_out_s, L0_gnn_W_out_v, L1_gnn_W_sc_s, L1_gnn_W_sc_v, L1_gnn_W1_s, L1_gnn_W1_v, L1_gnn_W2_s, L1_gnn_W2_v, L1_gnn_W3, L1_gnn_fcW1, L1_gnn_fcW2, L2_gnn_Wfc1, L2_gnn_Wfc2, L2_gnn_Wsc0, L2_gnn_Wsc1, L2_gnn_Wl1_0, L2_gnn_Wl1_1, L2_gnn_Wl2_s, L2_gnn_Wl2_v, L2_gnn_Wa, L3_gnn_gamma_s, L3_gnn_beta_s, L3_gnn_gamma_v, L3_gnn_Ws_src, L3_gnn_Wv_src, L3_gnn_Ws_dst, L3_gnn_Wv_dst, L3_gnn_W_rbf, L3_gnn_W_alpha, L3_gnn_alpha_dot, L3_gnn_Ws_val, L3_gnn_Wv_val, L3_gnn_Wg, L3_gnn_w2_ss, L3_gnn_w2_sv, L3_gnn_w2_vs, L3_gnn_w2_vv0, L3_gnn_w2_vv1, L3_gnn_Ws_vlin, L3_gnn_Wv_vlin, L3_gnn_Wps, L3_gnn_Wpv):
    import jax
    import jax.numpy as jnp

    def _L0_gnn_ref(node_feature, edge_attr, edge_feature, W_skip0, W_skip1, W_nl0, W_nl1, W_fc1, W_fc2, W_out_s, W_out_v, edge_index):
        import jax, jax.numpy as jnp
        import numpy as np
        N_NODES = 625
        N_EDGES = 20000
        MUL0, MUL1 = (64, 32)
        EDGE_DIM = 64
        W_NUMEL = 224
        DENOM = 32.0
        SQRT3 = 3.0 ** 0.5
        INV_SQRT3 = 1.0 / SQRT3
        INV_SQRT2 = 2.0 ** (-0.5)

        def _forward(node_feature, edge_attr, edge_feature, W_skip0, W_skip1, W_nl0, W_nl1, W_fc1, W_fc2, W_out_s, W_out_v, edge_index):
            N = node_feature.shape[0]
            E = edge_attr.shape[0]
            s = node_feature[:, :MUL0]
            v = node_feature[:, MUL0:].reshape(N, MUL1, 3)
            skip_s = s @ W_skip0
            skip_v = jnp.einsum('nmi,mk->nki', v, W_skip1)
            s = s @ W_nl0
            v = jnp.einsum('nmi,mk->nki', v, W_nl1)
            rhat = edge_attr / jnp.linalg.norm(edge_attr, axis=-1, keepdims=True)
            sh1 = SQRT3 * rhat
            w = jax.nn.relu(edge_feature @ W_fc1) @ W_fc2
            w0, w1, w2, w3, w4 = jnp.split(w, [64, 128, 160, 192], axis=-1)
            src, dst = (edge_index[0], edge_index[1])
            xs = s[dst]
            xv = v[dst]
            out0a = w0 * xs
            out0b = w3 * (jnp.einsum('emi,ei->em', xv, sh1) * INV_SQRT3)
            out1a = (w1 * xs)[:, :, None] * sh1[:, None, :]
            out1b = w2[:, :, None] * xv
            out1c = w4[:, :, None] * (jnp.cross(xv, sh1[:, None, :]) * INV_SQRT2)
            tp = jnp.concatenate([out0a, out0b, out1a.reshape(E, -1), out1b.reshape(E, -1), out1c.reshape(E, -1)], axis=-1)
            agg = jax.ops.segment_sum(tp, src, num_segments=N) / DENOM
            agg_s = agg[:, :96]
            agg_v = agg[:, 96:].reshape(N, 128, 3)
            out_s = agg_s @ W_out_s + skip_s
            out_v = jnp.einsum('nmi,mk->nki', agg_v, W_out_v) + skip_v
            fs = jax.nn.silu(out_s[:, :MUL0])
            gate = jax.nn.sigmoid(out_s[:, MUL0:MUL0 + 32])
            gv = gate[:, :, None] * out_v
            return jnp.concatenate([fs, gv.reshape(N, -1)], axis=-1)
        return _forward(node_feature, edge_attr, edge_feature, W_skip0, W_skip1, W_nl0, W_nl1, W_fc1, W_fc2, W_out_s, W_out_v, edge_index)

    def _L1_gnn_ref(node_input, node_attr, edge_attr, edge_scalars, W_sc_s, W_sc_v, W1_s, W1_v, W2_s, W2_v, W3, fcW1, fcW2, edge_src, edge_dst):
        import jax, jax.numpy as jnp
        import numpy as np
        N = 2500
        E = 25000
        MUL0, MUL1 = (64, 32)
        RAD, HID = (8, 64)
        WNUM = 192
        NUM_NEIGHBORS = 10.0
        INV3 = 1.0 / np.sqrt(3.0)

        def _lin(s, v, Ws, Wv, attr):
            out_s = s @ Ws * attr * (1.0 / np.sqrt(Ws.shape[0]))
            out_v = jnp.einsum('nud,uv->nvd', v, Wv) * attr[..., None] * (1.0 / np.sqrt(Wv.shape[0]))
            return (out_s, out_v)
        n = node_input.shape[0]
        s_in = node_input[:, :MUL0]
        v_in = node_input[:, MUL0:].reshape(n, MUL1, 3)
        sc_s, sc_v = _lin(s_in, v_in, W_sc_s, W_sc_v, node_attr)
        f_s, f_v = _lin(s_in, v_in, W1_s, W1_v, node_attr)
        h = jax.nn.silu(edge_scalars @ fcW1 * (1.0 / np.sqrt(RAD)))
        w = h @ fcW2 * (1.0 / np.sqrt(HID))
        wA, wB, wC, wD = (w[:, :64], w[:, 64:128], w[:, 128:160], w[:, 160:192])
        xs = f_s[edge_src]
        xv = f_v[edge_src]
        y0 = edge_attr[:, :1]
        y1 = edge_attr[:, 1:4]
        outA = wA * xs * y0
        outD = wD * jnp.einsum('eud,ed->eu', xv, y1) * INV3
        outB = wB[:, :, None] * xs[:, :, None] * y1[:, None, :]
        outC = wC[:, :, None] * xv * y0[:, :, None]
        edge_feat = jnp.concatenate([outA, outD, outB.reshape(-1, MUL0 * 3), outC.reshape(-1, MUL1 * 3)], axis=1)
        agg = jax.ops.segment_sum(edge_feat, edge_dst, num_segments=n)
        agg = agg * (1.0 / np.sqrt(NUM_NEIGHBORS))
        ms = agg[:, :MUL0 + MUL1]
        mv = agg[:, MUL0 + MUL1:].reshape(n, MUL0 + MUL1, 3)
        c_s, c_v = _lin(ms, mv, W2_s, W2_v, node_attr)
        conv = jnp.concatenate([c_s, c_v.reshape(n, -1)], axis=1)
        sc = jnp.concatenate([sc_s, sc_v.reshape(n, -1)], axis=1)
        angle = 0.1 * (ms @ W3) * node_attr * (1.0 / np.sqrt(MUL0 + MUL1))
        cos, sin = (jnp.cos(angle), jnp.sin(angle))
        return cos * sc + sin * conv

    def _L2_gnn_ref(x, node_attr, edge_scalars, edge_attr_sh, edge_src, edge_dst, Wfc1, Wfc2, Wsc0, Wsc1, Wl1_0, Wl1_1, Wl2_s, Wl2_v, Wa):
        import jax, jax.numpy as jnp
        import numpy as np
        N = 1250
        E = 20000
        MUL0 = 64
        MUL1 = 32
        FC_IN = 16
        FC_H = 64
        WNUM = 192
        n = x.shape[0]
        x0 = x[:, :MUL0]
        x1 = x[:, MUL0:].reshape(n, MUL1, 3)
        a = node_attr
        h = jax.nn.silu(edge_scalars @ (Wfc1 / jnp.sqrt(jnp.float32(FC_IN))))
        w = h @ (Wfc2 / jnp.sqrt(jnp.float32(FC_H)))
        w0 = w[:, :64]
        w1 = w[:, 64:128]
        w2 = w[:, 128:160]
        w3 = w[:, 160:192]
        inv8 = 1.0 / jnp.sqrt(jnp.float32(MUL0))
        inv32 = 1.0 / jnp.sqrt(jnp.float32(MUL1))
        sc = jnp.concatenate([x0 @ Wsc0 * a * inv8, (jnp.einsum('num,uv->nvm', x1, Wsc1) * a[..., None] * inv32).reshape(n, 3 * MUL1)], axis=1)
        f0 = x0 @ Wl1_0 * a * inv8
        f1 = jnp.einsum('num,uv->nvm', x1, Wl1_1) * a[..., None] * inv32
        e0 = f0[edge_src]
        e1 = f1[edge_src]
        sh0 = edge_attr_sh[:, :1]
        sh1 = edge_attr_sh[:, 1:4]
        mid0 = w0 * e0 * sh0
        mid1 = w3 * jnp.einsum('eum,em->eu', e1, sh1) / jnp.sqrt(3.0)
        mid2 = w1[:, :, None] * e0[:, :, None] * sh1[:, None, :]
        mid3 = w2[:, :, None] * e1 * sh0[:, :, None]
        cnt = jnp.clip(jax.ops.segment_sum(jnp.ones(edge_dst.shape, x.dtype), edge_dst, num_segments=n), 1.0)

        def smean(v):
            s = jax.ops.segment_sum(v, edge_dst, num_segments=n)
            return s / cnt.reshape((n,) + (1,) * (v.ndim - 1))
        n0, n1 = (smean(mid0), smean(mid1))
        n2, n3 = (smean(mid2), smean(mid3))
        scal = jnp.concatenate([n0, n1], axis=1)
        vec = jnp.concatenate([n2, n3], axis=1)
        inv96 = 1.0 / jnp.sqrt(jnp.float32(MUL0 + MUL1))
        alpha = scal @ Wa * a * inv96
        out_s = scal @ Wl2_s * a * inv96
        out_v = jnp.einsum('num,uv->nvm', vec, Wl2_v) * a[..., None] * inv96
        conv = jnp.concatenate([out_s, out_v.reshape(n, 3 * MUL1)], axis=1)
        return sc + alpha * conv

    def _L3_gnn_ref(node, rbf, rsh, gamma_s, beta_s, gamma_v, Ws_src, Wv_src, Ws_dst, Wv_dst, W_rbf, W_alpha, alpha_dot, Ws_val, Wv_val, Wg, w2_ss, w2_sv, w2_vs, w2_vv0, w2_vv1, Ws_vlin, Wv_vlin, Wps, Wpv, edge_index):
        import jax, jax.numpy as jnp
        import numpy as np
        N, E = (1250, 20000)
        CS, CV = (64, 32)
        AS_, AV, H = (16, 8, 4)
        NB = 16
        SQRT3 = 1.7320508075688772
        SQRT2 = 1.4142135623730951
        EPS = 1e-05

        def _cg_tp(s, v, y0, y1, w_ss, w_sv, w_vs, w_vv0, w_vv1):
            out_s = jnp.concatenate([w_ss * s * y0[:, None], w_vv0 * (jnp.einsum('eci,ei->ec', v, y1) / SQRT3)], axis=-1)
            out_v = jnp.concatenate([(w_sv * s)[:, :, None] * y1[:, None, :], (w_vs * jnp.ones_like(v[..., 0]))[..., None] * v * y0[:, None, None], (w_vv1 * jnp.ones_like(v[..., 0]))[..., None] * (jnp.cross(v, y1[:, None, :]) / SQRT2)], axis=1)
            return (out_s, out_v)

        def _equiv_layernorm(s, v, gamma_s, beta_s, gamma_v):
            mu = jnp.mean(s, axis=-1, keepdims=True)
            var = jnp.var(s, axis=-1, keepdims=True)
            s_n = (s - mu) * jax.lax.rsqrt(var + EPS) * gamma_s + beta_s
            rms = jnp.sqrt(jnp.mean(jnp.sum(v * v, axis=-1), axis=-1, keepdims=True) + EPS)
            v_n = v / rms[..., None] * gamma_v[None, :, None]
            return (s_n, v_n)
        n = node.shape[0]
        e = rsh.shape[0]
        s = node[:, :CS]
        v = node[:, CS:].reshape(n, CV, 3)
        s_n, v_n = _equiv_layernorm(s, v, gamma_s, beta_s, gamma_v)
        src, dst = (edge_index[0], edge_index[1])
        msg_s = (s_n @ Ws_src)[src] + (s_n @ Ws_dst)[dst]
        msg_v = jnp.einsum('ncx,cd->ndx', v_n, Wv_src)[src] + jnp.einsum('ncx,cd->ndx', v_n, Wv_dst)[dst]
        y0, y1 = (rsh[:, 0], rsh[:, 1:4])
        w1 = rbf @ W_rbf
        m1_s, m1_v = _cg_tp(msg_s, msg_v, y0, y1, w1[:, :CS], w1[:, CS:2 * CS], w1[:, 2 * CS:2 * CS + CV], w1[:, 2 * CS + CV:2 * CS + 2 * CV], w1[:, 2 * CS + 2 * CV:])
        a = (m1_s @ W_alpha).reshape(e, H, AS_)
        a = jnp.where(a > 0, a, 0.2 * a)
        a = jnp.sum(a * alpha_dot, axis=-1, keepdims=True)
        amax = jax.ops.segment_max(a, dst, num_segments=n)
        amax = jnp.where(jnp.isfinite(amax), amax, 0.0)
        ex = jnp.exp(a - amax[dst])
        den = jax.ops.segment_sum(ex, dst, num_segments=n)
        alpha = ex / (den[dst] + 1e-16)
        val_s = m1_s @ Ws_val
        val_v = jnp.einsum('ecx,cd->edx', m1_v, Wv_val)
        val_v = val_v * jax.nn.sigmoid(val_s @ Wg)[..., None]
        val_s = jax.nn.sigmoid(val_s)
        m2_s, m2_v = _cg_tp(val_s, val_v, y0, y1, w2_ss, w2_sv, w2_vs, w2_vv0, w2_vv1)
        hs = (m2_s @ Ws_vlin).reshape(e, H, AS_)
        hv = jnp.einsum('ecx,cd->edx', m2_v, Wv_vlin).reshape(e, H, AV, 3)
        h = jnp.concatenate([hs, hv.reshape(e, H, AV * 3)], axis=-1)
        agg = jax.ops.segment_sum(alpha * h, dst, num_segments=n)
        agg_s = agg[:, :, :AS_].reshape(n, H * AS_)
        agg_v = agg[:, :, AS_:].reshape(n, H * AV, 3)
        out = node + jnp.concatenate([agg_s @ Wps, jnp.einsum('ncx,cd->ndx', agg_v, Wpv).reshape(n, CV * 3)], axis=-1)
        return out
    edge_index = jnp.stack([src, dst])
    h = jnp.maximum(_layernorm(x, axis=-1), 0.0)
    x = x + _L0_gnn_ref(h, edge_attr_3, edge_attr_64, L0_gnn_W_skip0, L0_gnn_W_skip1, L0_gnn_W_nl0, L0_gnn_W_nl1, L0_gnn_W_fc1, L0_gnn_W_fc2, L0_gnn_W_out_s, L0_gnn_W_out_v, edge_index)
    h = jnp.maximum(_layernorm(x, axis=-1), 0.0)
    x = x + _L1_gnn_ref(h, node_vec1, edge_attr_4, edge_attr_8, L1_gnn_W_sc_s, L1_gnn_W_sc_v, L1_gnn_W1_s, L1_gnn_W1_v, L1_gnn_W2_s, L1_gnn_W2_v, L1_gnn_W3, L1_gnn_fcW1, L1_gnn_fcW2, src, dst)
    h = jnp.maximum(_layernorm(x, axis=-1), 0.0)
    x = x + _L2_gnn_ref(h, node_vec1, edge_attr_16, edge_attr_4, src, dst, L2_gnn_Wfc1, L2_gnn_Wfc2, L2_gnn_Wsc0, L2_gnn_Wsc1, L2_gnn_Wl1_0, L2_gnn_Wl1_1, L2_gnn_Wl2_s, L2_gnn_Wl2_v, L2_gnn_Wa)
    h = jnp.maximum(_layernorm(x, axis=-1), 0.0)
    x = x + _L3_gnn_ref(h, edge_attr_16, edge_attr_4, L3_gnn_gamma_s, L3_gnn_beta_s, L3_gnn_gamma_v, L3_gnn_Ws_src, L3_gnn_Wv_src, L3_gnn_Ws_dst, L3_gnn_Wv_dst, L3_gnn_W_rbf, L3_gnn_W_alpha, L3_gnn_alpha_dot, L3_gnn_Ws_val, L3_gnn_Wv_val, L3_gnn_Wg, L3_gnn_w2_ss, L3_gnn_w2_sv, L3_gnn_w2_vs, L3_gnn_w2_vv0, L3_gnn_w2_vv1, L3_gnn_Ws_vlin, L3_gnn_Wv_vlin, L3_gnn_Wps, L3_gnn_Wpv, edge_index)
    return x

_drawn_inputs = setup_inputs


def setup_inputs(seed=0):
    import zlib

    import numpy as np

    out = dict(_drawn_inputs(seed))
    spreads = {'L3_gnn_gamma_s': (1.0, 0.2), 'L3_gnn_beta_s': (0.0, 0.1), 'L3_gnn_gamma_v': (1.0, 0.2)}
    factors = {}
    for name, (base, spread) in spreads.items():
        noise = np.random.default_rng([zlib.crc32(name.encode()), seed]).standard_normal(out[name].shape)
        drawn = base * np.exp(spread * noise) if base else spread * noise
        out[name] = jnp.asarray(drawn.astype(out[name].dtype))
    for name, factor in factors.items():
        out[name] = (out[name] * factor).astype(out[name].dtype)
    return out
```

```python
import math
from contextlib import ExitStack

import concourse.bass as bass
from concourse import mybir

ALU = mybir.AluOpType
ACT = mybir.ActivationFunctionType
AX = mybir.AxisListType.X
F32 = mybir.dt.float32
I32 = mybir.dt.int32

P = 128
NODES, DIM = 3125, 160
SLOTS = 25
ROWS = P * SLOTS
TABLE_ROWS = ROWS + P
EDGES = 100000
TILES = 784
GROUP = 4
GROUPS = TILES // GROUP
QT, QK = 112, 7
PAD_NODE = ROWS - 1
S, V = 64, 32
CHAINS = 4
BIG = 1.0e38

SPEC = {
    0: dict(k=64, w=224, f=480, vec=128, table=224, out_s=96, skip=192),
    1: dict(k=8, w=192, f=384, vec=96, table=160, out_s=64, skip=160),
    2: dict(k=16, w=192, f=384, vec=96, table=160, out_s=64, skip=160),
    3: dict(k=16, w=224, f=164, vec=32, table=160, out_s=64, skip=160),
}


class Steps:

    def __init__(self):
        self.n = 0

    def step(self):
        self.n += 1
        return 1

    def reset(self):
        n, self.n = self.n, 0
        return -n


def pipelined(eng, count, stages):
    ahead, behind = min(lag for lag, _ in stages), max(lag for lag, _ in stages)
    lo = behind + 2
    lo += lo % 2
    hi = (count + ahead) // 2 * 2

    def step(i, parity):
        for lag, stage in stages:
            if isinstance(i, int) and parity is None:
                if 0 <= i - lag < count:
                    stage(i - lag, (i - lag) % 2, i - lag < 2, (i - lag) // 2)
            else:
                stage(i * 2 + (parity - lag), (parity - lag) % 2, False, i + (parity - lag) // 2)

    for i in range(ahead, lo):
        step(i, None)
    with eng.Fori(lo // 2, hi // 2) as it:
        for parity in range(2):
            step(it, parity)
    for i in range(hi, count + behind):
        step(i, None)


def build(nc, a, out, layers=(0, 1, 2, 3)):
    with ExitStack() as ctx:
        def sb(name, shape, dt=F32):
            return ctx.enter_context(nc.sbuf_tensor(name, shape, dt))

        def sem(name):
            return ctx.enter_context(nc.semaphore(name))

        def dram(name, shape, dt=F32):
            return nc.dram_tensor(name, shape, dt, kind="Internal").ap()

        node_table = {l: dram(f"node_table{l}", (ROWS, SPEC[l]["table"])) for l in (0, 1, 2)}
        src_table = dram("src_table", (ROWS, DIM))
        dst_table = dram("dst_table", (ROWS, DIM))
        src_sum = [dram(f"src_sum{c}", (TABLE_ROWS, SPEC[0]["f"])) for c in range(CHAINS)]
        run_rows = {l: dram(f"run_rows{l}", (TILES * P, SPEC[l]["f"])) for l in (1, 2, 3)}
        carry = {l: dram(f"carry{l}", (TABLE_ROWS, SPEC[l]["f"])) for l in (1, 2, 3)}
        edge_h = dram("edge_h", (TILES * P, DIM))
        ends = dram("ends", (ROWS + 1, 1))

        x = sb("x", [P, SLOTS, DIM])
        skip = sb("skip", [P, SLOTS, 192])
        fore = sb("fore", [P, SLOTS * 224])
        attr = sb("attr", [P, SLOTS])
        y = sb("y", [P, TILES, 6])
        aux = sb("aux", [P, TILES, 5])
        src_i = sb("src_i", [P, TILES], I32)
        dst_i = sb("dst_i", [P, TILES], I32)
        src_f = sb("src_f", [P, TILES])
        dst_f = sb("dst_f", [P, TILES])
        put_i = sb("put_i", [P, TILES], I32)
        ident = sb("ident", [P, P])
        lower = sb("lower", [P, P])
        spare = sb("spare", [P, 1])
        stats = sb("stats", [P, 12, SLOTS])
        last_i = sb("last_i", [P, SLOTS], I32)
        rcnt = sb("rcnt", [P, SLOTS])
        has = sb("has", [P, SLOTS])
        sel2 = sb("sel2", [QT, QK, QT])
        put2_i = sb("put2_i", [QT, QK], I32)
        work = sb("work", [P, 18432])

        def carve():
            at = [0]

            def get(*dims, dt=F32):
                n = math.prod(dims)
                n += n % 2
                assert at[0] + n <= 18432, (at[0], n)
                v = work[:, at[0]:at[0] + n]
                at[0] += n
                v = v[:, 0:math.prod(dims)]
                if dt != F32:
                    v = v.bitcast(dt)
                if len(dims) == 1:
                    return v
                names = " ".join(f"d{i}" for i in range(len(dims)))
                return v.rearrange(f"p ({names}) -> p {names}", **{f"d{i}": d for i, d in enumerate(dims)})

            return get

        bank = ctx.enter_context(nc.psum_tensor("bank", [P, 8, 512], F32))

        wt = {}

        def weight(name, rows, cols):
            wt[name] = sb("w_" + name, [rows, cols])

        weight("fc1_0", 64, 64)
        weight("fc2_0", 64, 224)
        weight("fc1_1", 8, 64)
        weight("fc2_1", 64, 192)
        weight("fc1_2", 16, 64)
        weight("fc2_2", 64, 192)
        weight("rbf", 16, 224)
        for l in range(4):
            weight(f"f_s{l}", 64, 64)
            weight(f"f_v{l}", 32, 32)
            weight(f"k_s{l}", 64, 96 if l == 0 else 64)
            weight(f"k_v{l}", 32, 32)
        weight("out_s0", 96, 96)
        weight("out_v0", 128, 32)
        for l in (1, 2):
            weight(f"out_s{l}", 96, 64)
            weight(f"out_v{l}", 96, 32)
            weight(f"out_a{l}", 96, 1)
        weight("out_s3", 64, 64)
        weight("out_v3", 32, 32)
        weight("val_s", 96, 128)
        weight("val_x", 128, 64)
        weight("val_yz", 128, 64)
        weight("gate", 64, 32)
        weight("lin_s", 96, 64)
        weight("lin_x", 128, 64)
        weight("lin_yz", 128, 64)
        gamma_s = sb("gamma_s", [64, 1])
        beta_s = sb("beta_s", [64, 1])
        gamma_v = sb("gamma_v", [32, 1])
        alpha_dot = sb("alpha_dot", [P, 64])
        w2 = sb("w2", [P, 3])

        phase = sem("phase")
        dve_own, act_own, pool_own = sem("dve_own"), sem("act_own"), sem("pool_own")
        loaded, zero_made, zeroed = sem("loaded"), sem("zero_made"), sem("zeroed")
        moved = sem("moved")
        weights_in = sem("weights_in")
        one = {n: sem(n) for n in (
            "node_in", "node_t", "node_tsb", "node_mm", "node_free", "carry_in0", "carry_in1", "sum_free",
            "row_in0", "row_in1", "sum_ready", "table_in",
            "attr_in0", "attr_in1", "attr_free", "key_in0", "key_in1", "key_free", "hid_mm", "hid_ready",
            "hid_free", "w_ready", "w_free", "got_free", "msg_ready", "msg_free", "run_mm", "run_free",
            "run_ready", "run_room", "put_ready",
            "store0", "store1", "f_ready", "t1_mm", "t1_ready", "c1_mm", "c1_free", "vt_ready", "vt_mm",
            "vtsb_ready", "gate_mm", "gate_ready", "f2_ready", "t2_mm", "t2_ready", "c2_mm", "c2_free",
            "hs_ready", "h_ready", "c2nd_mm", "c2nd_sb", "c2nd_in",
            "root_asked", "root_done", "scan_t", "scan_sb", "scan_mm", "scan_free")}
        keys_got = [sem(f"keys_got{b}") for b in range(2)]
        got = {l: [sem(f"got{l}_{b}") for b in range(2)] for l in range(4)}
        rows_got = {l: [sem(f"rows_got{l}_{b}") for b in range(2)] for l in (1, 2, 3)}
        carried = {l: sem(f"carried{l}") for l in (1, 2, 3)}
        put = [sem(f"put{c}") for c in range(CHAINS)]
        s = type("Signals", (), one)

        block = ctx.enter_context(nc.Block())
        phases = {"n": {}}

        def barrier(eng, name):
            n = phases["n"][name] = phases["n"].get(name, 0) + 1
            eng.drain().then_inc(phase, 1)
            eng.wait_ge(phase, 5 * n)

        def edge_views():
            g = carve()
            v = type("Edge", (), {})
            v.attr = g(2, 512)
            v.keys = g(2, 512, dt=I32)
            v.hid = g(2, 512)
            v.got = g(2, GROUP * 224)
            v.msg = g(2, GROUP * 544)
            v.sel = g(2, GROUP, P)
            v.run = g(2, GROUP * 480)
            v.t0, v.t1, v.t2 = g(GROUP * 160), g(GROUP * 96), g(GROUP * 96)
            v.first = g(P)
            v.idx = g(2, GROUP, dt=I32)
            v.pidx = g(2, GROUP, dt=I32)
            v.cnt = g(GROUP)
            v.pos = g(GROUP)
            return v

        E = edge_views()

        def node_views():
            g = carve()
            v = type("Node", (), {})
            v.h = g(2, DIM)
            v.hT = g(2, 4, P)
            v.big = g(SLOTS * DIM)
            v.row = g(2, 480)
            v.car = g(2, 4 * 480)
            v.sum = g(2, 480)
            v.c2 = g(480)
            v.c2in = g(480)
            v.idx = g(2, 2, dt=I32)
            v.small = g(8, SLOTS)
            v.smi = g(SLOTS, dt=I32)
            v.rden = g(8)
            return v

        Nv = node_views()

        def l3_views():
            g = carve()
            v = type("L3", (), {})
            v.rb = g(2, 256)
            v.gs, v.gd = g(2, 2, DIM), g(2, 2, DIM)
            v.m, v.my0 = g(2, DIM), g(2, DIM)
            v.f, v.f2 = g(2, 2, 352), g(2, 2, 352)
            v.t1, v.t2 = g(2, 2, 384), g(2, 2, 384)
            v.al, v.vs = g(2, 2, 64), g(2, 2, 64)
            v.al2 = g(2, 64)
            v.vT = g(2, 2, P)
            v.gate = g(2, 2, V)
            v.vv = g(2, 3, V)
            v.q, v.u1, v.u2 = g(2, 96), g(2, 96), g(2, 96)
            v.h = g(2, 2, DIM)
            v.idx = g(2, 2, 2, dt=I32)
            return v

        T = l3_views()

        def pass2_views():
            g = carve()
            v = type("Pass2", (), {})
            v.keys = g(2, 512, dt=I32)
            v.h = g(2, GROUP * DIM)
            v.msg = g(2, GROUP * 164)
            v.sel = g(2, GROUP, P)
            v.run = g(2, GROUP * 164)
            return v

        P2 = pass2_views()

        def scan_views():
            g = carve()
            v = type("Scan", (), {})
            v.aT = g(QK, 4, P)
            v.bw = g(4, P)
            v.fw = g(QK, 4, P)
            v.kI = g(QK, P, dt=I32)
            v.k = g(QK, P)
            v.b = g(P)
            v.b2 = g(P)
            v.edge = g(QK, 4, 2)
            v.lk, v.fk = g(TILES), g(TILES)
            v.lkI, v.fkI = g(TILES, dt=I32), g(TILES, dt=I32)
            v.m = g(2, TILES)
            v.j = g(2, TILES)
            v.c = g(2, TILES)
            v.cT = g(QK, 2, 4)
            return v

        C = scan_views()

        def setup_views():
            g = carve()
            v = type("Setup", (), {})
            v.lkI, v.nfI = g(TILES, dt=I32), g(TILES, dt=I32)
            v.lk, v.nf, v.t, v.j, v.one = g(TILES), g(TILES), g(TILES), g(TILES), g(TILES)
            v.e3 = g(TILES * 3)
            v.n2 = g(TILES)
            v.rowI = g(2, P, dt=I32)
            v.tile_i = g(SLOTS, dt=I32)
            v.node = g(SLOTS)
            v.node_i = g(SLOTS, dt=I32)
            v.tiles = g(SLOTS)
            v.in_tile = g(SLOTS)
            v.end = g(SLOTS)
            v.prev = g(SLOTS)
            v.lkc_i, v.nfc_i = g(QK, dt=I32), g(QK, dt=I32)
            v.lkc, v.nfc, v.tc, v.cc, v.kc = g(QK), g(QK), g(QK), g(QK), g(QK)
            v.zero = g(480)
            return v

        U = setup_views()

        def group_rows(d, width, per):
            return d.rearrange("(g t p) f -> g p t f", t=per, p=P)

        def wmm(k):
            return bank[:, 1 + 2 * k:3 + 2 * k, :].rearrange("p b (t c) -> p (b t) c", c=256)

        @block.sync
        def _(sp):
            n = 0

            def load(dst, src):
                nonlocal n
                sp.dma_start(dst, src).then_inc(loaded, 16)
                n += 16

            load(x[:], a["x"].rearrange("(p j) c -> p j c", j=SLOTS))
            load(attr[:], a["node_vec1"])
            load(src_i[:], a["src"])
            load(dst_i[:], a["dst"])
            load(U.lkI, a["tile_last"].partition_broadcast(P))
            load(U.nfI, a["next_first"].partition_broadcast(P))
            load(U.lkc_i[0:QT], a["last_col"])
            load(U.nfc_i[0:QT], a["next_col"])
            load(U.e3, a["edge_attr_3"])
            load(aux[:, :, 0:4], a["edge_attr_4"])
            assert n == LOADS
            sp.wait_ge(zero_made, 1)
            for table in ([*src_sum] if 0 in layers else []) + [carry[l] for l in (1, 2, 3) if l in layers]:
                width = table.shape[1]
                sp.dma_start(table.rearrange("(p r) f -> p r f", p=P),
                             U.zero[:, 0:width].unsqueeze(1).broadcast_to([P, TABLE_ROWS // P, width])).then_inc(zeroed, 16)
            sp.wait_ge(zeroed, 16 * ((CHAINS if 0 in layers else 0) + len([l for l in layers if l])))
            sp.wait_ge(s.table_in, 1)
            sp.sem_inc(s.table_in, -1)
            sp.dma_start(ends[1:ROWS + 1].rearrange("(p j) o -> p (j o)", j=SLOTS), U.end).then_inc(moved, 16)
            sp.dma_start(ends[0:1], U.zero[0:1, 0:1]).then_inc(moved, 16)
            sp.wait_ge(moved, 32)
            sp.dma_start(U.prev, ends[0:ROWS].rearrange("(p j) o -> p (j o)", j=SLOTS)).then_inc(moved, 16)
            barrier(sp, "sp")

            def table_out(l):
                sp.wait_ge(s.table_in, 1)
                sp.sem_inc(s.table_in, -1)
                if l < 3:
                    sp.dma_start(node_table[l].rearrange("(p j) c -> p (j c)", j=SLOTS),
                                 fore[:, 0:SLOTS * SPEC[l]["table"]]).then_inc(s.carry_in0, 16)
                    sp.wait_ge(s.carry_in0, 16)
                    sp.sem_inc(s.carry_in0, -16)
                else:
                    sp.dma_start(src_table.rearrange("(p j) c -> p (j c)", j=SLOTS),
                                 fore[:, 0:SLOTS * DIM]).then_inc(s.carry_in0, 16)
                    sp.dma_start(dst_table.rearrange("(p j) c -> p j c", j=SLOTS),
                                 skip[:, :, 0:DIM]).then_inc(s.carry_in0, 16)
                    sp.wait_ge(s.carry_in0, 32)
                    sp.sem_inc(s.carry_in0, -32)

            def loads(attr_name, k, keys_name, keys, attr_buf):
                def stage(g, b, first, half):
                    if k:
                        if not first:
                            sp.wait_ge(s.attr_free, 1)
                            sp.sem_inc(s.attr_free, -1)
                        sp.dma_start(attr_buf[0:k, b, :],
                                     a[attr_name].rearrange("k (g n) -> k g n", n=512)[:, bass.ds(g, 1), :]
                                     .rearrange("k o n -> k (o n)")).then_inc(s.attr_in0 if b == 0 else s.attr_in1, 16)
                    if not first:
                        sp.wait_ge(s.key_free, 1)
                        sp.sem_inc(s.key_free, -1)
                    sp.dma_start(keys[:, b, :],
                                 a[keys_name].rearrange("(g n) -> g n", n=512)[bass.ds(g, 1), :]
                                 .rearrange("o n -> (o n)").partition_broadcast(P)).then_inc(s.key_in0 if b == 0 else s.key_in1, 16)
                return stage

            def stores(l, run, f):
                def stage(g, b, first, half):
                    sp.wait_ge(s.run_ready, GROUP)
                    sp.sem_inc(s.run_ready, -GROUP)
                    sp.dma_start(group_rows(run_rows[l], f, GROUP)[bass.ds(g, 1)].rearrange("o p t f -> (o p) t f"),
                                 run[:, b, 0:GROUP * f].rearrange("p (t f) -> p t f", f=f)).then_inc(
                        s.store0 if b == 0 else s.store1, 16)
                return stage

            def post(l):
                f = SPEC[l]["f"]
                if l:
                    for k in range(QK):
                        if k:
                            sp.wait_ge(s.c2nd_in, 1)
                            sp.sem_inc(s.c2nd_in, -1)
                        sp.dma_start(Nv.c2in[0:QT, 0:f],
                                     run_rows[l].rearrange("(k q p) f -> q k p f", q=QT, p=P)[:, k, P - 1, :]).then_inc(s.row_in0, 16)
                    sp.wait_ge(s.c2nd_in, 1)
                    sp.sem_inc(s.c2nd_in, -1)

                def stage(j, b, first, half):
                    if not first:
                        sp.wait_ge(s.sum_free, 1)
                        sp.sem_inc(s.sum_free, -1)
                    for c in range(1 if l else CHAINS):
                        table = carry[l] if l else src_sum[c]
                        sp.dma_start(Nv.car[:, b, c * f:(c + 1) * f],
                                     table[0:ROWS].rearrange("(p j) f -> j p f", j=SLOTS)[bass.ds(j, 1)]
                                     .rearrange("o p f -> (o p) f")).then_inc(s.carry_in0 if b == 0 else s.carry_in1, 16)
                pipelined(sp, SLOTS, [(0, stage)])
                sp.wait_ge(s.sum_free, 2)
                sp.sem_inc(s.sum_free, -2)

            for l in (0, 1, 2):
                if l not in layers:
                    continue
                table_out(l)
                barrier(sp, "sp")
                stages = [(0, loads(("edge_attr_64", "edge_attr_8", "edge_attr_16")[l], SPEC[l]["k"],
                                    "src_row" if l == 0 else "dst_row", E.keys, E.attr))]
                if l:
                    stages.append((2, stores(l, E.run, SPEC[l]["f"])))
                pipelined(sp, GROUPS, stages)
                sp.wait_ge(s.attr_free, 2)
                sp.sem_inc(s.attr_free, -2)
                sp.wait_ge(s.key_free, 2)
                sp.sem_inc(s.key_free, -2)
                barrier(sp, "sp")
                post(l)
                barrier(sp, "sp")
            if 3 in layers:
                table_out(3)
                barrier(sp, "sp")

                def rbf(g, b, first, half):
                    if not first:
                        sp.wait_ge(s.attr_free, 1)
                        sp.sem_inc(s.attr_free, -1)
                    sp.dma_start(T.rb[0:16, b, :],
                                 a["edge_attr_16"].rearrange("k (g n) -> k g n", n=256)[:, bass.ds(g, 1), :]
                                 .rearrange("k o n -> k (o n)")).then_inc(s.attr_in0 if b == 0 else s.attr_in1, 16)

                def keep_h(g, b, first, half):
                    sp.wait_ge(s.h_ready, 1)
                    sp.sem_inc(s.h_ready, -1)
                    sp.dma_start(edge_h.rearrange("(g t p) f -> g p t f", t=2, p=P)[bass.ds(g, 1)]
                                 .rearrange("o p t f -> (o p) t f"), T.h[:, b]).then_inc(s.store0 if b == 0 else s.store1, 16)
                pipelined(sp, TILES // 2, [(0, rbf), (3, keep_h)])
                sp.wait_ge(s.attr_free, 2)
                sp.sem_inc(s.attr_free, -2)
                barrier(sp, "sp")
                sp.dma_start(C.kI[0:QT], a["dst_row"].rearrange("(k q n) -> q k n", q=QT, n=P)).then_inc(s.key_in0, 16)
                sp.dma_start(C.lkI, a["tile_last"].partition_broadcast(P)).then_inc(s.key_in0, 16)
                sp.dma_start(C.fkI, a["tile_first"].partition_broadcast(P)).then_inc(s.key_in0, 16)
                barrier(sp, "sp")

                def load_h(g, b, first, half):
                    if not first:
                        sp.wait_ge(s.attr_free, 1)
                        sp.sem_inc(s.attr_free, -1)
                    sp.dma_start(P2.h[:, b, :].rearrange("p (t f) -> p t f", f=DIM),
                                 group_rows(edge_h, DIM, GROUP)[bass.ds(g, 1)].rearrange("o p t f -> (o p) t f")).then_inc(
                        s.attr_in0 if b == 0 else s.attr_in1, 16)
                pipelined(sp, GROUPS, [(0, load_h), (0, loads(None, 0, "dst_row", P2.keys, None)),
                                       (2, stores(3, P2.run, SPEC[3]["f"]))])
                sp.wait_ge(s.attr_free, 2)
                sp.sem_inc(s.attr_free, -2)
                sp.wait_ge(s.key_free, 2)
                sp.sem_inc(s.key_free, -2)
                barrier(sp, "sp")
                post(3)
                barrier(sp, "sp")
            sp.dma_start(out.rearrange("(p j) c -> p j c", j=SLOTS), x[0:NODES // SLOTS]).then_inc(moved, 16)
            sp.wait_ge(moved, 64)

        @block.gpsimd
        def _(pool):
            own = Steps()
            last_row = pool.to_reg(ROWS - 1)
            last_table_row = pool.to_reg(TABLE_ROWS - 1)
            last_tile = pool.to_reg(TILES)

            def gather(dst, table, idx, bound):
                return pool.indirect_dma_start(dst, None, table, bass.IndirectOffsetOnAxis(ap=idx, axis=0),
                                               bounds_check=bound, oob_is_err=True)

            nc.gpsimd.memset(U.zero, 0.0).then_inc(pool_own, own.step())
            nc.gpsimd.memset(ident[:], 0.0).then_inc(pool_own, own.step())
            nc.gpsimd.memset(lower[:], 1.0).then_inc(pool_own, own.step())
            nc.gpsimd.iota(U.node_i, pattern=[[1, SLOTS]], base=0, channel_multiplier=SLOTS).then_inc(pool_own, own.step())
            nc.gpsimd.iota(U.lk.bitcast(I32), pattern=[[1, TILES]], base=4000, channel_multiplier=0).then_inc(pool_own, own.step())
            nc.gpsimd.iota(U.cc.bitcast(I32), pattern=[[QT, QK]], base=4000, channel_multiplier=1).then_inc(pool_own, own.step())
            nc.gpsimd.iota(U.kc.bitcast(I32), pattern=[[0, QK]], base=ROWS, channel_multiplier=1).then_inc(pool_own, own.step())
            pool.wait_ge(pool_own, own.n)
            nc.gpsimd.affine_select(out=ident[:], in_=ident[:], compare_op=ALU.not_equal, fill=1.0, base=0,
                                        pattern=[[-1, P]], channel_multiplier=1).then_inc(pool_own, own.step())
            nc.gpsimd.affine_select(out=lower[:], in_=lower[:], compare_op=ALU.is_gt, fill=0.0, base=0,
                                        pattern=[[-1, P]], channel_multiplier=1).then_inc(pool_own, own.step())
            pool.wait_ge(pool_own, own.n)
            pool.sem_inc(pool_own, own.reset())
            pool.sem_inc(zero_made, 2)
            pool.wait_ge(s.w_ready, 1)
            pool.sem_inc(s.w_ready, -1)
            for j in range(SLOTS):
                if j >= 2:
                    pool.wait_ge(s.got_free, 1)
                    pool.sem_inc(s.got_free, -1)
                nc.gpsimd.tensor_copy(put_i[:, j:j + 1], U.tile_i[:, j:j + 1]).then_inc(pool_own, own.step())
                pool.wait_ge(pool_own, own.n)
                pool.sem_inc(pool_own, own.reset())
                gather(U.rowI[:, j % 2, :], a["dst_tiles"], put_i[:, j:j + 1], last_tile).then_inc(
                    keys_got[j % 2], 16)
            pool.wait_ge(s.got_free, 2)
            pool.sem_inc(s.got_free, -2)
            barrier(pool, "pool")

            def gathers(l, table, indices, buf, width):
                def stage(g, b, first, half):
                    if not first:
                        pool.wait_ge(s.got_free, 1)
                        pool.sem_inc(s.got_free, -1)
                    nc.gpsimd.tensor_copy(E.idx[:, b, :], indices[:, bass.ds(g * GROUP, GROUP)]).then_inc(pool_own, own.step())
                    pool.wait_ge(pool_own, own.n)
                    pool.sem_inc(pool_own, own.reset())
                    for t in range(GROUP):
                        gather(buf[:, b, t * width:(t + 1) * width], table, E.idx[:, b, t:t + 1], last_row).then_inc(
                            got[l][b], 16)
                return stage

            def scatter(g, b, first, half):
                nc.gpsimd.tensor_copy(E.pidx[:, b, :], put_i[:, bass.ds(g * GROUP, GROUP)]).then_inc(pool_own, own.step())
                pool.wait_ge(pool_own, own.n)
                pool.sem_inc(pool_own, own.reset())
                for t in range(GROUP):
                    if not (isinstance(g, int) and g == 0):
                        pool.wait_ge(put[t], g * 16)
                    pool.wait_ge(s.run_ready, 1)
                    pool.sem_inc(s.run_ready, -1)
                    pool.indirect_dma_start(
                        src_sum[t], bass.IndirectOffsetOnAxis(ap=E.pidx[:, b, t:t + 1], axis=0),
                        E.run[:, b, t * 480:(t + 1) * 480], None, compute_op=ALU.add,
                        bounds_check=last_table_row, oob_is_err=True).then_inc(put[t], 16)

            def post(l):
                f = SPEC[l]["f"]
                if not l:
                    return
                for k in range(QK):
                    pool.wait_ge(s.c2nd_sb, 1)
                    pool.sem_inc(s.c2nd_sb, -1)
                    pool.indirect_dma_start(
                        carry[l], bass.IndirectOffsetOnAxis(ap=put2_i[:, k:k + 1], axis=0),
                        Nv.c2[0:QT, 0:f], None, compute_op=ALU.add,
                        bounds_check=last_table_row, oob_is_err=True).then_inc(carried[l], 16)
                    pool.wait_ge(carried[l], 16 * (k + 1))
                    pool.sem_inc(s.c2nd_in, 1)

                def stage(j, b, first, half):
                    if not first:
                        pool.wait_ge(s.got_free, 1)
                        pool.sem_inc(s.got_free, -1)
                    nc.gpsimd.tensor_copy(Nv.idx[:, b, 0:1], last_i[:, bass.ds(j, 1)]).then_inc(pool_own, own.step())
                    pool.wait_ge(pool_own, own.n)
                    pool.sem_inc(pool_own, own.reset())
                    gather(Nv.row[:, b, 0:f], run_rows[l], Nv.idx[:, b, 0:1], last_edge).then_inc(
                        rows_got[l][b], 16)
                pipelined(pool, SLOTS, [(0, stage)])
                pool.wait_ge(s.got_free, 2)
                pool.sem_inc(s.got_free, -2)

            last_edge = pool.to_reg(TILES * P - 1)
            for l in (0, 1, 2):
                if l not in layers:
                    continue
                barrier(pool, "pool")
                stages = [(0, gathers(l, node_table[l], src_i if l else dst_i, E.got, SPEC[l]["table"]))]
                if l == 0:
                    stages.append((2, scatter))
                pipelined(pool, GROUPS, stages)
                pool.wait_ge(s.got_free, 2)
                pool.sem_inc(s.got_free, -2)
                barrier(pool, "pool")
                post(l)
                barrier(pool, "pool")
            if 3 in layers:
                barrier(pool, "pool")

                def both(g, b, first, half):
                    if not first:
                        pool.wait_ge(s.got_free, 1)
                        pool.sem_inc(s.got_free, -1)
                    nc.gpsimd.tensor_copy(T.idx[:, b, 0, :], src_i[:, bass.ds(g * 2, 2)]).then_inc(pool_own, own.step())
                    nc.gpsimd.tensor_copy(T.idx[:, b, 1, :], dst_i[:, bass.ds(g * 2, 2)]).then_inc(pool_own, own.step())
                    pool.wait_ge(pool_own, own.n)
                    pool.sem_inc(pool_own, own.reset())
                    for t in range(2):
                        gather(T.gs[:, b, t, :], src_table, T.idx[:, b, 0, t:t + 1], last_row).then_inc(
                            got[3][b], 16)
                        gather(T.gd[:, b, t, :], dst_table, T.idx[:, b, 1, t:t + 1], last_row).then_inc(
                            got[3][b], 16)
                pipelined(pool, TILES // 2, [(0, both)])
                pool.wait_ge(s.got_free, 2)
                pool.sem_inc(s.got_free, -2)
                barrier(pool, "pool")
                barrier(pool, "pool")
                barrier(pool, "pool")
                post(3)
                barrier(pool, "pool")

        @block.scalar
        def _(act):
            own = Steps()

            def wload(dst, src):
                act.dma_start(dst, src).then_inc(weights_in, 16)
                wload.n += 16
            wload.n = 0
            for name, key in (("fc1_0", "L0_gnn_W_fc1"), ("fc2_0", "L0_gnn_W_fc2"), ("fc1_1", "L1_gnn_fcW1"),
                              ("fc2_1", "L1_gnn_fcW2"), ("fc1_2", "L2_gnn_Wfc1"), ("fc2_2", "L2_gnn_Wfc2"),
                              ("rbf", "L3_gnn_W_rbf"),
                              ("f_s0", "L0_gnn_W_nl0"), ("f_v0", "L0_gnn_W_nl1"), ("k_s0", "L0_gnn_W_skip0"), ("k_v0", "L0_gnn_W_skip1"),
                              ("f_s1", "L1_gnn_W1_s"), ("f_v1", "L1_gnn_W1_v"), ("k_s1", "L1_gnn_W_sc_s"), ("k_v1", "L1_gnn_W_sc_v"),
                              ("f_s2", "L2_gnn_Wl1_0"), ("f_v2", "L2_gnn_Wl1_1"), ("k_s2", "L2_gnn_Wsc0"), ("k_v2", "L2_gnn_Wsc1"),
                              ("f_s3", "L3_gnn_Ws_src"), ("f_v3", "L3_gnn_Wv_src"), ("k_s3", "L3_gnn_Ws_dst"), ("k_v3", "L3_gnn_Wv_dst"),
                              ("out_s0", "L0_gnn_W_out_s"), ("out_v0", "L0_gnn_W_out_v"),
                              ("out_s1", "L1_gnn_W2_s"), ("out_v1", "L1_gnn_W2_v"), ("out_a1", "L1_gnn_W3"),
                              ("out_s2", "L2_gnn_Wl2_s"), ("out_v2", "L2_gnn_Wl2_v"), ("out_a2", "L2_gnn_Wa"),
                              ("out_s3", "L3_gnn_Wps"), ("out_v3", "L3_gnn_Wpv"), ("gate", "L3_gnn_Wg"), ("lin_s", "L3_gnn_Ws_vlin")):
                wload(wt[name][:], a[key])
            wload(wt["val_s"][:, 0:64], a["L3_gnn_W_alpha"])
            wload(wt["val_s"][:, 64:128], a["L3_gnn_Ws_val"])
            for col, key in ((0, "L3_gnn_gamma_s"), (1, "L3_gnn_beta_s"), (2, "L3_gnn_gamma_v")):
                wload((gamma_s, beta_s, gamma_v)[col][:], a[key])
            wload(alpha_dot[:], a["L3_gnn_alpha_dot"].partition_broadcast(P))
            wload(w2[0:64, 0:1], a["L3_gnn_w2_ss"])
            wload(w2[64:96, 0:1], a["L3_gnn_w2_vv0"])
            wload(w2[0:64, 1:2], a["L3_gnn_w2_sv"])
            for at, col, key in ((64, 1, "w2_vs"), (96, 1, "w2_vv1"), (0, 2, "w2_vs"), (32, 2, "w2_vv1"),
                                 (64, 2, "w2_vs"), (96, 2, "w2_vv1")):
                wload(w2[at:at + 32, col:col + 1], a["L3_gnn_" + key])
            act.wait_ge(weights_in, wload.n)
            act.wait_ge(s.hid_ready, 1)
            act.sem_inc(s.hid_ready, -1)
            for name, key in (("val", "L3_gnn_Wv_val"), ("lin", "L3_gnn_Wv_vlin")):
                wload(wt[name + "_x"][0:64, 0:32], a[key][0:64])
                wload(wt[name + "_x"][64:128, 32:64], a[key][64:128])
                wload(wt[name + "_yz"][0:64, 0:32], a[key][64:128])
                wload(wt[name + "_yz"][64:128, 32:64], a[key][64:128])
            act.wait_ge(weights_in, wload.n)
            act.sem_inc(s.hid_free, 1)
            act.wait_ge(s.hid_ready, 1)
            act.sem_inc(s.hid_ready, -1)

            def root(t, v):
                act.wait_ge(s.root_asked, 1)
                act.sem_inc(s.root_asked, -1)
                act.activation(t, v, ACT.Sqrt).then_inc(s.root_done, 1)
            root(U.j, U.n2)
            barrier(act, "act")

            def prep(l):
                for row in (0,) if l < 3 else (0, 2, 4):
                    root(stats[:, 8, :], stats[:, row, :])

                def features(j, b, first, half):
                    act.wait_ge(s.node_in, 1)
                    act.sem_inc(s.node_in, -1)
                    if l < 3:
                        act.activation(Nv.h[:, b, :], x[:, bass.ds(j, 1), :].rearrange("p o c -> p (o c)"), ACT.Relu,
                                       bias=stats[:, 1, bass.ds(j, 1)], scale=stats[:, 0, bass.ds(j, 1)]).then_inc(s.h_ready, 1)
                    else:
                        act.activation(Nv.h[:, b, :], fore[:, bass.ds(j * DIM, DIM)], ACT.Copy).then_inc(s.h_ready, 1)

                def turned(j, b, first, half):
                    act.wait_ge(s.node_t, 1)
                    act.sem_inc(s.node_t, -1)
                    if l < 3:
                        act.activation(Nv.hT[0:64, b, 0, :], bank[0:64, b, 0:128], ACT.Copy).then_inc(act_own, own.step())
                        act.activation(Nv.hT[0:32, b, 1:4, :], bank[0:32, b, 128:512].rearrange("p (i n) -> p i n", i=3),
                                       ACT.Copy).then_inc(s.node_tsb, 1)
                    else:
                        act.activation(Nv.hT[0:64, b, 0, :], bank[0:64, b, 0:128], ACT.Identity,
                                           bias=beta_s[:], scale=gamma_s[:]).then_inc(act_own, own.step())
                        act.activation(Nv.hT[0:32, b, 1:4, :], bank[0:32, b, 128:512].rearrange("p (i n) -> p i n", i=3),
                                       ACT.Copy, scale=gamma_v[:]).then_inc(s.node_tsb, 1)
                    act.wait_ge(act_own, own.n)
                    act.sem_inc(act_own, own.reset())
                pipelined(act, SLOTS, [(0, features), (1, turned)])

            def hidden(l):
                def stage(g, b, first, half):
                    act.wait_ge(s.hid_mm, 1)
                    act.sem_inc(s.hid_mm, -1)
                    act.sem_inc(s.attr_free, 1)
                    if not first:
                        act.wait_ge(s.hid_free, 1)
                        act.sem_inc(s.hid_free, -1)
                    act.activation(E.hid[0:64, b, :], bank[0:64, 0, :], ACT.Relu if l == 0 else ACT.Silu,
                                   scale=(1.0, 8 ** -0.5, 0.25)[l]).then_inc(s.hid_ready, 1)
                return stage

            def evacuate(l, run, f, store):
                def stage(g, b, first, half):
                    if store and not first:
                        act.wait_ge(s.store0 if b == 0 else s.store1, 16)
                        act.sem_inc(s.store0 if b == 0 else s.store1, -16)
                    for t in range(GROUP):
                        if not store and not first:
                            act.wait_ge(put[t], (g - 1) * 16)
                        act.wait_ge(s.run_mm, 1)
                        act.sem_inc(s.run_mm, -1)
                        if t == GROUP - 1:
                            act.sem_inc(s.msg_free, 1)
                        act.activation(run[:, b, t * f:(t + 1) * f], bank[:, 5 + t % 2, 0:f], ACT.Copy).then_inc(s.run_free, 1)
                return stage

            def post(l):
                f, vec = SPEC[l]["f"], SPEC[l]["vec"]
                top = 64 if l == 3 else 96
                if l:
                    for k in range(QK):
                        act.wait_ge(s.c2nd_mm, 1)
                        act.sem_inc(s.c2nd_mm, -1)
                        act.activation(Nv.c2[0:QT, 0:f], bank[0:QT, 4, 0:f], ACT.Copy).then_inc(s.c2nd_sb, 1)

                def turned(j, b, first, half):
                    act.wait_ge(s.node_t, 1)
                    act.sem_inc(s.node_t, -1)
                    act.activation(Nv.hT[0:top, b, 0, :], bank[0:top, b, 0:128], ACT.Copy).then_inc(act_own, own.step())
                    act.activation(Nv.hT[0:vec, b, 1:4, :], bank[0:vec, b, 128:512].rearrange("p (i n) -> p i n", i=3),
                                   ACT.Copy).then_inc(s.node_tsb, 1)
                    act.wait_ge(act_own, own.n)
                    act.sem_inc(act_own, own.reset())
                pipelined(act, SLOTS, [(0, turned)])
                if l == 0:
                    o = fore[:, 0:SLOTS * 192].rearrange("p (j c) -> p j c", c=192)
                    act.wait_ge(s.vt_ready, 1)
                    act.sem_inc(s.vt_ready, -1)
                    act.activation(skip[:, :, 0:96], o[:, :, 0:96], ACT.Sigmoid).then_inc(act_own, own.step())
                    act.wait_ge(act_own, own.n)
                    act.sem_inc(act_own, own.reset())
                    act.sem_inc(s.gate_ready, 1)
                if l == 1:
                    act.wait_ge(s.vt_ready, 1)
                    act.sem_inc(s.vt_ready, -1)
                    act.activation(Nv.small[:, 4:6, :], Nv.small[:, 2:4, :], ACT.Sin, scale=2 * math.pi).then_inc(act_own, own.step())
                    act.wait_ge(act_own, own.n)
                    act.sem_inc(act_own, own.reset())
                    act.sem_inc(s.gate_ready, 1)

            for l in (0, 1, 2):
                if l not in layers:
                    continue
                prep(l)
                barrier(act, "act")
                pipelined(act, GROUPS, [(1, evacuate(l, E.run, SPEC[l]["f"], l > 0)), (-1, hidden(l))])
                if l == 0:
                    for t in range(GROUP):
                        act.wait_ge(put[t], GROUPS * 16)
                else:
                    act.wait_ge(s.store0, 16)
                    act.sem_inc(s.store0, -16)
                    act.wait_ge(s.store1, 16)
                    act.sem_inc(s.store1, -16)
                act.wait_ge(s.hid_free, 2)
                act.sem_inc(s.hid_free, -2)
                barrier(act, "act")
                post(l)
                barrier(act, "act")
            if 3 in layers:
                prep(3)
                barrier(act, "act")

                def first_half(g, b, first, half):
                    act.wait_ge(s.t1_mm, 1)
                    act.sem_inc(s.t1_mm, -1)
                    act.activation(T.t1[0:96, b, :, 0:128], bank[0:96, 1:3, 0:128], ACT.Copy).then_inc(act_own, own.step())
                    act.activation(T.t1[:, b, :, 128:384], bank[:, 1:3, 128:384], ACT.Copy).then_inc(act_own, own.step())
                    act.wait_ge(act_own, own.n)
                    act.sem_inc(act_own, own.reset())
                    act.sem_inc(s.t1_ready, 1)
                    c1 = bank[:, 3, :].rearrange("p (t c) -> p t c", t=2)
                    act.wait_ge(s.c1_mm, 1)
                    act.sem_inc(s.c1_mm, -1)
                    act.activation(T.vs[:, b], c1[:, :, 64:128], ACT.Copy).then_inc(act_own, own.step())
                    act.wait_ge(act_own, own.n)
                    act.sem_inc(act_own, own.reset())
                    act.sem_inc(s.vt_ready, 1)
                    act.activation(T.al[:, b], c1[:, :, 0:64], ACT.Copy).then_inc(act_own, own.step())
                    act.activation(T.f2[:, b, :, 96:160], c1[:, :, 64:128], ACT.Sigmoid).then_inc(act_own, own.step())
                    act.wait_ge(s.vt_mm, 1)
                    act.sem_inc(s.vt_mm, -1)
                    act.activation(T.vT[0:64, b], bank[0:64, 7, 0:256].rearrange("p (t n) -> p t n", t=2), ACT.Copy).then_inc(s.vtsb_ready, 1)
                    act.wait_ge(s.gate_mm, 1)
                    act.sem_inc(s.gate_mm, -1)
                    act.activation(T.gate[:, b], bank[:, 7, 256:320].rearrange("p (t c) -> p t c", t=2), ACT.Sigmoid).then_inc(act_own, own.step())
                    act.wait_ge(act_own, own.n)
                    act.sem_inc(act_own, own.reset())
                    act.sem_inc(s.gate_ready, 1)

                def second_half(g, b, first, half):
                    act.wait_ge(s.t2_mm, 1)
                    act.sem_inc(s.t2_mm, -1)
                    act.activation(T.t2[0:96, b, :, 0:128], bank[0:96, 4:6, 0:128], ACT.Copy).then_inc(act_own, own.step())
                    act.activation(T.t2[:, b, :, 128:384], bank[:, 4:6, 128:384], ACT.Copy).then_inc(act_own, own.step())
                    act.wait_ge(act_own, own.n)
                    act.sem_inc(act_own, own.reset())
                    act.sem_inc(s.t2_ready, 1)
                    if not first:
                        act.wait_ge(s.store0 if b == 0 else s.store1, 16)
                        act.sem_inc(s.store0 if b == 0 else s.store1, -16)
                    act.wait_ge(s.c2_mm, 1)
                    act.sem_inc(s.c2_mm, -1)
                    act.activation(T.h[:, b, :, 0:64], bank[:, 6, 0:384].rearrange("p (t c) -> p t c", t=2)[:, :, 0:64],
                                   ACT.Copy).then_inc(s.hs_ready, 1)
                pipelined(act, TILES // 2, [(-1, first_half), (0, second_half)])
                act.wait_ge(s.store0, 16)
                act.sem_inc(s.store0, -16)
                act.wait_ge(s.store1, 16)
                act.sem_inc(s.store1, -16)
                barrier(act, "act")
                for k in range(QK):
                    act.wait_ge(s.scan_t, 1)
                    act.sem_inc(s.scan_t, -1)
                    act.activation(C.aT[0:QT, k], bank[0:QT, k % 2, :].rearrange("p (h n) -> p h n", h=4), ACT.Copy).then_inc(s.scan_sb, 1)
                act.wait_ge(s.hid_ready, 1)
                act.sem_inc(s.hid_ready, -1)
                act.activation(aux[:, :, 0:4], aux[:, :, 0:4], ACT.Exp).then_inc(act_own, own.step())
                act.wait_ge(act_own, own.n)
                act.sem_inc(act_own, own.reset())
                barrier(act, "act")
                pipelined(act, GROUPS, [(1, evacuate(3, P2.run, SPEC[3]["f"], True))])
                act.wait_ge(s.store0, 16)
                act.sem_inc(s.store0, -16)
                act.wait_ge(s.store1, 16)
                act.sem_inc(s.store1, -16)
                barrier(act, "act")
                post(3)
                barrier(act, "act")

        @block.tensor
        def _(pe):
            barrier(pe, "pe")

            def turn(l, what, j, b, blocks):
                for i, (c0, step, w) in enumerate(blocks):
                    last = nc.tensor.transpose(bank[0:w, b, i * P:(i + 1) * P], what[:, b, c0:c0 + step * (w - 1) + 1:step], ident[:])
                last.then_inc(s.node_t, 1)

            def prep(l):
                blocks = [(0, 1, 64)] + [(64 + i, 3, 32) if l < 3 else (64 + 32 * i, 1, 32) for i in range(3)]

                def turns(j, b, first, half):
                    pe.wait_ge(s.h_ready, 1)
                    pe.sem_inc(s.h_ready, -1)
                    turn(l, Nv.h, j, b, blocks)

                def products(j, b, first, half):
                    pe.wait_ge(s.node_tsb, 1)
                    pe.sem_inc(s.node_tsb, -1)
                    if not first:
                        pe.wait_ge(s.node_free, 1)
                        pe.sem_inc(s.node_free, -1)
                    o = bank[:, 2 + b, :]
                    ks = 96 if l == 0 else 64
                    nc.tensor.matmul(o[:, 0:64], Nv.hT[0:64, b, 0, :], wt[f"f_s{l}"][:], start=True, stop=True)
                    nc.tensor.matmul(o[:, 160:160 + ks], Nv.hT[0:64, b, 0, :], wt[f"k_s{l}"][:], start=True, stop=True)
                    for i in range(3):
                        nc.tensor.matmul(o[:, 64 + V * i:96 + V * i], Nv.hT[0:32, b, 1 + i, :], wt[f"f_v{l}"][:], start=True, stop=True)
                        last = nc.tensor.matmul(o[:, 160 + ks + V * i:192 + ks + V * i], Nv.hT[0:32, b, 1 + i, :], wt[f"k_v{l}"][:],
                                                start=True, stop=True)
                    last.then_inc(s.node_mm, 1)
                pipelined(pe, SLOTS, [(0, turns), (1, products)])
                pe.wait_ge(s.node_free, 2)
                pe.sem_inc(s.node_free, -2)

            def hidden(l):
                def stage(g, b, first, half):
                    pe.wait_ge(s.attr_in0 if b == 0 else s.attr_in1, 16)
                    pe.sem_inc(s.attr_in0 if b == 0 else s.attr_in1, -16)
                    k = SPEC[l]["k"]
                    nc.tensor.matmul(bank[0:64, 0, :], wt[f"fc1_{l}"][:], E.attr[0:k, b, :], start=True, stop=True).then_inc(s.hid_mm, 1)
                return stage

            def edge_weights(l):
                def stage(g, b, first, half):
                    pe.wait_ge(s.hid_ready, 1)
                    pe.sem_inc(s.hid_ready, -1)
                    if not first:
                        pe.wait_ge(s.w_free, 1)
                        pe.sem_inc(s.w_free, -1)
                    for t in range(GROUP):
                        last = nc.tensor.matmul(wmm(b)[:, t, 0:SPEC[l]["w"]], E.hid[0:64, b, t * P:(t + 1) * P], wt[f"fc2_{l}"][:],
                                                start=True, stop=True)
                    last.then_inc(s.w_ready, 1)
                return stage

            def sums(sel, msg, f):
                def stage(g, b, first, half):
                    pe.wait_ge(s.msg_ready, 1)
                    pe.sem_inc(s.msg_ready, -1)
                    for t in range(GROUP):
                        if not (isinstance(g, int) and g == 0 and t < 2):
                            pe.wait_ge(s.run_free, 1)
                            pe.sem_inc(s.run_free, -1)
                            pe.sem_inc(s.run_ready, 1)
                        nc.tensor.matmul(bank[:, 5 + t % 2, 0:f], sel[:, b, t, :], msg[:, b, t * f:(t + 1) * f],
                                         start=True, stop=True).then_inc(s.run_mm, 1)
                return stage

            def finish_sums():
                for _ in range(2):
                    pe.wait_ge(s.run_free, 1)
                    pe.sem_inc(s.run_free, -1)
                    pe.sem_inc(s.run_ready, 1)

            def post(l):
                f, vec = SPEC[l]["f"], SPEC[l]["vec"]
                top = 64 if l == 3 else 96
                out_s = SPEC[l]["out_s"]
                if l:
                    for k in range(QK):
                        pe.wait_ge(s.row_in0, 16)
                        pe.sem_inc(s.row_in0, -16)
                        nc.tensor.matmul(bank[0:QT, 4, 0:f], sel2[:, k, :], Nv.c2in[0:QT, 0:f], start=True, stop=True).then_inc(s.c2nd_mm, 1)

                def turns(j, b, first, half):
                    pe.wait_ge(s.sum_ready, 1)
                    pe.sem_inc(s.sum_ready, -1)
                    turn(l, Nv.sum, j, b, [(0, 1, top)] + [(top + vec * i, 1, vec) for i in range(3)])

                def products(j, b, first, half):
                    pe.wait_ge(s.node_tsb, 1)
                    pe.sem_inc(s.node_tsb, -1)
                    if not first:
                        pe.wait_ge(s.node_free, 1)
                        pe.sem_inc(s.node_free, -1)
                    o = bank[:, 2 + b, :]
                    last = nc.tensor.matmul(o[:, 0:out_s], Nv.hT[0:top, b, 0, :], wt[f"out_s{l}"][:], start=True, stop=True)
                    for i in range(3):
                        last = nc.tensor.matmul(o[:, out_s + V * i:out_s + V * (i + 1)], Nv.hT[0:vec, b, 1 + i, :], wt[f"out_v{l}"][:],
                                                start=True, stop=True)
                    if l in (1, 2):
                        last = nc.tensor.matmul(o[:, 160:161], Nv.hT[0:96, b, 0, :], wt[f"out_a{l}"][:], start=True, stop=True)
                    last.then_inc(s.node_mm, 1)
                pipelined(pe, SLOTS, [(0, turns), (1, products)])
                pe.wait_ge(s.node_free, 2)
                pe.sem_inc(s.node_free, -2)

            for l in (0, 1, 2):
                if l not in layers:
                    continue
                prep(l)
                barrier(pe, "pe")
                pipelined(pe, GROUPS, [(0, edge_weights(l)), (1, sums(E.sel, E.msg, SPEC[l]["f"])), (-1, hidden(l))])
                finish_sums()
                pe.wait_ge(s.w_free, 2)
                pe.sem_inc(s.w_free, -2)
                barrier(pe, "pe")
                post(l)
                barrier(pe, "pe")
            if 3 in layers:
                prep(3)
                barrier(pe, "pe")

                def edge_w3(g, b, first, half):
                    pe.wait_ge(s.attr_in0 if b == 0 else s.attr_in1, 16)
                    pe.sem_inc(s.attr_in0 if b == 0 else s.attr_in1, -16)
                    for t in range(2):
                        last = nc.tensor.matmul(bank[:, 0, t * 256:t * 256 + 224], T.rb[0:16, b, t * P:(t + 1) * P], wt["rbf"][:],
                                                start=True, stop=True)
                    last.then_inc(s.w_ready, 1)

                def turn3(f, b, at, signal):
                    for t in range(2):
                        nc.tensor.transpose(bank[0:96, at + t, 0:128], f[:, b, t, 0:96], ident[:])
                        nc.tensor.transpose(bank[:, at + t, 128:256], f[:, b, t, 96:224], ident[:])
                        last = nc.tensor.transpose(bank[:, at + t, 256:384], f[:, b, t, 224:352], ident[:])
                    last.then_inc(signal, 1)

                def turn_m1(g, b, first, half):
                    pe.wait_ge(s.f_ready, 1)
                    pe.sem_inc(s.f_ready, -1)
                    turn3(T.f, b, 1, s.t1_mm)

                def values(g, b, first, half):
                    pe.wait_ge(s.t1_ready, 1)
                    pe.sem_inc(s.t1_ready, -1)
                    if not (isinstance(g, int) and g == 0):
                        pe.wait_ge(s.c1_free, 1)
                        pe.sem_inc(s.c1_free, -1)
                    for t in range(2):
                        o = bank[:, 3, t * 256:(t + 1) * 256]
                        nc.tensor.matmul(o[:, 0:128], T.t1[0:96, b, t, 0:128], wt["val_s"][:], start=True, stop=True)
                        nc.tensor.matmul(o[:, 128:192], T.t1[:, b, t, 128:256], wt["val_x"][:], start=True, stop=True)
                        last = nc.tensor.matmul(o[:, 192:256], T.t1[:, b, t, 256:384], wt["val_yz"][:], start=True, stop=True)
                    last.then_inc(s.c1_mm, 1)
                    pe.wait_ge(s.vt_ready, 1)
                    pe.sem_inc(s.vt_ready, -1)
                    for t in range(2):
                        last = nc.tensor.transpose(bank[0:64, 7, t * P:(t + 1) * P], T.vs[:, b, t, :], ident[:])
                    last.then_inc(s.vt_mm, 1)
                    pe.wait_ge(s.vtsb_ready, 1)
                    pe.sem_inc(s.vtsb_ready, -1)
                    for t in range(2):
                        last = nc.tensor.matmul(bank[:, 7, 256 + V * t:256 + V * (t + 1)], T.vT[0:64, b, t, :], wt["gate"][:], start=True, stop=True)
                    last.then_inc(s.gate_mm, 1)

                def linear(g, b, first, half):
                    pe.wait_ge(s.f2_ready, 1)
                    pe.sem_inc(s.f2_ready, -1)
                    turn3(T.f2, b, 4, s.t2_mm)
                    pe.wait_ge(s.t2_ready, 1)
                    pe.sem_inc(s.t2_ready, -1)
                    if not (isinstance(g, int) and g == 0):
                        pe.wait_ge(s.c2_free, 1)
                        pe.sem_inc(s.c2_free, -1)
                    for t in range(2):
                        o = bank[:, 6, t * 192:(t + 1) * 192]
                        nc.tensor.matmul(o[:, 0:64], T.t2[0:96, b, t, 0:128], wt["lin_s"][:], start=True, stop=True)
                        nc.tensor.matmul(o[:, 64:128], T.t2[:, b, t, 128:256], wt["lin_x"][:], start=True, stop=True)
                        last = nc.tensor.matmul(o[:, 128:192], T.t2[:, b, t, 256:384], wt["lin_yz"][:], start=True, stop=True)
                    last.then_inc(s.c2_mm, 1)
                pipelined(pe, TILES // 2, [(-1, turn_m1), (-2, edge_w3), (-1, values), (0, linear)])
                pe.wait_ge(s.c1_free, 1)
                pe.sem_inc(s.c1_free, -1)
                pe.wait_ge(s.c2_free, 1)
                pe.sem_inc(s.c2_free, -1)
                barrier(pe, "pe")
                for k in range(QK):
                    if k >= 2:
                        pe.wait_ge(s.scan_free, 1)
                        pe.sem_inc(s.scan_free, -1)
                    for h in range(4):
                        last = nc.tensor.transpose(bank[0:QT, k % 2, h * P:(h + 1) * P], aux[:, k * QT:(k + 1) * QT, h], ident[:])
                    last.then_inc(s.scan_t, 1)
                pe.wait_ge(s.scan_free, 2)
                pe.sem_inc(s.scan_free, -2)
                pe.wait_ge(s.scan_mm, 1)
                pe.sem_inc(s.scan_mm, -1)
                for e in range(2):
                    for k in range(QK):
                        last = nc.tensor.transpose(bank[0:4, 2 + 2 * e + k // 4, (k % 4) * QT:(k % 4 + 1) * QT], C.edge[0:QT, k, :, e],
                                                   ident[0:QT, 0:QT])
                last.then_inc(s.vt_mm, 1)
                pe.wait_ge(s.scan_mm, 1)
                pe.sem_inc(s.scan_mm, -1)
                for k in range(QK):
                    for e in range(2):
                        last = nc.tensor.transpose(bank[0:QT, 6, (2 * k + e) * 4:(2 * k + e) * 4 + 4], C.c[0:4, e, k * QT:(k + 1) * QT],
                                                   ident[0:4, 0:4])
                last.then_inc(s.vt_mm, 1)
                for k in range(QK):
                    pe.wait_ge(s.scan_mm, 1)
                    pe.sem_inc(s.scan_mm, -1)
                    if k >= 2:
                        pe.wait_ge(s.scan_free, 1)
                        pe.sem_inc(s.scan_free, -1)
                    for h in range(4):
                        last = nc.tensor.transpose(bank[:, k % 2, h * QT:(h + 1) * QT], C.fw[0:QT, k, h, :], ident[0:QT, 0:QT])
                    last.then_inc(s.vt_mm, 1)
                pe.wait_ge(s.scan_free, 2)
                pe.sem_inc(s.scan_free, -2)
                barrier(pe, "pe")
                pipelined(pe, GROUPS, [(1, sums(P2.sel, P2.msg, SPEC[3]["f"]))])
                finish_sums()
                barrier(pe, "pe")
                post(3)
                barrier(pe, "pe")

        @block.vector
        def _(dve):
            V_ = nc.vector
            c = Steps()

            def tt(o, p, q, op):
                return V_.tensor_tensor(o, p, q, op)

            def bc(ap, axis, n):
                v = ap.unsqueeze(axis)
                shape = list(v.shape)
                shape[axis] = n
                return v.broadcast_to(shape)

            def inverse_root(v, width, eps, t, r):
                V_.tensor_scalar(v, v, 1.0 / width, eps, ALU.mult, ALU.add).then_inc(dve_own, c.step())
                dve.wait_ge(dve_own, c.n)
                dve.sem_inc(s.root_asked, 1)
                dve.wait_ge(s.root_done, 1)
                dve.sem_inc(s.root_done, -1)
                V_.reciprocal(r, t).then_inc(dve_own, c.step())
                dve.wait_ge(dve_own, c.n)
                tt(t, r, r, ALU.mult).then_inc(dve_own, c.step())
                dve.wait_ge(dve_own, c.n)
                tt(t, t, v, ALU.mult).then_inc(dve_own, c.step())
                dve.wait_ge(dve_own, c.n)
                V_.tensor_scalar(t, t, -0.5, 1.5, ALU.mult, ALU.add).then_inc(dve_own, c.step())
                dve.wait_ge(dve_own, c.n)
                tt(v, r, t, ALU.mult).then_inc(dve_own, c.step())
                dve.wait_ge(dve_own, c.n)

            V_.memset(wt["val_x"][:], 0.0).then_inc(dve_own, c.step())
            dve.wait_ge(dve_own, c.n)
            V_.memset(wt["lin_x"][:], 0.0).then_inc(dve_own, c.step())
            dve.wait_ge(dve_own, c.n)
            V_.memset(wt["val_yz"][:], 0.0).then_inc(dve_own, c.step())
            dve.wait_ge(dve_own, c.n)
            V_.memset(wt["lin_yz"][:], 0.0).then_inc(dve_own, c.step())
            dve.wait_ge(dve_own, c.n)
            dve.sem_inc(s.hid_ready, 2)
            dve.wait_ge(zero_made, 2)
            V_.tensor_copy(U.node, U.node_i).then_inc(dve_own, c.step())
            V_.tensor_copy(U.t, U.lk.bitcast(I32)).then_inc(dve_own, c.step())
            V_.tensor_copy(U.tc, U.cc.bitcast(I32)).then_inc(dve_own, c.step())
            V_.tensor_copy(U.prev[:, 0:QK], U.kc.bitcast(I32)).then_inc(dve_own, c.step())
            dve.wait_ge(dve_own, c.n)
            V_.tensor_copy(spare[:], U.prev[:, 0:1]).then_inc(dve_own, c.step())
            dve.wait_ge(dve_own, c.n)
            dve.wait_ge(loaded, LOADS)
            V_.tensor_copy(src_f[:], src_i[:]).then_inc(dve_own, c.step())
            V_.tensor_copy(dst_f[:], dst_i[:]).then_inc(dve_own, c.step())
            V_.tensor_copy(U.lk, U.lkI).then_inc(dve_own, c.step())
            V_.tensor_copy(U.nf, U.nfI).then_inc(dve_own, c.step())
            V_.tensor_copy(U.lkc[0:QT], U.lkc_i[0:QT]).then_inc(dve_own, c.step())
            V_.tensor_copy(U.nfc[0:QT], U.nfc_i[0:QT]).then_inc(dve_own, c.step())
            V_.tensor_copy(y[:, :, 0:4], aux[:, :, 0:4]).then_inc(dve_own, c.step())
            V_.tensor_copy(y[:, :, 4:6], aux[:, :, 1:3]).then_inc(dve_own, c.step())
            dve.wait_ge(dve_own, c.n)
            e3 = U.e3.rearrange("p (t i) -> p t i", i=3)
            tt(aux[:, :, 0:3], e3, e3, ALU.mult).then_inc(dve_own, c.step())
            dve.wait_ge(dve_own, c.n)
            V_.tensor_reduce(U.n2, aux[:, :, 0:3], AX, ALU.add).then_inc(dve_own, c.step())
            dve.wait_ge(dve_own, c.n)
            inverse_root(U.n2, 3.0, 0.0, U.j, U.one)
            tt(aux[:, :, 0:3], e3, bc(U.n2, 2, 3), ALU.mult).then_inc(dve_own, c.step())
            dve.wait_ge(dve_own, c.n)
            V_.tensor_copy(aux[:, :, 3:5], aux[:, :, 0:2]).then_inc(dve_own, c.step())
            dve.wait_ge(dve_own, c.n)
            V_.memset(U.one, 1.0).then_inc(dve_own, c.step())
            dve.wait_ge(dve_own, c.n)
            for j in range(SLOTS):
                V_.scalar_tensor_tensor(U.j, U.lk, U.node[:, j:j + 1], U.one, ALU.is_le, ALU.mult, accum_out=U.tiles[:, j:j + 1]).then_inc(dve_own, c.step())
                dve.wait_ge(dve_own, c.n)
            V_.tensor_copy(U.tile_i, U.tiles).then_inc(dve_own, c.step())
            dve.wait_ge(dve_own, c.n)
            dve.sem_inc(s.w_ready, 1)
            for j in range(SLOTS):
                dve.wait_ge(keys_got[j % 2], 16 * (j // 2 + 1))
                V_.scalar_tensor_tensor(U.j[:, 0:P], U.rowI[:, j % 2, :], U.node[:, j:j + 1], U.one[:, 0:P], ALU.is_le, ALU.mult,
                                               accum_out=U.in_tile[:, j:j + 1]).then_inc(dve_own, c.step())
                dve.wait_ge(dve_own, c.n)
                dve.sem_inc(s.got_free, 1)
            V_.scalar_tensor_tensor(U.end, U.tiles, float(P), U.in_tile, ALU.mult, ALU.add).then_inc(dve_own, c.step())
            dve.wait_ge(dve_own, c.n)
            dve.sem_inc(s.table_in, 1)
            V_.tensor_scalar(U.in_tile, U.end, -1.0, 0.0, ALU.add, ALU.max).then_inc(dve_own, c.step())
            dve.wait_ge(dve_own, c.n)
            V_.tensor_copy(last_i[:], U.in_tile).then_inc(dve_own, c.step())
            dve.wait_ge(dve_own, c.n)
            def second_keys(key, last, following, number):
                tt(key, last, following, ALU.is_equal).then_inc(dve_own, c.step())
                dve.wait_ge(dve_own, c.n)
                tt(U.j[0:last.shape[0], 0:last.shape[1]], last, number, ALU.subtract).then_inc(dve_own, c.step())
                dve.wait_ge(dve_own, c.n)
                tt(U.j[0:last.shape[0], 0:last.shape[1]], U.j[0:last.shape[0], 0:last.shape[1]], key, ALU.mult).then_inc(dve_own, c.step())
                dve.wait_ge(dve_own, c.n)
                return U.j[0:last.shape[0], 0:last.shape[1]]
            t_ = second_keys(U.one, U.lk, U.nf, U.t)
            tt(U.lk, t_, U.t, ALU.add).then_inc(dve_own, c.step())
            dve.wait_ge(dve_own, c.n)
            t_ = second_keys(U.cc[0:QT], U.lkc[0:QT], U.nfc[0:QT], U.tc[0:QT])
            tt(U.kc[0:QT], t_, U.tc[0:QT], ALU.add).then_inc(dve_own, c.step())
            dve.wait_ge(dve_own, c.n)
            for k in range(QK):
                V_.tensor_scalar(sel2[:, k, :], U.lk[0:QT, k * QT:(k + 1) * QT], U.kc[0:QT, k:k + 1], None, ALU.is_equal).then_inc(dve_own, c.step())
                dve.wait_ge(dve_own, c.n)
                V_.scalar_tensor_tensor(U.j[0:QT, 0:QT], U.lk[0:QT, k * QT:(k + 1) * QT], U.kc[0:QT, k:k + 1], lower[0:QT, 0:QT],
                                               ALU.is_equal, ALU.mult, accum_out=U.nfc[0:QT, k:k + 1]).then_inc(dve_own, c.step())
                dve.wait_ge(dve_own, c.n)
            V_.tensor_scalar(U.nfc[0:QT], U.nfc[0:QT], 1.0, None, ALU.is_lt).then_inc(dve_own, c.step())
            dve.wait_ge(dve_own, c.n)
            tt(U.cc[0:QT], U.cc[0:QT], U.nfc[0:QT], ALU.mult).then_inc(dve_own, c.step())
            dve.wait_ge(dve_own, c.n)
            tt(U.lkc[0:QT], U.lkc[0:QT], spare[0:QT, 0:1].broadcast_to([QT, QK]), ALU.subtract).then_inc(dve_own, c.step())
            dve.wait_ge(dve_own, c.n)
            tt(U.lkc[0:QT], U.lkc[0:QT], U.cc[0:QT], ALU.mult).then_inc(dve_own, c.step())
            dve.wait_ge(dve_own, c.n)
            tt(U.lkc[0:QT], U.lkc[0:QT], spare[0:QT, 0:1].broadcast_to([QT, QK]), ALU.add).then_inc(dve_own, c.step())
            dve.wait_ge(dve_own, c.n)
            V_.tensor_copy(put2_i[:], U.lkc[0:QT]).then_inc(dve_own, c.step())
            dve.wait_ge(dve_own, c.n)
            dve.wait_ge(moved, 48)
            tt(U.in_tile, U.end, U.prev, ALU.subtract).then_inc(dve_own, c.step())
            dve.wait_ge(dve_own, c.n)
            V_.tensor_scalar(has[:], U.in_tile, 1.0, None, ALU.min).then_inc(dve_own, c.step())
            dve.wait_ge(dve_own, c.n)
            V_.tensor_scalar(rcnt[:], U.in_tile, 1.0, None, ALU.max).then_inc(dve_own, c.step())
            dve.wait_ge(dve_own, c.n)
            V_.reciprocal(rcnt[:], rcnt[:]).then_inc(dve_own, c.step())
            dve.wait_ge(dve_own, c.n)
            dve.wait_ge(s.hid_free, 1)
            dve.sem_inc(s.hid_free, -1)

            def scale(name, by, c0=0, c1=None):
                w = wt[name]
                V_.tensor_scalar(w[:, c0:c1 or w.shape[1]], w[:, c0:c1 or w.shape[1]], by, None, ALU.mult).then_inc(dve_own, c.step())
                dve.wait_ge(dve_own, c.n)
            r3, r2 = 3 ** -0.5, 2 ** -0.5
            scale("fc2_0", r3, 160, 192)
            scale("fc2_0", r2, 192, 224)
            for l in (1, 2):
                scale(f"fc2_{l}", 0.125)
                scale(f"fc2_{l}", r3, 160, 192)
                for w in ("f_s", "k_s"):
                    scale(f"{w}{l}", 0.125)
                for w in ("f_v", "k_v"):
                    scale(f"{w}{l}", 32 ** -0.5)
                down = 96 ** -0.5 * (10 ** -0.5 if l == 1 else 1.0)
                for w in ("out_s", "out_v"):
                    scale(f"{w}{l}", down)
                scale(f"out_a{l}", down * (0.1 if l == 1 else 1.0))
            scale("rbf", r3, 160, 192)
            scale("rbf", r2, 192, 224)
            for at, rows, col, by in ((64, 32, 0, r3), (96, 32, 1, r2), (32, 32, 2, r2), (96, 32, 2, r2)):
                V_.tensor_scalar(w2[at:at + rows, col:col + 1], w2[at:at + rows, col:col + 1], by, None, ALU.mult).then_inc(dve_own, c.step())
                dve.wait_ge(dve_own, c.n)
            V_.tensor_scalar(wt["lin_s"][:], wt["lin_s"][:], w2[0:96, 0:1], None, ALU.mult).then_inc(dve_own, c.step())
            dve.wait_ge(dve_own, c.n)
            V_.tensor_scalar(wt["lin_x"][:], wt["lin_x"][:], w2[:, 1:2], None, ALU.mult).then_inc(dve_own, c.step())
            dve.wait_ge(dve_own, c.n)
            V_.tensor_scalar(wt["lin_yz"][:], wt["lin_yz"][:], w2[:, 2:3], None, ALU.mult).then_inc(dve_own, c.step())
            dve.wait_ge(dve_own, c.n)
            dve.wait_ge(dve_own, c.n)
            dve.sem_inc(dve_own, c.reset())
            barrier(dve, "dve")

            big = Nv.big.rearrange("p (j c) -> p j c", c=DIM)

            def mean_var(src, width, mean, rstd, eps, scratch):
                V_.tensor_reduce(stats[:, mean, :], src, AX, ALU.add).then_inc(dve_own, c.step())
                dve.wait_ge(dve_own, c.n)
                V_.tensor_scalar(stats[:, mean, :], stats[:, mean, :], 1.0 / width, None, ALU.mult).then_inc(dve_own, c.step())
                dve.wait_ge(dve_own, c.n)
                tt(scratch, src, bc(stats[:, mean, :], 2, width), ALU.subtract).then_inc(dve_own, c.step())
                dve.wait_ge(dve_own, c.n)
                tt(scratch, scratch, scratch, ALU.mult).then_inc(dve_own, c.step())
                dve.wait_ge(dve_own, c.n)
                V_.tensor_reduce(stats[:, rstd, :], scratch, AX, ALU.add).then_inc(dve_own, c.step())
                dve.wait_ge(dve_own, c.n)
                inverse_root(stats[:, rstd, :], width, eps, stats[:, 8, :], stats[:, 9, :])

            def prep(l):
                mean_var(x[:], DIM, 1, 0, 1e-5, big)
                tt(stats[:, 1, :], stats[:, 1, :], stats[:, 0, :], ALU.mult).then_inc(dve_own, c.step())
                dve.wait_ge(dve_own, c.n)
                V_.tensor_scalar(stats[:, 1, :], stats[:, 1, :], -1.0, None, ALU.mult).then_inc(dve_own, c.step())
                dve.wait_ge(dve_own, c.n)
                if l == 3:
                    tt(big, x[:], bc(stats[:, 0, :], 2, DIM), ALU.mult).then_inc(dve_own, c.step())
                    dve.wait_ge(dve_own, c.n)
                    tt(big, big, bc(stats[:, 1, :], 2, DIM), ALU.add).then_inc(dve_own, c.step())
                    dve.wait_ge(dve_own, c.n)
                    V_.tensor_scalar(big, big, 0.0, None, ALU.max).then_inc(dve_own, c.step())
                    dve.wait_ge(dve_own, c.n)
                    tt(x[:], x[:], big, ALU.add).then_inc(dve_own, c.step())
                    dve.wait_ge(dve_own, c.n)
                    normed = fore[:, 0:SLOTS * DIM].rearrange("p (j c) -> p j c", c=DIM)
                    hs = big[:, :, 0:S]
                    mean_var(hs, S, 3, 2, 1e-5, normed[:, :, 0:S])
                    tt(normed[:, :, 0:S], hs, bc(stats[:, 3, :], 2, S), ALU.subtract).then_inc(dve_own, c.step())
                    dve.wait_ge(dve_own, c.n)
                    tt(normed[:, :, 0:S], normed[:, :, 0:S], bc(stats[:, 2, :], 2, S), ALU.mult).then_inc(dve_own, c.step())
                    dve.wait_ge(dve_own, c.n)
                    hv = big[:, :, S:DIM]
                    nv = normed[:, :, S:DIM]
                    tt(nv, hv, hv, ALU.mult).then_inc(dve_own, c.step())
                    dve.wait_ge(dve_own, c.n)
                    V_.tensor_reduce(stats[:, 4, :], nv, AX, ALU.add).then_inc(dve_own, c.step())
                    dve.wait_ge(dve_own, c.n)
                    inverse_root(stats[:, 4, :], V, 1e-5, stats[:, 8, :], stats[:, 9, :])
                    for i in range(3):
                        tt(nv[:, :, V * i:V * (i + 1)], hv[:, :, i:3 * V:3], bc(stats[:, 4, :], 2, V), ALU.mult).then_inc(dve_own, c.step())
                        dve.wait_ge(dve_own, c.n)
                dve.wait_ge(dve_own, c.n)
                dve.sem_inc(dve_own, c.reset())
                dve.sem_inc(s.node_in, SLOTS)
                width = SPEC[l]["table"]
                ks = SPEC[l]["skip"]
                def stage(j, b, first, half):
                    dve.wait_ge(s.node_mm, 1)
                    dve.sem_inc(s.node_mm, -1)
                    o = bank[:, 2 + b, :]
                    t0 = fore[:, bass.ds(j * width, 160)]
                    k0 = skip[:, bass.ds(j, 1), 0:ks].rearrange("p o c -> p (o c)")
                    if l in (1, 2):
                        V_.tensor_scalar(t0, o[:, 0:160], attr[:, bass.ds(j, 1)], None, ALU.mult).then_inc(dve_own, c.step())
                        V_.tensor_scalar(k0, o[:, 160:160 + ks], attr[:, bass.ds(j, 1)], None, ALU.mult).then_inc(dve_own, c.step())
                    else:
                        V_.tensor_copy(t0, o[:, 0:160]).then_inc(dve_own, c.step())
                        V_.tensor_copy(k0, o[:, 160:160 + ks]).then_inc(dve_own, c.step())
                    if l == 0:
                        V_.tensor_copy(fore[:, bass.ds(j * width + 160, 64)], o[:, 64:128]).then_inc(dve_own, c.step())
                    dve.wait_ge(dve_own, c.n)
                    dve.sem_inc(dve_own, c.reset())
                    dve.sem_inc(s.node_free, 1)
                pipelined(dve, SLOTS, [(0, stage)])
                dve.sem_inc(s.table_in, 1)

            def select(g, b, keys, sel, scalar):
                for t in range(GROUP):
                    V_.tensor_scalar(sel[:, b, t, :], keys[:, b, t * P:(t + 1) * P],
                                       scalar[:, bass.ds(g * GROUP + t, 1)], None, ALU.is_equal).then_inc(dve_own, c.step())

            def edges(l):
                def stage(g, b, first, half):
                    f = SPEC[l]["f"]
                    dve.wait_ge(s.key_in0 if b == 0 else s.key_in1, 16)
                    dve.sem_inc(s.key_in0 if b == 0 else s.key_in1, -16)
                    if not first:
                        dve.wait_ge(s.msg_free, 1)
                        dve.sem_inc(s.msg_free, -1)
                    select(g, b, E.keys, E.sel, src_f if l == 0 else dst_f)
                    if l == 0:
                        for t in range(GROUP):
                            V_.scalar_tensor_tensor(E.first, E.keys[:, b, t * P:(t + 1) * P], src_f[:, bass.ds(g * GROUP + t, 1)],
                                                      lower[:], ALU.is_equal, ALU.mult, accum_out=E.cnt[:, t:t + 1]).then_inc(dve_own, c.step())
                            dve.wait_ge(dve_own, c.n)
                        keys4 = src_f[:, bass.ds(g * GROUP, GROUP)]
                        V_.tensor_scalar(E.cnt, E.cnt, 1.0, None, ALU.is_lt).then_inc(dve_own, c.step())
                        dve.wait_ge(dve_own, c.n)
                        V_.scalar_tensor_tensor(E.pos, keys4, spare[:], E.cnt, ALU.subtract, ALU.mult).then_inc(dve_own, c.step())
                        dve.wait_ge(dve_own, c.n)
                        V_.tensor_scalar(put_i[:, bass.ds(g * GROUP, GROUP)], E.pos, spare[:], None, ALU.add).then_inc(dve_own, c.step())
                        dve.wait_ge(dve_own, c.n)
                    dve.wait_ge(got[l][b], (half + 1) * (16 * GROUP))
                    dve.wait_ge(s.w_ready, 1)
                    dve.sem_inc(s.w_ready, -1)
                    dve.sem_inc(s.hid_free, 1)
                    w = wmm(b)
                    width = SPEC[l]["table"]
                    rows = E.got[:, b, 0:GROUP * width].rearrange("p (t c) -> p t c", c=width)
                    xs = rows[:, :, 0:S]
                    msg = E.msg[:, b, 0:GROUP * f].rearrange("p (t c) -> p t c", c=f)
                    vec = SPEC[l]["vec"]
                    blocks = msg[:, :, 96:96 + 3 * vec].rearrange("p t (i c) -> p t i c", c=vec)
                    t0 = E.t0[:, 0:GROUP * S].rearrange("p (t c) -> p t c", c=S)
                    t1 = E.t1.rearrange("p (t i c) -> p t i c", i=3, c=V)
                    t2 = E.t2.rearrange("p (t i c) -> p t i c", i=3, c=V)

                    def wv(c0):
                        return bc(w[:, :, c0:c0 + V], 2, 3)
                    if l == 0:
                        xv = rows[:, :, S:224].rearrange("p t (i c) -> p t i c", c=V)
                        sh = aux[:, bass.ds(g * GROUP, GROUP), :]
                        tt(t0, w[:, :, 64:128], xs, ALU.mult).then_inc(dve_own, c.step())
                        tt(t1, xv[:, :, 0:3, :], bc(sh[:, :, 0:3], 3, V), ALU.mult).then_inc(dve_own, c.step())
                        a_q = c.n
                        tt(msg[:, :, 0:S], w[:, :, 0:64], xs, ALU.mult).then_inc(dve_own, c.step())
                        dve.wait_ge(dve_own, a_q)
                        tt(blocks[:, :, :, 0:S], bc(t0, 2, 3), bc(sh[:, :, 0:3], 3, S), ALU.mult).then_inc(dve_own, c.step())
                        tt(t2[:, :, 0, :], t1[:, :, 0, :], t1[:, :, 1, :], ALU.add).then_inc(dve_own, c.step())
                        n1 = c.n
                        tt(blocks[:, :, :, S:96], wv(128), xv[:, :, 0:3, :], ALU.mult).then_inc(dve_own, c.step())
                        dve.wait_ge(dve_own, n1)
                        tt(t2[:, :, 0, :], t2[:, :, 0, :], t1[:, :, 2, :], ALU.add).then_inc(dve_own, c.step())
                        dve.wait_ge(dve_own, c.n)
                        tt(msg[:, :, S:96], t2[:, :, 0, :], w[:, :, 160:192], ALU.mult).then_inc(dve_own, c.step())
                        dve.wait_ge(dve_own, c.n)
                        tt(t1, xv[:, :, 1:4, :], bc(sh[:, :, 2:5], 3, V), ALU.mult).then_inc(dve_own, c.step())
                        tt(t2, xv[:, :, 2:5, :], bc(sh[:, :, 1:4], 3, V), ALU.mult).then_inc(dve_own, c.step())
                        dve.wait_ge(dve_own, c.n)
                        tt(t1, t1, t2, ALU.subtract).then_inc(dve_own, c.step())
                        dve.wait_ge(dve_own, c.n)
                        tt(blocks[:, :, :, 96:128], t1, wv(192), ALU.mult).then_inc(dve_own, c.step())
                    else:
                        yy = y[:, bass.ds(g * GROUP, GROUP), :]
                        xv = rows[:, :, S:DIM].rearrange("p t (i c) -> p t i c", c=V)
                        x0 = E.t0.rearrange("p (t c) -> p t c", c=DIM)
                        x0v = x0[:, :, S:DIM].rearrange("p t (i c) -> p t i c", c=V)
                        wb = msg[:, :, 0:S]
                        tt(x0, rows, yy[:, :, 0:1].broadcast_to([P, GROUP, DIM]), ALU.mult).then_inc(dve_own, c.step())
                        tt(t1, xv, bc(yy[:, :, 1:4], 3, V), ALU.mult).then_inc(dve_own, c.step())
                        tt(wb, w[:, :, 64:128], xs, ALU.mult).then_inc(dve_own, c.step())
                        dve.wait_ge(dve_own, c.n)
                        tt(t2[:, :, 0, :], t1[:, :, 0, :], t1[:, :, 1, :], ALU.add).then_inc(dve_own, c.step())
                        tt(blocks[:, :, :, 0:S], bc(wb, 2, 3), bc(yy[:, :, 1:4], 3, S), ALU.mult).then_inc(dve_own, c.step())
                        dve.wait_ge(dve_own, c.n)
                        tt(t2[:, :, 0, :], t2[:, :, 0, :], t1[:, :, 2, :], ALU.add).then_inc(dve_own, c.step())
                        n1 = c.n
                        tt(msg[:, :, 0:S], w[:, :, 0:64], x0[:, :, 0:S], ALU.mult).then_inc(dve_own, c.step())
                        dve.wait_ge(dve_own, n1)
                        tt(msg[:, :, S:96], t2[:, :, 0, :], w[:, :, 160:192], ALU.mult).then_inc(dve_own, c.step())
                        tt(blocks[:, :, :, S:96], wv(128), x0v, ALU.mult).then_inc(dve_own, c.step())
                    dve.wait_ge(dve_own, c.n)
                    dve.sem_inc(dve_own, c.reset())
                    dve.sem_inc(s.msg_ready, 1)
                    dve.sem_inc(s.w_free, 1)
                    dve.sem_inc(s.got_free, 1)
                    dve.sem_inc(s.key_free, 1)
                pipelined(dve, GROUPS, [(0, stage)])
                dve.wait_ge(s.msg_free, 2)
                dve.sem_inc(s.msg_free, -2)

            def post(l):
                f = SPEC[l]["f"]
                out_w = {0: 192, 1: 161, 2: 161, 3: 160}[l]
                conv = fore[:, 0:SLOTS * out_w].rearrange("p (j c) -> p j c", c=out_w)

                def sums(j, b, first, half):
                    dve.wait_ge(s.carry_in0 if b == 0 else s.carry_in1, 16 * (1 if l else CHAINS))
                    dve.sem_inc(s.carry_in0 if b == 0 else s.carry_in1, -(16 * (1 if l else CHAINS)))
                    car = Nv.car[:, b, :]
                    o = Nv.sum[:, b, 0:f]
                    if l:
                        dve.wait_ge(rows_got[l][b], (half + 1) * 16)
                        V_.scalar_tensor_tensor(o, Nv.row[:, b, 0:f], has[:, bass.ds(j, 1)], car[:, 0:f], ALU.mult, ALU.add).then_inc(dve_own, c.step())
                        dve.wait_ge(dve_own, c.n)
                    else:
                        tt(o, car[:, 0:f], car[:, f:2 * f], ALU.add).then_inc(dve_own, c.step())
                        tt(car[:, 2 * f:3 * f], car[:, 2 * f:3 * f], car[:, 3 * f:4 * f], ALU.add).then_inc(dve_own, c.step())
                        dve.wait_ge(dve_own, c.n)
                        tt(o, o, car[:, 2 * f:3 * f], ALU.add).then_inc(dve_own, c.step())
                        dve.wait_ge(dve_own, c.n)
                    if l == 3:
                        V_.tensor_scalar(Nv.rden[:, 0:4], o[:, 160:164], 1e-16, None, ALU.add).then_inc(dve_own, c.step())
                        dve.wait_ge(dve_own, c.n)
                        V_.reciprocal(Nv.rden[:, 0:4], Nv.rden[:, 0:4]).then_inc(dve_own, c.step())
                        dve.wait_ge(dve_own, c.n)
                        hs = o[:, 0:64].rearrange("p (h c) -> p h c", h=4)
                        hv = o[:, 64:160].rearrange("p (i h c) -> p i h c", i=3, h=4)
                        tt(hs, hs, bc(Nv.rden[:, 0:4], 2, 16), ALU.mult).then_inc(dve_own, c.step())
                        tt(hv, hv, bc(bc(Nv.rden[:, 0:4], 1, 3), 3, 8), ALU.mult).then_inc(dve_own, c.step())
                    dve.wait_ge(dve_own, c.n)
                    dve.sem_inc(dve_own, c.reset())
                    dve.sem_inc(s.sum_ready, 1)
                    dve.sem_inc(s.sum_free, 1)
                    if l:
                        dve.sem_inc(s.got_free, 1)

                def products(j, b, first, half):
                    dve.wait_ge(s.node_mm, 1)
                    dve.sem_inc(s.node_mm, -1)
                    o = bank[:, 2 + b, 0:out_w]
                    to = fore[:, bass.ds(j * out_w, out_w)]
                    if l == 1:
                        V_.tensor_scalar(to, o, attr[:, bass.ds(j, 1)], None, ALU.mult).then_inc(dve_own, c.step())
                    elif l == 2:
                        V_.tensor_scalar(to, o, attr[:, bass.ds(j, 1)], rcnt[:, bass.ds(j, 1)], ALU.mult, ALU.mult).then_inc(dve_own, c.step())
                    else:
                        V_.tensor_copy(to, o).then_inc(dve_own, c.step())
                    dve.wait_ge(dve_own, c.n)
                    dve.sem_inc(dve_own, c.reset())
                    dve.sem_inc(s.node_free, 1)
                pipelined(dve, SLOTS, [(2, products), (0, sums)])

                def add_to_x(res):
                    tt(x[:, :, 0:S], x[:, :, 0:S], res[:, :, 0:S], ALU.add).then_inc(dve_own, c.step())
                    for i in range(3):
                        tt(x[:, :, S + i:DIM:3], x[:, :, S + i:DIM:3], res[:, :, S + V * i:S + V * (i + 1)], ALU.add).then_inc(dve_own, c.step())
                    dve.wait_ge(dve_own, c.n)
                if l == 0:
                    V_.scalar_tensor_tensor(conv, conv, 1.0 / 32.0, skip[:], ALU.mult, ALU.add).then_inc(dve_own, c.step())
                    dve.wait_ge(dve_own, c.n)
                    dve.wait_ge(dve_own, c.n)
                    dve.sem_inc(dve_own, c.reset())
                    dve.sem_inc(s.vt_ready, 1)
                    dve.wait_ge(s.gate_ready, 1)
                    dve.sem_inc(s.gate_ready, -1)
                    tt(big[:, :, 0:S], conv[:, :, 0:S], skip[:, :, 0:S], ALU.mult).then_inc(dve_own, c.step())
                    for i in range(3):
                        tt(big[:, :, S + V * i:S + V * (i + 1)], conv[:, :, 96 + V * i:128 + V * i], skip[:, :, S:96], ALU.mult).then_inc(dve_own, c.step())
                    dve.wait_ge(dve_own, c.n)
                    add_to_x(big)
                elif l == 1:
                    turns = Nv.small
                    V_.tensor_scalar(turns[:, 0, :], conv[:, :, 160], 1.0 / (2 * math.pi), None, ALU.mult).then_inc(dve_own, c.step())
                    dve.wait_ge(dve_own, c.n)
                    V_.tensor_copy(Nv.smi, turns[:, 0, :]).then_inc(dve_own, c.step())
                    dve.wait_ge(dve_own, c.n)
                    V_.tensor_copy(turns[:, 1, :], Nv.smi).then_inc(dve_own, c.step())
                    dve.wait_ge(dve_own, c.n)
                    tt(turns[:, 2, :], turns[:, 0, :], turns[:, 1, :], ALU.subtract).then_inc(dve_own, c.step())
                    dve.wait_ge(dve_own, c.n)
                    V_.tensor_scalar(turns[:, 3, :], turns[:, 2, :], 0.25, None, ALU.add).then_inc(dve_own, c.step())
                    dve.wait_ge(dve_own, c.n)
                    for _ in range(2):
                        V_.tensor_scalar(turns[:, 6:8, :], turns[:, 2:4, :], 0.5, None, ALU.is_gt).then_inc(dve_own, c.step())
                        dve.wait_ge(dve_own, c.n)
                        tt(turns[:, 2:4, :], turns[:, 2:4, :], turns[:, 6:8, :], ALU.subtract).then_inc(dve_own, c.step())
                        dve.wait_ge(dve_own, c.n)
                        V_.tensor_scalar(turns[:, 6:8, :], turns[:, 2:4, :], -0.5, None, ALU.is_lt).then_inc(dve_own, c.step())
                        dve.wait_ge(dve_own, c.n)
                        tt(turns[:, 2:4, :], turns[:, 2:4, :], turns[:, 6:8, :], ALU.add).then_inc(dve_own, c.step())
                        dve.wait_ge(dve_own, c.n)
                    dve.wait_ge(dve_own, c.n)
                    dve.sem_inc(dve_own, c.reset())
                    dve.sem_inc(s.vt_ready, 1)
                    dve.wait_ge(s.gate_ready, 1)
                    dve.sem_inc(s.gate_ready, -1)
                    tt(big, skip[:, :, 0:DIM], bc(turns[:, 5, :], 2, DIM), ALU.mult).then_inc(dve_own, c.step())
                    tt(conv[:, :, 0:DIM], conv[:, :, 0:DIM], bc(turns[:, 4, :], 2, DIM), ALU.mult).then_inc(dve_own, c.step())
                    dve.wait_ge(dve_own, c.n)
                    tt(big, big, conv[:, :, 0:DIM], ALU.add).then_inc(dve_own, c.step())
                    dve.wait_ge(dve_own, c.n)
                    add_to_x(big)
                elif l == 2:
                    tt(big, conv[:, :, 0:DIM], conv[:, :, 160:161].broadcast_to([P, SLOTS, DIM]), ALU.mult).then_inc(dve_own, c.step())
                    dve.wait_ge(dve_own, c.n)
                    tt(big, big, skip[:, :, 0:DIM], ALU.add).then_inc(dve_own, c.step())
                    dve.wait_ge(dve_own, c.n)
                    add_to_x(big)
                else:
                    add_to_x(conv)
                dve.wait_ge(dve_own, c.n)
                dve.sem_inc(dve_own, c.reset())

            for l in (0, 1, 2):
                if l not in layers:
                    continue
                prep(l)
                barrier(dve, "dve")
                edges(l)
                barrier(dve, "dve")
                post(l)
                barrier(dve, "dve")

            def cross(o, v, ys, u1, u2):
                tt(u1[:, :, 0:2, :], v[:, :, 1:3, :], bc(ys[:, :, 2:4], 3, V), ALU.mult).then_inc(dve_own, c.step())
                tt(u1[:, :, 2:3, :], v[:, :, 0:1, :], bc(ys[:, :, 4:5], 3, V), ALU.mult).then_inc(dve_own, c.step())
                tt(u2[:, :, 0:1, :], v[:, :, 2:3, :], bc(ys[:, :, 1:2], 3, V), ALU.mult).then_inc(dve_own, c.step())
                tt(u2[:, :, 1:3, :], v[:, :, 0:2, :], bc(ys[:, :, 2:4], 3, V), ALU.mult).then_inc(dve_own, c.step())
                dve.wait_ge(dve_own, c.n)
                tt(o, u1, u2, ALU.subtract).then_inc(dve_own, c.step())

            def dot(o, v, ys, q):
                tt(q, v, bc(ys[:, :, 0:3], 3, V), ALU.mult).then_inc(dve_own, c.step())
                dve.wait_ge(dve_own, c.n)
                tt(o, q[:, :, 0, :], q[:, :, 1, :], ALU.add).then_inc(dve_own, c.step())
                dve.wait_ge(dve_own, c.n)
                tt(o, o, q[:, :, 2, :], ALU.add).then_inc(dve_own, c.step())

            if 3 in layers:
                prep(3)
                barrier(dve, "dve")

                def planes(ap):
                    return ap.rearrange("p t (i c) -> p t i c", i=3)

                q, u1, u2 = planes(T.q), planes(T.u1), planes(T.u2)

                def m1(g, b, first, half):
                    dve.wait_ge(got[3][b], (half + 1) * 64)
                    yy = y[:, bass.ds(g * 2, 2), :]
                    y0 = yy[:, :, 0:1]
                    ys = yy[:, :, 1:6]
                    m, my0 = T.m, T.my0
                    w = bank[:, 0, :].rearrange("p (t c) -> p t c", t=2)
                    f = T.f[:, b]
                    vsl = f[:, :, 160:352].rearrange("p t (i c) -> p t i c", c=64)
                    tt(m, T.gs[:, b], T.gd[:, b], ALU.add).then_inc(dve_own, c.step())
                    dve.wait_ge(dve_own, c.n)
                    tt(my0, m, y0.broadcast_to([P, 2, DIM]), ALU.mult).then_inc(dve_own, c.step())
                    mv = planes(m[:, :, S:DIM])
                    dot(u1[:, :, 0, :], mv, ys, q)
                    dve.wait_ge(s.w_ready, 1)
                    dve.sem_inc(s.w_ready, -1)
                    dve.sem_inc(s.attr_free, 1)
                    dve.wait_ge(dve_own, c.n)
                    tt(f[:, :, 64:96], u1[:, :, 0, :], w[:, :, 160:192], ALU.mult).then_inc(dve_own, c.step())
                    tt(f[:, :, 0:64], my0[:, :, 0:S], w[:, :, 0:64], ALU.mult).then_inc(dve_own, c.step())
                    tt(f[:, :, 96:160], m[:, :, 0:S], w[:, :, 64:128], ALU.mult).then_inc(dve_own, c.step())
                    tt(vsl[:, :, :, 0:V], planes(my0[:, :, S:DIM]), bc(w[:, :, 128:160], 2, 3), ALU.mult).then_inc(dve_own, c.step())
                    dve.wait_ge(dve_own, c.n)
                    cross(q, mv, ys, u1, u2)
                    dve.wait_ge(dve_own, c.n)
                    tt(vsl[:, :, :, V:64], q, bc(w[:, :, 192:224], 2, 3), ALU.mult).then_inc(dve_own, c.step())
                    dve.wait_ge(dve_own, c.n)
                    dve.sem_inc(dve_own, c.reset())
                    dve.sem_inc(s.f_ready, 1)
                    dve.sem_inc(s.got_free, 1)

                def m2(g, b, first, half):
                    dve.wait_ge(s.gate_ready, 1)
                    dve.sem_inc(s.gate_ready, -1)
                    yy = y[:, bass.ds(g * 2, 2), :]
                    ys = yy[:, :, 1:6]
                    c1 = bank[:, 3, :].rearrange("p (t c) -> p t c", t=2)
                    V_.scalar_tensor_tensor(T.al2, T.al[:, b], 0.2, T.al[:, b], ALU.mult, ALU.max).then_inc(dve_own, c.step())
                    tt(vv, bc(c1[:, :, 128:160], 2, 3), bc(ys[:, :, 0:3], 3, V), ALU.mult).then_inc(dve_own, c.step())
                    dve.wait_ge(dve_own, c.n)
                    tt(T.al2, T.al2, bc(alpha_dot[:], 1, 2), ALU.mult).then_inc(dve_own, c.step())
                    tt(vv, vv, c1[:, :, 160:256].rearrange("p t (i c) -> p t i c", i=3), ALU.add).then_inc(dve_own, c.step())
                    dve.wait_ge(dve_own, c.n)
                    dve.sem_inc(s.c1_free, 1)
                    V_.tensor_reduce(aux[:, bass.ds(g * 2, 2), 0:4], T.al2.rearrange("p t (h c) -> p t h c", h=4), AX, ALU.add).then_inc(dve_own, c.step())
                    tt(vv, vv, bc(T.gate[:, b], 2, 3), ALU.mult).then_inc(dve_own, c.step())
                    dve.wait_ge(dve_own, c.n)
                    f = T.f2[:, b]
                    vsl = f[:, :, 160:352].rearrange("p t (i c) -> p t i c", c=64)
                    tt(f[:, :, 0:64], f[:, :, 96:160], yy[:, :, 0:1].broadcast_to([P, 2, S]), ALU.mult).then_inc(dve_own, c.step())
                    dot(f[:, :, 64:96], vv, ys, q)
                    tt(vsl[:, :, :, 0:V], vv, y0_planes(yy), ALU.mult).then_inc(dve_own, c.step())
                    cross(vsl[:, :, :, V:64], vv, ys, u1, u2)
                    dve.wait_ge(dve_own, c.n)
                    dve.sem_inc(dve_own, c.reset())
                    dve.sem_inc(s.f2_ready, 1)

                vv = T.vv

                def y0_planes(yy):
                    return bc(yy[:, :, 0:1].broadcast_to([P, 2, 3]), 3, V)

                def edge_out(g, b, first, half):
                    dve.wait_ge(s.hs_ready, 1)
                    dve.sem_inc(s.hs_ready, -1)
                    ys = y[:, bass.ds(g * 2, 2), 1:4]
                    c2 = bank[:, 6, 0:384].rearrange("p (t c) -> p t c", t=2)
                    hv = planes(T.h[:, b, :, S:DIM])
                    tt(q, bc(c2[:, :, 64:96], 2, 3), bc(ys, 3, V), ALU.mult).then_inc(dve_own, c.step())
                    dve.wait_ge(dve_own, c.n)
                    tt(hv, q, c2[:, :, 96:192].rearrange("p t (i c) -> p t i c", i=3), ALU.add).then_inc(dve_own, c.step())
                    dve.wait_ge(dve_own, c.n)
                    dve.sem_inc(dve_own, c.reset())
                    dve.sem_inc(s.c2_free, 1)
                    dve.sem_inc(s.h_ready, 1)
                pipelined(dve, TILES // 2, [(-1, m1), (0, m2), (1, edge_out)])
                barrier(dve, "dve")

                dve.wait_ge(s.key_in0, 48)
                dve.sem_inc(s.key_in0, -48)
                V_.tensor_copy(C.k[0:QT], C.kI[0:QT]).then_inc(dve_own, c.step())
                V_.tensor_copy(C.lk, C.lkI).then_inc(dve_own, c.step())
                V_.tensor_copy(C.fk, C.fkI).then_inc(dve_own, c.step())
                dve.wait_ge(dve_own, c.n)

                def same(o, p_, q_):
                    tt(o, p_, q_, ALU.is_equal).then_inc(dve_own, c.step())
                    dve.wait_ge(dve_own, c.n)
                    V_.tensor_scalar(o, o, -1.0, BIG, ALU.add, ALU.mult).then_inc(dve_own, c.step())
                    dve.wait_ge(dve_own, c.n)

                V_.memset(C.b, -BIG).then_inc(dve_own, c.step())
                dve.wait_ge(dve_own, c.n)
                V_.memset(C.b2, -BIG).then_inc(dve_own, c.step())
                dve.wait_ge(dve_own, c.n)
                for k in range(QK):
                    kk = C.k[0:QT, k, :]
                    same(C.b[0:QT, 1:P], kk[:, 1:P], kk[:, 0:P - 1])
                    V_.tensor_copy(C.b2[0:QT, 0:P - 1], C.b[0:QT, 1:P]).then_inc(dve_own, c.step())
                    dve.wait_ge(dve_own, c.n)
                    dve.wait_ge(s.scan_sb, 1)
                    dve.sem_inc(s.scan_sb, -1)
                    dve.sem_inc(s.scan_free, 1)
                    for h in range(4):
                        fw, bw, at = C.fw[0:QT, k, h, :], C.bw[0:QT, h, :], C.aT[0:QT, k, h, :]
                        V_.tensor_tensor_scan(fw, C.b[0:QT], at, 0.0, ALU.add, ALU.max).then_inc(dve_own, c.step())
                        V_.tensor_tensor_scan(bw[:, ::-1], C.b2[0:QT, ::-1], at[:, ::-1], 0.0, ALU.add, ALU.max).then_inc(dve_own, c.step())
                    dve.wait_ge(dve_own, c.n)
                    V_.tensor_copy(C.edge[0:QT, k, :, 0], C.fw[0:QT, k, :, P - 1]).then_inc(dve_own, c.step())
                    V_.tensor_copy(C.edge[0:QT, k, :, 1], C.bw[0:QT, :, 0]).then_inc(dve_own, c.step())
                    dve.wait_ge(dve_own, c.n)
                    tt(C.fw[0:QT, k], C.fw[0:QT, k], C.bw[0:QT], ALU.max).then_inc(dve_own, c.step())
                    dve.wait_ge(dve_own, c.n)
                dve.sem_inc(s.scan_mm, 1)
                dve.wait_ge(s.vt_mm, 1)
                dve.sem_inc(s.vt_mm, -1)
                for e in range(2):
                    V_.tensor_copy(C.m[0:4, e, 0:4 * QT], bank[0:4, 2 + 2 * e, 0:4 * QT]).then_inc(dve_own, c.step())
                    V_.tensor_copy(C.m[0:4, e, 4 * QT:TILES], bank[0:4, 3 + 2 * e, 0:3 * QT]).then_inc(dve_own, c.step())
                V_.memset(C.j[0:4], -BIG).then_inc(dve_own, c.step())
                dve.wait_ge(dve_own, c.n)
                V_.memset(C.c[0:4], -BIG).then_inc(dve_own, c.step())
                dve.wait_ge(dve_own, c.n)
                lk, fk = C.lk[0:4], C.fk[0:4]
                same(C.j[0:4, 0, 1:TILES], lk[:, 1:TILES], lk[:, 0:TILES - 1])
                same(C.j[0:4, 1, 0:TILES - 1], fk[:, 1:TILES], fk[:, 0:TILES - 1])
                V_.tensor_tensor_scan(C.c[0:4, 0, :], C.j[0:4, 0, :], C.m[0:4, 0, :], 0.0, ALU.add, ALU.max).then_inc(dve_own, c.step())
                dve.wait_ge(dve_own, c.n)
                V_.tensor_tensor_scan(C.c[0:4, 1, ::-1], C.j[0:4, 1, ::-1], C.m[0:4, 1, ::-1], 0.0, ALU.add, ALU.max).then_inc(dve_own, c.step())
                dve.wait_ge(dve_own, c.n)
                same(C.j[0:4, 0, 1:TILES], fk[:, 1:TILES], lk[:, 0:TILES - 1])
                V_.tensor_copy(C.m[0:4, 0, 1:TILES], C.c[0:4, 0, 0:TILES - 1]).then_inc(dve_own, c.step())
                dve.wait_ge(dve_own, c.n)
                V_.tensor_copy(C.m[0:4, 1, 0:TILES - 1], C.c[0:4, 1, 1:TILES]).then_inc(dve_own, c.step())
                dve.wait_ge(dve_own, c.n)
                V_.memset(C.c[0:4], -BIG).then_inc(dve_own, c.step())
                dve.wait_ge(dve_own, c.n)
                tt(C.c[0:4, 0, 1:TILES], C.m[0:4, 0, 1:TILES], C.j[0:4, 0, 1:TILES], ALU.add).then_inc(dve_own, c.step())
                dve.wait_ge(dve_own, c.n)
                tt(C.c[0:4, 1, 0:TILES - 1], C.m[0:4, 1, 0:TILES - 1], C.j[0:4, 0, 1:TILES], ALU.add).then_inc(dve_own, c.step())
                dve.wait_ge(dve_own, c.n)
                dve.sem_inc(s.scan_mm, 1)
                dve.wait_ge(s.vt_mm, 1)
                dve.sem_inc(s.vt_mm, -1)
                V_.tensor_copy(C.cT[0:QT].rearrange("p k e h -> p (k e h)"), bank[0:QT, 6, 0:QK * 8]).then_inc(dve_own, c.step())
                dve.wait_ge(dve_own, c.n)
                for k in range(QK):
                    kk = C.k[0:QT, k, :]
                    for e, at in ((0, 0), (1, P - 1)):
                        V_.tensor_scalar(C.b[0:QT], kk, kk[:, at:at + 1], None, ALU.is_equal).then_inc(dve_own, c.step())
                        dve.wait_ge(dve_own, c.n)
                        V_.tensor_scalar(C.b[0:QT], C.b[0:QT], -1.0, BIG, ALU.add, ALU.mult).then_inc(dve_own, c.step())
                        dve.wait_ge(dve_own, c.n)
                        for h in range(4):
                            V_.scalar_tensor_tensor(C.fw[0:QT, k, h, :], C.b[0:QT], C.cT[0:QT, k, e, h:h + 1], C.fw[0:QT, k, h, :],
                                                      ALU.add, ALU.max).then_inc(dve_own, c.step())
                        dve.wait_ge(dve_own, c.n)
                    dve.sem_inc(s.scan_mm, 1)
                    dve.wait_ge(s.vt_mm, 1)
                    dve.sem_inc(s.vt_mm, -1)
                    sc = aux[:, k * QT:(k + 1) * QT, 0:4]
                    tt(sc, sc, bank[:, k % 2, 0:4 * QT].rearrange("p (h t) -> p t h", h=4), ALU.subtract).then_inc(dve_own, c.step())
                    dve.wait_ge(dve_own, c.n)
                    dve.sem_inc(s.scan_free, 1)
                dve.sem_inc(s.hid_ready, 1)
                dve.wait_ge(dve_own, c.n)
                dve.sem_inc(dve_own, c.reset())
                barrier(dve, "dve")

                def weigh(g, b, first, half):
                    f = SPEC[3]["f"]
                    dve.wait_ge(s.key_in0 if b == 0 else s.key_in1, 16)
                    dve.sem_inc(s.key_in0 if b == 0 else s.key_in1, -16)
                    if not first:
                        dve.wait_ge(s.msg_free, 1)
                        dve.sem_inc(s.msg_free, -1)
                    select(g, b, P2.keys, P2.sel, dst_f)
                    dve.wait_ge(s.attr_in0 if b == 0 else s.attr_in1, 16)
                    dve.sem_inc(s.attr_in0 if b == 0 else s.attr_in1, -16)
                    pp = aux[:, bass.ds(g * GROUP, GROUP), 0:4]
                    msg = P2.msg[:, b, :].rearrange("p (t c) -> p t c", c=f)
                    hh = P2.h[:, b, :].rearrange("p (t c) -> p t c", c=DIM)
                    V_.tensor_copy(msg[:, :, 160:164], pp).then_inc(dve_own, c.step())
                    tt(msg[:, :, 0:S].rearrange("p t (h c) -> p t h c", h=4), hh[:, :, 0:S].rearrange("p t (h c) -> p t h c", h=4),
                         bc(pp, 3, 16), ALU.mult).then_inc(dve_own, c.step())
                    for i in range(3):
                        lo = S + V * i
                        tt(msg[:, :, lo:lo + V].rearrange("p t (h c) -> p t h c", h=4),
                             hh[:, :, lo:lo + V].rearrange("p t (h c) -> p t h c", h=4), bc(pp, 3, 8), ALU.mult).then_inc(dve_own, c.step())
                    dve.wait_ge(dve_own, c.n)
                    dve.sem_inc(dve_own, c.reset())
                    dve.sem_inc(s.msg_ready, 1)
                    dve.sem_inc(s.attr_free, 1)
                    dve.sem_inc(s.key_free, 1)
                pipelined(dve, GROUPS, [(0, weigh)])
                dve.wait_ge(s.msg_free, 2)
                dve.sem_inc(s.msg_free, -2)
                barrier(dve, "dve")
                post(3)
                barrier(dve, "dve")


LOADS = 16 * 10
WEIGHTS = [
    "L0_gnn_W_skip0", "L0_gnn_W_skip1", "L0_gnn_W_nl0", "L0_gnn_W_nl1", "L0_gnn_W_fc1", "L0_gnn_W_fc2",
    "L0_gnn_W_out_s", "L0_gnn_W_out_v", "L1_gnn_W_sc_s", "L1_gnn_W_sc_v", "L1_gnn_W1_s", "L1_gnn_W1_v",
    "L1_gnn_W2_s", "L1_gnn_W2_v", "L1_gnn_W3", "L1_gnn_fcW1", "L1_gnn_fcW2", "L2_gnn_Wfc1", "L2_gnn_Wfc2",
    "L2_gnn_Wsc0", "L2_gnn_Wsc1", "L2_gnn_Wl1_0", "L2_gnn_Wl1_1", "L2_gnn_Wl2_s", "L2_gnn_Wl2_v", "L2_gnn_Wa",
    "L3_gnn_Ws_src", "L3_gnn_Wv_src", "L3_gnn_Ws_dst", "L3_gnn_Wv_dst", "L3_gnn_W_rbf", "L3_gnn_W_alpha",
    "L3_gnn_Ws_val", "L3_gnn_Wv_val", "L3_gnn_Wg", "L3_gnn_Ws_vlin", "L3_gnn_Wv_vlin", "L3_gnn_Wps", "L3_gnn_Wpv",
]
COLUMNS = ["L3_gnn_gamma_s", "L3_gnn_beta_s", "L3_gnn_gamma_v", "L3_gnn_w2_ss", "L3_gnn_w2_sv", "L3_gnn_w2_vs",
           "L3_gnn_w2_vv0", "L3_gnn_w2_vv1"]


def laid_out(inputs):
    import numpy as np

    more = TILES * P - EDGES
    d = {}

    def edges_first(v, fill=0.0):
        v = np.concatenate([v, np.full((more, v.shape[1]), fill, v.dtype)])
        return v.reshape(TILES, P, -1).transpose(1, 0, 2).reshape(P, -1)

    def features_first(v):
        return np.concatenate([v, np.zeros((more, v.shape[1]), v.dtype)]).T

    d["x"] = np.concatenate([inputs["x"], np.zeros((ROWS - NODES, DIM), np.float32)])
    d["node_vec1"] = np.concatenate([inputs["node_vec1"][:, 0], np.zeros(ROWS - NODES, np.float32)]).reshape(P, SLOTS)
    for name in ("src", "dst"):
        v = np.concatenate([inputs[name], np.full(more, PAD_NODE, np.int32)])
        d[name + "_row"] = v
        d[name] = v.reshape(TILES, P).T
    keys = d["dst_row"].reshape(TILES, P)
    d["dst_tiles"] = np.concatenate([keys, np.full((1, P), ROWS, np.int32)])
    d["tile_last"], d["tile_first"] = keys[:, -1], keys[:, 0]
    d["next_first"] = np.concatenate([keys[1:, 0], np.full(1, ROWS, np.int32)])
    d["last_col"] = d["tile_last"].reshape(QK, QT).T
    d["next_col"] = d["next_first"].reshape(QK, QT).T
    d["edge_attr_3"] = edges_first(inputs["edge_attr_3"], 1.0)
    d["edge_attr_4"] = edges_first(inputs["edge_attr_4"]).reshape(P, TILES, 4)
    for k in (8, 16, 64):
        d[f"edge_attr_{k}"] = features_first(inputs[f"edge_attr_{k}"])
    for name in WEIGHTS:
        d[name] = inputs[name]
    for name in COLUMNS:
        d[name] = inputs[name].reshape(-1, 1)
    d["L3_gnn_alpha_dot"] = inputs["L3_gnn_alpha_dot"].reshape(-1)
    return {k: np.ascontiguousarray(v) for k, v in d.items()}


def kernel(**inputs):
    import numpy as np
    import concourse.bacc as bacc
    from concourse.bass_utils import run_bass_kernel_spmd

    nc = bacc.Bacc("TRN2", target_bir_lowering=False, num_devices=1)
    arrays, args = {}, {}
    for name, v in laid_out({k: np.asarray(v) for k, v in inputs.items()}).items():
        arrays["in_" + name] = v
        args[name] = nc.dram_tensor("in_" + name, v.shape, mybir.dt.from_np(v.dtype), kind="ExternalInput").ap()
    out = nc.dram_tensor("out_x", (NODES, DIM), F32, kind="ExternalOutput").ap()
    build(nc, args, out, LAYERS)
    return run_bass_kernel_spmd(nc, [arrays], core_ids=[0]).results[0]["out_x"]


LAYERS = (0, 1, 2, 3)
```

```python
import math
from contextlib import ExitStack

import concourse.bass as bass
from concourse import mybir

ALU = mybir.AluOpType
ACT = mybir.ActivationFunctionType
AX = mybir.AxisListType.X
F32 = mybir.dt.float32
I32 = mybir.dt.int32

P = 128
NODES, DIM = 3125, 160
SLOTS = 25
ROWS = P * SLOTS
TABLE_ROWS = ROWS + P
EDGES = 100000
TILES = 784
GROUP = 4
GROUPS = TILES // GROUP
QT, QK = 112, 7
PAD_NODE = ROWS - 1
S, V = 64, 32
CHAINS = 4
DEPTH = 4
RUN_BANKS = (2, 3, 3, 3)
BIG = 1.0e38

SPEC = {
    0: dict(k=64, w=224, f=480, vec=128, table=224, out_s=96, skip=192),
    1: dict(k=8, w=192, f=384, vec=96, table=160, out_s=64, skip=160),
    2: dict(k=16, w=192, f=384, vec=96, table=160, out_s=64, skip=160),
    3: dict(k=16, w=224, f=164, vec=32, table=160, out_s=64, skip=160),
}


class Steps:

    def __init__(self):
        self.n = 0

    def step(self):
        self.n += 1
        return 1

    def reset(self):
        n, self.n = self.n, 0
        return -n


def pipelined(eng, count, stages, unroll=2):
    ahead, behind = min(lag for lag, _ in stages), max(lag for lag, _ in stages)
    lo = -(-(behind + unroll) // unroll) * unroll
    hi = (count + ahead) // unroll * unroll

    def step(i, part):
        for lag, stage in stages:
            if part is None:
                if 0 <= i - lag < count:
                    stage(i - lag, (i - lag) % unroll, i - lag < 2, (i - lag) // unroll)
            else:
                stage(i * unroll + (part - lag), (part - lag) % unroll, False, i + (part - lag) // unroll)

    for i in range(ahead, lo):
        step(i, None)
    with eng.Fori(lo // unroll, hi // unroll) as it:
        for part in range(unroll):
            step(it, part)
    for i in range(hi, count + behind):
        step(i, None)


def among_first(g, n):
    return isinstance(g, int) and g < n


def build(nc, a, out, layers=(0, 1, 2, 3)):
    with ExitStack() as ctx:
        def sb(name, shape, dt=F32):
            return ctx.enter_context(nc.sbuf_tensor(name, shape, dt))

        def sem(name):
            return ctx.enter_context(nc.semaphore(name))

        def dram(name, shape, dt=F32):
            return nc.dram_tensor(name, shape, dt, kind="Internal").ap()

        node_table = {l: dram(f"node_table{l}", (ROWS, SPEC[l]["table"])) for l in (0, 1, 2)}
        src_table = dram("src_table", (ROWS, DIM))
        dst_table = dram("dst_table", (ROWS, DIM))
        src_sum = [dram(f"src_sum{c}", (TABLE_ROWS, SPEC[0]["f"])) for c in range(CHAINS)]
        run_rows = {l: dram(f"run_rows{l}", (TILES * P, SPEC[l]["f"])) for l in (1, 2, 3)}
        carry = {l: dram(f"carry{l}", (TABLE_ROWS, SPEC[l]["f"])) for l in (1, 2, 3)}
        edge_h = dram("edge_h", (TILES * P, DIM))
        ends = dram("ends", (ROWS + 1, 1))

        x = sb("x", [P, SLOTS, DIM])
        skip = sb("skip", [P, SLOTS, 192])
        fore = sb("fore", [P, SLOTS * 224])
        attr = sb("attr", [P, SLOTS])
        y = sb("y", [P, TILES, 6])
        aux = sb("aux", [P, TILES, 5])
        src_i = sb("src_i", [P, TILES], I32)
        dst_i = sb("dst_i", [P, TILES], I32)
        src_f = sb("src_f", [P, TILES])
        dst_f = sb("dst_f", [P, TILES])
        put_i = sb("put_i", [P, TILES], I32)
        ident = sb("ident", [P, P])
        lower = sb("lower", [P, P])
        spare = sb("spare", [P, 1])
        stats = sb("stats", [P, 12, SLOTS])
        last_i = sb("last_i", [P, SLOTS], I32)
        rcnt = sb("rcnt", [P, SLOTS])
        has = sb("has", [P, SLOTS])
        sel2 = sb("sel2", [QT, QK, QT])
        put2_i = sb("put2_i", [QT, QK], I32)
        work = sb("work", [P, 18432])

        def carve():
            at = [0]

            def get(*dims, dt=F32):
                n = math.prod(dims)
                n += n % 2
                assert at[0] + n <= 18432, (at[0], n)
                v = work[:, at[0]:at[0] + n]
                at[0] += n
                v = v[:, 0:math.prod(dims)]
                if dt != F32:
                    v = v.bitcast(dt)
                if len(dims) == 1:
                    return v
                names = " ".join(f"d{i}" for i in range(len(dims)))
                return v.rearrange(f"p ({names}) -> p {names}", **{f"d{i}": d for i, d in enumerate(dims)})

            return get

        bank = ctx.enter_context(nc.psum_tensor("bank", [P, 8, 512], F32))

        wt = {}

        def weight(name, rows, cols):
            wt[name] = sb("w_" + name, [rows, cols])

        weight("fc1_0", 64, 64)
        weight("fc2_0", 64, 224)
        weight("fc1_1", 8, 64)
        weight("fc2_1", 64, 192)
        weight("fc1_2", 16, 64)
        weight("fc2_2", 64, 192)
        weight("rbf", 16, 224)
        for l in range(4):
            weight(f"f_s{l}", 64, 64)
            weight(f"f_v{l}", 32, 32)
            weight(f"k_s{l}", 64, 96 if l == 0 else 64)
            weight(f"k_v{l}", 32, 32)
        weight("out_s0", 96, 96)
        weight("out_v0", 128, 32)
        for l in (1, 2):
            weight(f"out_s{l}", 96, 64)
            weight(f"out_v{l}", 96, 32)
            weight(f"out_a{l}", 96, 1)
        weight("out_s3", 64, 64)
        weight("out_v3", 32, 32)
        weight("val_s", 96, 160)
        weight("val_x", 128, 128)
        weight("val_yz", 128, 128)
        weight("gate", 64, 32)
        weight("lin_s", 96, 64)
        weight("lin_x", 128, 128)
        weight("lin_yz", 128, 128)
        val_sT = sb("val_sT", [64, 96])
        gamma_s = sb("gamma_s", [64, 1])
        beta_s = sb("beta_s", [64, 1])
        gamma_v = sb("gamma_v", [32, 1])
        alpha_dot = sb("alpha_dot", [P, 64])
        w2 = sb("w2", [P, 3])

        phase = sem("phase")
        dve_own, act_own, pool_own = sem("dve_own"), sem("act_own"), sem("pool_own")
        loaded, zero_made, zeroed = sem("loaded"), sem("zero_made"), sem("zeroed")
        moved = sem("moved")
        weights_in = sem("weights_in")
        one = {n: sem(n) for n in (
            "node_in", "node_t", "node_tsb", "node_mm", "node_free", "carry_in0", "carry_in1", "sum_free",
            "row_in0", "weights_ready", "wy_ready", "m_ready", "sum_ready", "table_in",
            "attr_in0", "attr_in1", "attr_free", "key_in0", "key_in1", "key_free", "hid_mm", "hid_ready",
            "hid_free", "w_ready", "w_free", "got_free", "msg_ready", "msg_free", "run_mm", "run_free",
            "run_ready", 
            "store0", "store1", "f_ready", "t1_mm", "t1_ready", "c1_mm", "c1_free", "vt_ready", "vt_mm",
            "vtsb_ready", "gate_mm", "gate_ready", "f2_ready", "t2_mm", "t2_ready", "c2_mm", "c2_free",
            "hs_ready", "h_ready", "c2nd_mm", "c2nd_sb", "c2nd_in",
            "root_asked", "root_done", "scan_t", "scan_sb", "scan_mm", "scan_free")}
        keys_got = [sem(f"keys_got{b}") for b in range(2)]
        got = {l: [sem(f"got{l}_{b}") for b in range(DEPTH)] for l in range(4)}
        rows_got = {l: [sem(f"rows_got{l}_{b}") for b in range(2)] for l in (1, 2, 3)}
        carried = {l: sem(f"carried{l}") for l in (1, 2, 3)}
        put = [sem(f"put{c}") for c in range(CHAINS)]
        s = type("Signals", (), one)

        block = ctx.enter_context(nc.Block())
        phases = {"n": {}}

        def barrier(eng, name):
            n = phases["n"][name] = phases["n"].get(name, 0) + 1
            eng.drain().then_inc(phase, 1)
            eng.wait_ge(phase, 5 * n)

        def edge_views():
            g = carve()
            v = type("Edge", (), {})
            v.attr = g(2, 512)
            v.keys = g(2, 512, dt=I32)
            v.hid = g(2, 512)
            v.got = fore[:, 0:DEPTH * GROUP * 224].rearrange("p (b c) -> p b c", b=DEPTH)
            v.w = g(2, GROUP, 192)
            v.msg = g(2, GROUP * 480)
            v.sel = g(2, GROUP, P)
            v.run = g(2, GROUP * 480)
            v.t0, v.t1, v.t2 = g(GROUP * 160), g(GROUP * 96), g(GROUP * 96)
            v.first = g(GROUP, P)
            v.u1, v.u2 = g(GROUP, 3, V), g(GROUP, 3, V)
            v.idx = g(DEPTH, GROUP, dt=I32)
            v.pidx = g(2, GROUP, dt=I32)
            v.cnt = g(GROUP)
            v.pos = g(GROUP)
            return v

        E = edge_views()

        def node_views():
            g = carve()
            v = type("Node", (), {})
            v.h = g(2, DIM)
            v.hT = g(2, 4, P)
            v.big = g(SLOTS * DIM)
            v.row = g(2, 480)
            v.car = g(2, 4 * 480)
            v.sum = g(2, 480)
            v.c2 = g(480)
            v.c2in = g(480)
            v.idx = g(2, 2, dt=I32)
            v.small = g(8, SLOTS)
            v.smi = g(SLOTS, dt=I32)
            v.rden = g(8)
            return v

        Nv = node_views()

        def l3_views():
            g = carve()
            v = type("L3", (), {})
            v.rb = g(2, 256)
            rows = fore[:, 0:DEPTH * 4 * DIM].rearrange("p (b k t c) -> p b k t c", b=DEPTH, k=2, c=DIM)
            v.gs, v.gd = rows[:, :, 0], rows[:, :, 1]
            v.m = g(2, 2, DIM)
            v.w = g(2, 2, 224)
            v.cv = g(2, 2, 192)
            v.f, v.f2 = g(2, 2, 352), g(2, 2, 352)
            v.t1, v.t2 = g(2, 2, 384), g(2, 2, 384)
            v.al2 = g(2, 64)
            v.dot = g(2, V)
            v.vv = g(2, 3, V)
            v.q, v.u1, v.u2 = g(2, 96), g(2, 96), g(2, 96)
            v.h = g(2, 2, DIM)
            v.idx = g(DEPTH, 2, 2, dt=I32)
            return v

        T = l3_views()

        def pass2_views():
            g = carve()
            v = type("Pass2", (), {})
            v.keys = g(2, 512, dt=I32)
            v.h = g(2, GROUP * DIM)
            v.msg = g(2, GROUP * 164)
            v.sel = g(2, GROUP, P)
            v.run = g(2, GROUP * 164)
            return v

        P2 = pass2_views()

        def scan_views():
            g = carve()
            v = type("Scan", (), {})
            v.aT = g(QK, 4, P)
            v.bw = g(4, P)
            v.fw = g(QK, 4, P)
            v.kI = g(QK, P, dt=I32)
            v.k = g(QK, P)
            v.b = g(P)
            v.b2 = g(P)
            v.edge = g(QK, 4, 2)
            v.lk, v.fk = g(TILES), g(TILES)
            v.lkI, v.fkI = g(TILES, dt=I32), g(TILES, dt=I32)
            v.m = g(2, TILES)
            v.j = g(2, TILES)
            v.c = g(2, TILES)
            v.cT = g(QK, 2, 4)
            return v

        C = scan_views()

        def setup_views():
            g = carve()
            v = type("Setup", (), {})
            v.lkI, v.nfI = g(TILES, dt=I32), g(TILES, dt=I32)
            v.lk, v.nf, v.t, v.j, v.one = g(TILES), g(TILES), g(TILES), g(TILES), g(TILES)
            v.e3 = g(TILES * 3)
            v.n2 = g(TILES)
            v.rowI = g(2, P, dt=I32)
            v.tile_i = g(SLOTS, dt=I32)
            v.node = g(SLOTS)
            v.node_i = g(SLOTS, dt=I32)
            v.tiles = g(SLOTS)
            v.in_tile = g(SLOTS)
            v.end = g(SLOTS)
            v.prev = g(SLOTS)
            v.lkc_i, v.nfc_i = g(QK, dt=I32), g(QK, dt=I32)
            v.lkc, v.nfc, v.tc, v.cc, v.kc = g(QK), g(QK), g(QK), g(QK), g(QK)
            v.zero = g(480)
            return v

        U = setup_views()

        def group_rows(d, width, per):
            return d.rearrange("(g t p) f -> g p t f", t=per, p=P)

        def wmm(k):
            return bank[:, 1 + 2 * k:3 + 2 * k, :].rearrange("p b (t c) -> p (b t) c", c=256)

        @block.sync
        def _(sp):
            n = 0

            def load(dst, src):
                nonlocal n
                sp.dma_start(dst, src).then_inc(loaded, 16)
                n += 16

            load(x[:], a["x"].rearrange("(p j) c -> p j c", j=SLOTS))
            load(attr[:], a["node_vec1"])
            load(src_i[:], a["src"])
            load(dst_i[:], a["dst"])
            load(U.lkI, a["tile_last"].partition_broadcast(P))
            load(U.nfI, a["next_first"].partition_broadcast(P))
            load(U.lkc_i[0:QT], a["last_col"])
            load(U.nfc_i[0:QT], a["next_col"])
            load(U.e3, a["edge_attr_3"])
            load(aux[:, :, 0:4], a["edge_attr_4"])
            assert n == LOADS
            sp.wait_ge(zero_made, 1)
            for table in ([*src_sum] if 0 in layers else []) + [carry[l] for l in (1, 2, 3) if l in layers]:
                width = table.shape[1]
                sp.dma_start(table.rearrange("(p r) f -> p r f", p=P),
                             U.zero[:, 0:width].unsqueeze(1).broadcast_to([P, TABLE_ROWS // P, width])).then_inc(zeroed, 16)
            sp.wait_ge(zeroed, 16 * ((CHAINS if 0 in layers else 0) + len([l for l in layers if l])))
            sp.wait_ge(s.table_in, 1)
            sp.sem_inc(s.table_in, -1)
            sp.dma_start(ends[1:ROWS + 1].rearrange("(p j) o -> p (j o)", j=SLOTS), U.end).then_inc(moved, 16)
            sp.dma_start(ends[0:1], U.zero[0:1, 0:1]).then_inc(moved, 16)
            sp.wait_ge(moved, 32)
            sp.dma_start(U.prev, ends[0:ROWS].rearrange("(p j) o -> p (j o)", j=SLOTS)).then_inc(moved, 16)
            barrier(sp, "sp")

            def table_out(l):
                sp.wait_ge(s.table_in, 1)
                sp.sem_inc(s.table_in, -1)
                if l < 3:
                    sp.dma_start(node_table[l].rearrange("(p j) c -> p (j c)", j=SLOTS),
                                 fore[:, 0:SLOTS * SPEC[l]["table"]]).then_inc(s.carry_in0, 16)
                    sp.wait_ge(s.carry_in0, 16)
                    sp.sem_inc(s.carry_in0, -16)
                else:
                    sp.dma_start(src_table.rearrange("(p j) c -> p (j c)", j=SLOTS),
                                 fore[:, 0:SLOTS * DIM]).then_inc(s.carry_in0, 16)
                    sp.dma_start(dst_table.rearrange("(p j) c -> p j c", j=SLOTS),
                                 skip[:, :, 0:DIM]).then_inc(s.carry_in0, 16)
                    sp.wait_ge(s.carry_in0, 32)
                    sp.sem_inc(s.carry_in0, -32)

            def load_attr(attr_name, k):
                def stage(g, b, first, half):
                    if not first:
                        sp.wait_ge(s.attr_free, 1)
                        sp.sem_inc(s.attr_free, -1)
                    sp.dma_start(E.attr[0:k, b, :],
                                 a[attr_name].rearrange("k (g n) -> k g n", n=512)[:, bass.ds(g, 1), :]
                                 .rearrange("k o n -> k (o n)")).then_inc(s.attr_in0 if b == 0 else s.attr_in1, 16)
                return stage

            def load_keys(name, keys):
                def stage(g, b, first, half):
                    if not first:
                        sp.wait_ge(s.key_free, 1)
                        sp.sem_inc(s.key_free, -1)
                    sp.dma_start(keys[:, b, :],
                                 a[name].rearrange("(g n) -> g n", n=512)[bass.ds(g, 1), :]
                                 .rearrange("o n -> (o n)").partition_broadcast(P)).then_inc(s.key_in0 if b == 0 else s.key_in1, 16)
                return stage

            def stores(l, run, f):
                def stage(g, b, first, half):
                    sp.wait_ge(s.run_ready, GROUP)
                    sp.sem_inc(s.run_ready, -GROUP)
                    sp.dma_start(group_rows(run_rows[l], f, GROUP)[bass.ds(g, 1)].rearrange("o p t f -> (o p) t f"),
                                 run[:, b, 0:GROUP * f].rearrange("p (t f) -> p t f", f=f)).then_inc(
                        s.store0 if b == 0 else s.store1, 16)
                return stage

            def post(l):
                f = SPEC[l]["f"]
                if l:
                    for k in range(QK):
                        if k:
                            sp.wait_ge(s.c2nd_in, 1)
                            sp.sem_inc(s.c2nd_in, -1)
                        sp.dma_start(Nv.c2in[0:QT, 0:f],
                                     run_rows[l].rearrange("(k q p) f -> q k p f", q=QT, p=P)[:, k, P - 1, :]).then_inc(s.row_in0, 16)
                    sp.wait_ge(s.c2nd_in, 1)
                    sp.sem_inc(s.c2nd_in, -1)

                def stage(j, b, first, half):
                    if not first:
                        sp.wait_ge(s.sum_free, 1)
                        sp.sem_inc(s.sum_free, -1)
                    for c in range(1 if l else CHAINS):
                        table = carry[l] if l else src_sum[c]
                        sp.dma_start(Nv.car[:, b, c * f:(c + 1) * f],
                                     table[0:ROWS].rearrange("(p j) f -> j p f", j=SLOTS)[bass.ds(j, 1)]
                                     .rearrange("o p f -> (o p) f")).then_inc(s.carry_in0 if b == 0 else s.carry_in1, 16)
                pipelined(sp, SLOTS, [(0, stage)])
                sp.wait_ge(s.sum_free, 2)
                sp.sem_inc(s.sum_free, -2)

            for l in (0, 1, 2):
                if l not in layers:
                    continue
                table_out(l)
                barrier(sp, "sp")
                stages = [(-3 if l else -2, load_attr(("edge_attr_64", "edge_attr_8", "edge_attr_16")[l], SPEC[l]["k"])),
                          (0, load_keys("src_row" if l == 0 else "dst_row", E.keys))]
                if l:
                    stages.append((2, stores(l, E.run, SPEC[l]["f"])))
                pipelined(sp, GROUPS, stages)
                sp.wait_ge(s.attr_free, 2)
                sp.sem_inc(s.attr_free, -2)
                sp.wait_ge(s.key_free, 2)
                sp.sem_inc(s.key_free, -2)
                barrier(sp, "sp")
                post(l)
                barrier(sp, "sp")
            if 3 in layers:
                table_out(3)
                barrier(sp, "sp")

                def rbf(g, b, first, half):
                    if not first:
                        sp.wait_ge(s.attr_free, 1)
                        sp.sem_inc(s.attr_free, -1)
                    sp.dma_start(T.rb[0:16, b, :],
                                 a["edge_attr_16"].rearrange("k (g n) -> k g n", n=256)[:, bass.ds(g, 1), :]
                                 .rearrange("k o n -> k (o n)")).then_inc(s.attr_in0 if b == 0 else s.attr_in1, 16)

                def keep_h(g, b, first, half):
                    sp.wait_ge(s.h_ready, 1)
                    sp.sem_inc(s.h_ready, -1)
                    sp.dma_start(edge_h.rearrange("(g t p) f -> g p t f", t=2, p=P)[bass.ds(g, 1)]
                                 .rearrange("o p t f -> (o p) t f"), T.h[:, b]).then_inc(s.store0 if b == 0 else s.store1, 16)
                pipelined(sp, TILES // 2, [(0, rbf), (5, keep_h)])
                sp.wait_ge(s.attr_free, 2)
                sp.sem_inc(s.attr_free, -2)
                barrier(sp, "sp")
                sp.dma_start(C.kI[0:QT], a["dst_row"].rearrange("(k q n) -> q k n", q=QT, n=P)).then_inc(s.key_in0, 16)
                sp.dma_start(C.lkI, a["tile_last"].partition_broadcast(P)).then_inc(s.key_in0, 16)
                sp.dma_start(C.fkI, a["tile_first"].partition_broadcast(P)).then_inc(s.key_in0, 16)
                barrier(sp, "sp")

                def load_h(g, b, first, half):
                    if not first:
                        sp.wait_ge(s.attr_free, 1)
                        sp.sem_inc(s.attr_free, -1)
                    sp.dma_start(P2.h[:, b, :].rearrange("p (t f) -> p t f", f=DIM),
                                 group_rows(edge_h, DIM, GROUP)[bass.ds(g, 1)].rearrange("o p t f -> (o p) t f")).then_inc(
                        s.attr_in0 if b == 0 else s.attr_in1, 16)
                pipelined(sp, GROUPS, [(0, load_h), (0, load_keys("dst_row", P2.keys)),
                                       (2, stores(3, P2.run, SPEC[3]["f"]))])
                sp.wait_ge(s.attr_free, 2)
                sp.sem_inc(s.attr_free, -2)
                sp.wait_ge(s.key_free, 2)
                sp.sem_inc(s.key_free, -2)
                barrier(sp, "sp")
                post(3)
                barrier(sp, "sp")
            sp.dma_start(out.rearrange("(p j) c -> p j c", j=SLOTS), x[0:NODES // SLOTS]).then_inc(moved, 16)
            sp.wait_ge(moved, 64)

        @block.gpsimd
        def _(pool):
            own = Steps()
            last_row = pool.to_reg(ROWS - 1)
            last_table_row = pool.to_reg(TABLE_ROWS - 1)
            last_tile = pool.to_reg(TILES)

            def gather(dst, table, idx, bound):
                return pool.indirect_dma_start(dst, None, table, bass.IndirectOffsetOnAxis(ap=idx, axis=0),
                                               bounds_check=bound, oob_is_err=True)

            nc.gpsimd.memset(U.zero, 0.0).then_inc(pool_own, own.step())
            nc.gpsimd.memset(ident[:], 0.0).then_inc(pool_own, own.step())
            nc.gpsimd.memset(lower[:], 1.0).then_inc(pool_own, own.step())
            nc.gpsimd.iota(U.node_i, pattern=[[1, SLOTS]], base=0, channel_multiplier=SLOTS).then_inc(pool_own, own.step())
            nc.gpsimd.iota(U.lk.bitcast(I32), pattern=[[1, TILES]], base=4000, channel_multiplier=0).then_inc(pool_own, own.step())
            nc.gpsimd.iota(U.cc.bitcast(I32), pattern=[[QT, QK]], base=4000, channel_multiplier=1).then_inc(pool_own, own.step())
            nc.gpsimd.iota(U.kc.bitcast(I32), pattern=[[0, QK]], base=ROWS, channel_multiplier=1).then_inc(pool_own, own.step())
            pool.wait_ge(pool_own, own.n)
            nc.gpsimd.affine_select(out=ident[:], in_=ident[:], compare_op=ALU.not_equal, fill=1.0, base=0,
                                        pattern=[[-1, P]], channel_multiplier=1).then_inc(pool_own, own.step())
            nc.gpsimd.affine_select(out=lower[:], in_=lower[:], compare_op=ALU.is_gt, fill=0.0, base=0,
                                        pattern=[[-1, P]], channel_multiplier=1).then_inc(pool_own, own.step())
            pool.wait_ge(pool_own, own.n)
            pool.sem_inc(pool_own, own.reset())
            pool.sem_inc(zero_made, 2)
            pool.wait_ge(s.w_ready, 1)
            pool.sem_inc(s.w_ready, -1)
            for j in range(SLOTS):
                if j >= 2:
                    pool.wait_ge(s.got_free, 1)
                    pool.sem_inc(s.got_free, -1)
                nc.gpsimd.tensor_copy(put_i[:, j:j + 1], U.tile_i[:, j:j + 1]).then_inc(pool_own, own.step())
                pool.wait_ge(pool_own, own.n)
                pool.sem_inc(pool_own, own.reset())
                gather(U.rowI[:, j % 2, :], a["dst_tiles"], put_i[:, j:j + 1], last_tile).then_inc(
                    keys_got[j % 2], 16)
            pool.wait_ge(s.got_free, 2)
            pool.sem_inc(s.got_free, -2)
            barrier(pool, "pool")

            def gathers(l, table, indices, buf, width):
                def stage(g, b, first, half):
                    if not among_first(g, DEPTH):
                        pool.wait_ge(s.got_free, 1)
                        pool.sem_inc(s.got_free, -1)
                    nc.gpsimd.tensor_copy(E.idx[:, b, :], indices[:, bass.ds(g * GROUP, GROUP)]).then_inc(pool_own, own.step())
                    pool.wait_ge(pool_own, own.n)
                    pool.sem_inc(pool_own, own.reset())
                    for t in range(GROUP):
                        gather(buf[:, b, t * width:(t + 1) * width], table, E.idx[:, b, t:t + 1], last_row).then_inc(
                            got[l][b], 16)
                return stage

            def scatter(g, b, first, half):
                for t in range(GROUP):
                    if not (isinstance(g, int) and g == 0):
                        pool.wait_ge(put[t], g * 16)
                    pool.wait_ge(s.run_ready, 1)
                    pool.sem_inc(s.run_ready, -1)
                    if t == 0:
                        nc.gpsimd.tensor_copy(E.pidx[:, b % 2, :], put_i[:, bass.ds(g * GROUP, GROUP)]).then_inc(pool_own, own.step())
                        pool.wait_ge(pool_own, own.n)
                        pool.sem_inc(pool_own, own.reset())
                    pool.indirect_dma_start(
                        src_sum[t], bass.IndirectOffsetOnAxis(ap=E.pidx[:, b % 2, t:t + 1], axis=0),
                        E.run[:, b % 2, t * 480:(t + 1) * 480], None, compute_op=ALU.add,
                        bounds_check=last_table_row, oob_is_err=True).then_inc(put[t], 16)

            def post(l):
                f = SPEC[l]["f"]
                if not l:
                    return
                for k in range(QK):
                    pool.wait_ge(s.c2nd_sb, 1)
                    pool.sem_inc(s.c2nd_sb, -1)
                    pool.indirect_dma_start(
                        carry[l], bass.IndirectOffsetOnAxis(ap=put2_i[:, k:k + 1], axis=0),
                        Nv.c2[0:QT, 0:f], None, compute_op=ALU.add,
                        bounds_check=last_table_row, oob_is_err=True).then_inc(carried[l], 16)
                    pool.wait_ge(carried[l], 16 * (k + 1))
                    pool.sem_inc(s.c2nd_in, 1)

                def stage(j, b, first, half):
                    if not first:
                        pool.wait_ge(s.got_free, 1)
                        pool.sem_inc(s.got_free, -1)
                    nc.gpsimd.tensor_copy(Nv.idx[:, b, 0:1], last_i[:, bass.ds(j, 1)]).then_inc(pool_own, own.step())
                    pool.wait_ge(pool_own, own.n)
                    pool.sem_inc(pool_own, own.reset())
                    gather(Nv.row[:, b, 0:f], run_rows[l], Nv.idx[:, b, 0:1], last_edge).then_inc(
                        rows_got[l][b], 16)
                pipelined(pool, SLOTS, [(0, stage)])
                pool.wait_ge(s.got_free, 2)
                pool.sem_inc(s.got_free, -2)

            last_edge = pool.to_reg(TILES * P - 1)
            for l in (0, 1, 2):
                if l not in layers:
                    continue
                barrier(pool, "pool")
                stages = [(0, gathers(l, node_table[l], src_i if l else dst_i, E.got, SPEC[l]["table"]))]
                if l == 0:
                    stages.append((2, scatter))
                pipelined(pool, GROUPS, stages, unroll=DEPTH)
                pool.wait_ge(s.got_free, DEPTH)
                pool.sem_inc(s.got_free, -DEPTH)
                barrier(pool, "pool")
                post(l)
                barrier(pool, "pool")
            if 3 in layers:
                barrier(pool, "pool")

                def gather_both(g, b, first, half):
                    nc.gpsimd.tensor_copy(T.idx[:, b, 0, :], src_i[:, bass.ds(g * 2, 2)]).then_inc(pool_own, own.step())
                    nc.gpsimd.tensor_copy(T.idx[:, b, 1, :], dst_i[:, bass.ds(g * 2, 2)]).then_inc(pool_own, own.step())
                    pool.wait_ge(pool_own, own.n)
                    pool.sem_inc(pool_own, own.reset())
                    for t in range(2):
                        gather(T.gs[:, b, t, :], src_table, T.idx[:, b, 0, t:t + 1], last_row).then_inc(
                            got[3][b], 16)
                        gather(T.gd[:, b, t, :], dst_table, T.idx[:, b, 1, t:t + 1], last_row).then_inc(
                            got[3][b], 16)

                def add_both(g, b, first, half):
                    pool.wait_ge(got[3][b], (half + 1) * 64)
                    if not among_first(g, 2):
                        pool.wait_ge(s.got_free, 1)
                        pool.sem_inc(s.got_free, -1)
                    nc.gpsimd.tensor_tensor(T.m[:, b % 2], T.gs[:, b], T.gd[:, b], ALU.add).then_inc(s.m_ready, 1)
                pipelined(pool, TILES // 2, [(2, add_both), (0, gather_both)], unroll=DEPTH)
                pool.wait_ge(s.got_free, 2)
                pool.sem_inc(s.got_free, -2)
                barrier(pool, "pool")
                barrier(pool, "pool")
                barrier(pool, "pool")
                post(3)
                barrier(pool, "pool")

        BY_Y0 = ((0, 0, 64), (64, 128, 32), (96, 64, 64), (160, 160, 64))

        @block.scalar
        def _(act):
            own = Steps()

            def wload(dst, src):
                act.dma_start(dst, src).then_inc(weights_in, 16)
                wload.n += 16
            wload.n = 0
            for name, key in (("fc1_0", "L0_gnn_W_fc1"), ("fc2_0", "L0_gnn_W_fc2"), ("fc1_1", "L1_gnn_fcW1"),
                              ("fc1_2", "L2_gnn_Wfc1"),
                              ("f_s0", "L0_gnn_W_nl0"), ("f_v0", "L0_gnn_W_nl1"), ("k_s0", "L0_gnn_W_skip0"), ("k_v0", "L0_gnn_W_skip1"),
                              ("f_s1", "L1_gnn_W1_s"), ("f_v1", "L1_gnn_W1_v"), ("k_s1", "L1_gnn_W_sc_s"), ("k_v1", "L1_gnn_W_sc_v"),
                              ("f_s2", "L2_gnn_Wl1_0"), ("f_v2", "L2_gnn_Wl1_1"), ("k_s2", "L2_gnn_Wsc0"), ("k_v2", "L2_gnn_Wsc1"),
                              ("f_s3", "L3_gnn_Ws_src"), ("f_v3", "L3_gnn_Wv_src"), ("k_s3", "L3_gnn_Ws_dst"), ("k_v3", "L3_gnn_Wv_dst"),
                              ("out_s0", "L0_gnn_W_out_s"), ("out_v0", "L0_gnn_W_out_v"),
                              ("out_s1", "L1_gnn_W2_s"), ("out_v1", "L1_gnn_W2_v"), ("out_a1", "L1_gnn_W3"),
                              ("out_s2", "L2_gnn_Wl2_s"), ("out_v2", "L2_gnn_Wl2_v"), ("out_a2", "L2_gnn_Wa"),
                              ("out_s3", "L3_gnn_Wps"), ("out_v3", "L3_gnn_Wpv"), ("gate", "L3_gnn_Wg"), ("lin_s", "L3_gnn_Ws_vlin")):
                wload(wt[name][:], a[key])
            for name, key in (("fc2_1", "L1_gnn_fcW2"), ("fc2_2", "L2_gnn_Wfc2"), ("rbf", "L3_gnn_W_rbf")):
                for to, at, n in BY_Y0:
                    n = min(n, wt[name].shape[1] - to)
                    wload(wt[name][:, to:to + n], a[key][:, at:at + n])
            wload(wt["val_s"][:, 32:96], a["L3_gnn_Ws_val"])
            wload(wt["val_s"][:, 96:160], a["L3_gnn_W_alpha"])
            wload(val_sT[:], a["Ws_val_T"])
            for col, key in ((0, "L3_gnn_gamma_s"), (1, "L3_gnn_beta_s"), (2, "L3_gnn_gamma_v")):
                wload((gamma_s, beta_s, gamma_v)[col][:], a[key])
            wload(alpha_dot[:], a["L3_gnn_alpha_dot"].partition_broadcast(P))
            wload(w2[0:64, 0:1], a["L3_gnn_w2_ss"])
            wload(w2[64:96, 0:1], a["L3_gnn_w2_vv0"])
            wload(w2[0:64, 1:2], a["L3_gnn_w2_sv"])
            for at, col, key in ((64, 1, "w2_vs"), (96, 1, "w2_vv1"), (0, 2, "w2_vs"), (32, 2, "w2_vv1"),
                                 (64, 2, "w2_vs"), (96, 2, "w2_vv1")):
                wload(w2[at:at + 32, col:col + 1], a["L3_gnn_" + key])
            act.wait_ge(weights_in, wload.n)
            act.wait_ge(s.hid_ready, 1)
            act.sem_inc(s.hid_ready, -1)
            for name, key in (("val", "L3_gnn_Wv_val"), ("lin", "L3_gnn_Wv_vlin")):
                wload(wt[name + "_x"][0:64, 0:32], a[key][0:64])
                wload(wt[name + "_x"][64:128, 32:64], a[key][64:128])
                wload(wt[name + "_yz"][0:64, 64:96], a[key][64:128])
                wload(wt[name + "_yz"][64:128, 96:128], a[key][64:128])
            act.wait_ge(weights_in, wload.n)
            act.sem_inc(s.weights_ready, 1)
            act.wait_ge(s.gate_mm, 1)
            act.sem_inc(s.gate_mm, -1)
            act.activation(wt["val_s"][:, 0:32], bank[0:96, 0, 0:32], ACT.Copy).then_inc(act_own, own.step())
            act.wait_ge(act_own, own.n)
            act.sem_inc(act_own, own.reset())
            act.sem_inc(s.hid_free, 1)
            act.wait_ge(s.hid_ready, 1)
            act.sem_inc(s.hid_ready, -1)

            def root(t, v):
                act.wait_ge(s.root_asked, 1)
                act.sem_inc(s.root_asked, -1)
                act.activation(t, v, ACT.Sqrt).then_inc(s.root_done, 1)
            root(U.j, U.n2)
            barrier(act, "act")

            def prep(l):
                for row in (0,) if l < 3 else (0, 2, 4):
                    root(stats[:, 8, :], stats[:, row, :])

                def features(j, b, first, half):
                    act.wait_ge(s.node_in, 1)
                    act.sem_inc(s.node_in, -1)
                    if l < 3:
                        act.activation(Nv.h[:, b, :], x[:, bass.ds(j, 1), :].rearrange("p o c -> p (o c)"), ACT.Relu,
                                       bias=stats[:, 1, bass.ds(j, 1)], scale=stats[:, 0, bass.ds(j, 1)]).then_inc(s.h_ready, 1)
                    else:
                        act.activation(Nv.h[:, b, :], fore[:, bass.ds(j * DIM, DIM)], ACT.Copy).then_inc(s.h_ready, 1)

                def turned(j, b, first, half):
                    act.wait_ge(s.node_t, 1)
                    act.sem_inc(s.node_t, -1)
                    if l < 3:
                        act.activation(Nv.hT[0:64, b, 0, :], bank[0:64, b, 0:128], ACT.Copy).then_inc(act_own, own.step())
                        act.activation(Nv.hT[0:32, b, 1:4, :], bank[0:32, b, 128:512].rearrange("p (i n) -> p i n", i=3),
                                       ACT.Copy).then_inc(s.node_tsb, 1)
                    else:
                        act.activation(Nv.hT[0:64, b, 0, :], bank[0:64, b, 0:128], ACT.Identity,
                                           bias=beta_s[:], scale=gamma_s[:]).then_inc(act_own, own.step())
                        act.activation(Nv.hT[0:32, b, 1:4, :], bank[0:32, b, 128:512].rearrange("p (i n) -> p i n", i=3),
                                       ACT.Copy, scale=gamma_v[:]).then_inc(s.node_tsb, 1)
                    act.wait_ge(act_own, own.n)
                    act.sem_inc(act_own, own.reset())
                pipelined(act, SLOTS, [(0, features), (1, turned)])

            def hidden(l):
                def stage(g, part, first, half):
                    b = part % 2
                    act.wait_ge(s.hid_mm, 1)
                    act.sem_inc(s.hid_mm, -1)
                    act.sem_inc(s.attr_free, 1)
                    if l == 0 and not first:
                        act.wait_ge(s.hid_free, 1)
                        act.sem_inc(s.hid_free, -1)
                    act.activation(E.hid[0:64, b, :], bank[0:64, 0 if l else 7 * b, :], ACT.Relu if l == 0 else ACT.Silu,
                                   scale=(1.0, 8 ** -0.5, 0.25)[l]).then_inc(s.hid_ready, 1)
                return stage

            def weights_out(g, part, first, half):
                b = part % 2
                act.wait_ge(s.w_ready, 1)
                act.sem_inc(s.w_ready, -1)
                if not first:
                    act.wait_ge(s.w_free, 1)
                    act.sem_inc(s.w_free, -1)
                for t in range(GROUP):
                    act.activation(E.w[:, b, t, 0:96], wmm(b)[:, t, 0:96], ACT.Copy,
                                   scale=y[:, bass.ds(g * GROUP + t, 1), 0]).then_inc(act_own, own.step())
                act.activation(E.w[:, b, :, 96:192], wmm(b)[:, :, 96:192], ACT.Copy).then_inc(act_own, own.step())
                act.wait_ge(act_own, own.n)
                act.sem_inc(act_own, own.reset())
                act.sem_inc(s.wy_ready, 1)

            def evacuate(l, run):
                f, store = SPEC[l]["f"], l > 0

                def stage(g, part, first, half):
                    b = part % 2
                    if store and not first:
                        act.wait_ge(s.store0 if b == 0 else s.store1, 16)
                        act.sem_inc(s.store0 if b == 0 else s.store1, -16)
                    for t in range(GROUP):
                        if not store and not first:
                            act.wait_ge(put[t], (g - 1) * 16)
                        act.wait_ge(s.run_mm, 1)
                        act.sem_inc(s.run_mm, -1)
                        if t == GROUP - 1:
                            act.sem_inc(s.msg_free, 1)
                        act.activation(run[:, b, t * f:(t + 1) * f], bank[:, 5 + (part * GROUP + t) % RUN_BANKS[l], 0:f], ACT.Copy).then_inc(act_own, own.step())
                        act.wait_ge(act_own, own.n)
                        act.sem_inc(act_own, own.reset())
                        act.sem_inc(s.run_free, 1)
                        act.sem_inc(s.run_ready, 1)
                return stage

            def post(l):
                f, vec = SPEC[l]["f"], SPEC[l]["vec"]
                top = 64 if l == 3 else 96
                if l:
                    for k in range(QK):
                        act.wait_ge(s.c2nd_mm, 1)
                        act.sem_inc(s.c2nd_mm, -1)
                        act.activation(Nv.c2[0:QT, 0:f], bank[0:QT, 4, 0:f], ACT.Copy).then_inc(s.c2nd_sb, 1)

                def turned(j, b, first, half):
                    act.wait_ge(s.node_t, 1)
                    act.sem_inc(s.node_t, -1)
                    act.activation(Nv.hT[0:top, b, 0, :], bank[0:top, b, 0:128], ACT.Copy).then_inc(act_own, own.step())
                    act.activation(Nv.hT[0:vec, b, 1:4, :], bank[0:vec, b, 128:512].rearrange("p (i n) -> p i n", i=3),
                                   ACT.Copy).then_inc(s.node_tsb, 1)
                    act.wait_ge(act_own, own.n)
                    act.sem_inc(act_own, own.reset())
                pipelined(act, SLOTS, [(0, turned)])
                if l == 0:
                    o = fore[:, 0:SLOTS * 192].rearrange("p (j c) -> p j c", c=192)
                    act.wait_ge(s.vt_ready, 1)
                    act.sem_inc(s.vt_ready, -1)
                    act.activation(skip[:, :, 0:96], o[:, :, 0:96], ACT.Sigmoid).then_inc(act_own, own.step())
                    act.wait_ge(act_own, own.n)
                    act.sem_inc(act_own, own.reset())
                    act.sem_inc(s.gate_ready, 1)
                if l == 1:
                    act.wait_ge(s.vt_ready, 1)
                    act.sem_inc(s.vt_ready, -1)
                    act.activation(Nv.small[:, 4:6, :], Nv.small[:, 2:4, :], ACT.Sin, scale=2 * math.pi).then_inc(act_own, own.step())
                    act.wait_ge(act_own, own.n)
                    act.sem_inc(act_own, own.reset())
                    act.sem_inc(s.gate_ready, 1)

            for l in (0, 1, 2):
                if l not in layers:
                    continue
                prep(l)
                barrier(act, "act")
                evacuating = (1, evacuate(l, E.run))
                pipelined(act, GROUPS, [evacuating, (-2, weights_out), (-3, hidden(l))] if l else [(-2, hidden(l)), evacuating],
                          unroll=2 * RUN_BANKS[l])
                if l == 0:
                    for t in range(GROUP):
                        act.wait_ge(put[t], GROUPS * 16)
                else:
                    act.wait_ge(s.store0, 16)
                    act.sem_inc(s.store0, -16)
                    act.wait_ge(s.store1, 16)
                    act.sem_inc(s.store1, -16)
                if l == 0:
                    act.wait_ge(s.hid_free, 2)
                    act.sem_inc(s.hid_free, -2)
                else:
                    act.wait_ge(s.w_free, 2)
                    act.sem_inc(s.w_free, -2)
                barrier(act, "act")
                post(l)
                barrier(act, "act")
            if 3 in layers:
                prep(3)
                barrier(act, "act")

                def m1_turned(g, b, first, half):
                    act.wait_ge(s.t1_mm, 1)
                    act.sem_inc(s.t1_mm, -1)
                    act.activation(T.t1[0:96, b, :, 0:128], bank[0:96, 1:3, 0:128], ACT.Copy).then_inc(act_own, own.step())
                    act.activation(T.t1[:, b, :, 128:384], bank[:, 1:3, 128:384], ACT.Copy).then_inc(act_own, own.step())
                    act.wait_ge(act_own, own.n)
                    act.sem_inc(act_own, own.reset())
                    act.sem_inc(s.t1_ready, 1)

                def weights_by_y0_3(g, b, first, half):
                    act.wait_ge(s.w_ready, 1)
                    act.sem_inc(s.w_ready, -1)
                    act.sem_inc(s.attr_free, 1)
                    for t in range(2):
                        act.activation(T.w[:, b, t, 0:96], bank[:, 0, t * 256:t * 256 + 96], ACT.Copy,
                                       scale=y[:, bass.ds(g * 2 + t, 1), 0]).then_inc(act_own, own.step())
                    act.activation(T.w[:, b, :, 96:224], bank[:, 0, :].rearrange("p (t c) -> p t c", t=2)[:, :, 96:224],
                                   ACT.Copy).then_inc(act_own, own.step())
                    act.wait_ge(act_own, own.n)
                    act.sem_inc(act_own, own.reset())
                    act.sem_inc(s.wy_ready, 1)
                    act.sem_inc(s.w_free, 1)

                def values_out(g, b, first, half):
                    act.wait_ge(s.c1_mm, 1)
                    act.sem_inc(s.c1_mm, -1)
                    c1 = bank[:, 6:8, 0:288]
                    act.activation(T.f2[:, b, :, 64:160], c1[:, :, 0:96], ACT.Sigmoid).then_inc(act_own, own.step())
                    act.activation(T.cv[:, b], c1[:, :, 96:288], ACT.Copy).then_inc(act_own, own.step())
                    act.wait_ge(act_own, own.n)
                    for t in range(2):
                        act.activation(T.f2[:, b, t, 0:64], T.f2[:, b, t, 96:160], ACT.Copy,
                                       scale=y[:, bass.ds(g * 2 + t, 1), 0]).then_inc(act_own, own.step())
                    act.wait_ge(act_own, own.n)
                    act.sem_inc(act_own, own.reset())
                    act.sem_inc(s.gate_ready, 1)

                def m2_turned(g, b, first, half):
                    act.wait_ge(s.t2_mm, 1)
                    act.sem_inc(s.t2_mm, -1)
                    act.activation(T.t2[0:96, b, :, 0:128], bank[0:96, 4:6, 0:128], ACT.Copy).then_inc(act_own, own.step())
                    act.activation(T.t2[:, b, :, 128:384], bank[:, 4:6, 128:384], ACT.Copy).then_inc(act_own, own.step())
                    act.wait_ge(act_own, own.n)
                    act.sem_inc(act_own, own.reset())
                    act.sem_inc(s.t2_ready, 1)

                def scalars_out(g, b, first, half):
                    if not first:
                        act.wait_ge(s.store0 if b == 0 else s.store1, 16)
                        act.sem_inc(s.store0 if b == 0 else s.store1, -16)
                    act.wait_ge(s.c2_mm, 1)
                    act.sem_inc(s.c2_mm, -1)
                    act.activation(T.h[:, b, :, 0:64], bank[:, 3, 0:384].rearrange("p (t c) -> p t c", t=2)[:, :, 0:64],
                                   ACT.Copy).then_inc(s.hs_ready, 1)
                pipelined(act, TILES // 2, [(-1, m1_turned), (1, scalars_out), (-1, values_out), (0, m2_turned), (-3, weights_by_y0_3)])
                act.wait_ge(s.store0, 16)
                act.sem_inc(s.store0, -16)
                act.wait_ge(s.store1, 16)
                act.sem_inc(s.store1, -16)
                barrier(act, "act")
                for k in range(QK):
                    act.wait_ge(s.scan_t, 1)
                    act.sem_inc(s.scan_t, -1)
                    act.activation(C.aT[0:QT, k], bank[0:QT, k % 2, :].rearrange("p (h n) -> p h n", h=4), ACT.Copy).then_inc(s.scan_sb, 1)
                act.wait_ge(s.hid_ready, 1)
                act.sem_inc(s.hid_ready, -1)
                act.activation(aux[:, :, 0:4], aux[:, :, 0:4], ACT.Exp).then_inc(act_own, own.step())
                act.wait_ge(act_own, own.n)
                act.sem_inc(act_own, own.reset())
                barrier(act, "act")
                pipelined(act, GROUPS, [(1, evacuate(3, P2.run))], unroll=2 * RUN_BANKS[3])
                act.wait_ge(s.store0, 16)
                act.sem_inc(s.store0, -16)
                act.wait_ge(s.store1, 16)
                act.sem_inc(s.store1, -16)
                barrier(act, "act")
                post(3)
                barrier(act, "act")

        @block.tensor
        def _(pe):
            pe.wait_ge(s.weights_ready, 1)
            pe.sem_inc(s.weights_ready, -1)
            nc.tensor.matmul(bank[0:96, 0, 0:32], val_sT[:], wt["gate"][:], start=True, stop=True).then_inc(s.gate_mm, 1)
            barrier(pe, "pe")

            def turn(l, what, j, b, blocks):
                for i, (c0, step, w) in enumerate(blocks):
                    last = nc.tensor.transpose(bank[0:w, b, i * P:(i + 1) * P], what[:, b, c0:c0 + step * (w - 1) + 1:step], ident[:])
                last.then_inc(s.node_t, 1)

            def prep(l):
                blocks = [(0, 1, 64)] + [(64 + i, 3, 32) if l < 3 else (64 + 32 * i, 1, 32) for i in range(3)]

                def turns(j, b, first, half):
                    pe.wait_ge(s.h_ready, 1)
                    pe.sem_inc(s.h_ready, -1)
                    turn(l, Nv.h, j, b, blocks)

                def products(j, b, first, half):
                    pe.wait_ge(s.node_tsb, 1)
                    pe.sem_inc(s.node_tsb, -1)
                    if not first:
                        pe.wait_ge(s.node_free, 1)
                        pe.sem_inc(s.node_free, -1)
                    o = bank[:, 2 + b, :]
                    ks = 96 if l == 0 else 64
                    nc.tensor.matmul(o[:, 0:64], Nv.hT[0:64, b, 0, :], wt[f"f_s{l}"][:], start=True, stop=True)
                    nc.tensor.matmul(o[:, 160:160 + ks], Nv.hT[0:64, b, 0, :], wt[f"k_s{l}"][:], start=True, stop=True)
                    for i in range(3):
                        nc.tensor.matmul(o[:, 64 + V * i:96 + V * i], Nv.hT[0:32, b, 1 + i, :], wt[f"f_v{l}"][:], start=True, stop=True)
                        last = nc.tensor.matmul(o[:, 160 + ks + V * i:192 + ks + V * i], Nv.hT[0:32, b, 1 + i, :], wt[f"k_v{l}"][:],
                                                start=True, stop=True)
                    last.then_inc(s.node_mm, 1)
                pipelined(pe, SLOTS, [(0, turns), (1, products)])
                pe.wait_ge(s.node_free, 2)
                pe.sem_inc(s.node_free, -2)

            def hidden(l):
                def stage(g, part, first, half):
                    b = part % 2
                    pe.wait_ge(s.attr_in0 if b == 0 else s.attr_in1, 16)
                    pe.sem_inc(s.attr_in0 if b == 0 else s.attr_in1, -16)
                    k = SPEC[l]["k"]
                    nc.tensor.matmul(bank[0:64, 0 if l else 7 * b, :], wt[f"fc1_{l}"][:], E.attr[0:k, b, :], start=True, stop=True).then_inc(s.hid_mm, 1)
                return stage

            def edge_weights(l):
                def stage(g, part, first, half):
                    b = part % 2
                    pe.wait_ge(s.hid_ready, 1)
                    pe.sem_inc(s.hid_ready, -1)
                    if l == 0 and not first:
                        pe.wait_ge(s.w_free, 1)
                        pe.sem_inc(s.w_free, -1)
                    for t in range(GROUP):
                        last = nc.tensor.matmul(wmm(b)[:, t, 0:SPEC[l]["w"]], E.hid[0:64, b, t * P:(t + 1) * P], wt[f"fc2_{l}"][:],
                                                start=True, stop=True)
                    last.then_inc(s.w_ready, 1)
                return stage

            def sums(l, sel, msg):
                f = SPEC[l]["f"]

                def stage(g, part, first, half):
                    b = part % 2
                    pe.wait_ge(s.msg_ready, 1)
                    pe.sem_inc(s.msg_ready, -1)
                    for t in range(GROUP):
                        if not (among_first(g, 1) and t < RUN_BANKS[l]):
                            pe.wait_ge(s.run_free, 1)
                            pe.sem_inc(s.run_free, -1)
                        nc.tensor.matmul(bank[:, 5 + (part * GROUP + t) % RUN_BANKS[l], 0:f], sel[:, b, t, :], msg[:, b, t * f:(t + 1) * f],
                                         start=True, stop=True).then_inc(s.run_mm, 1)
                return stage

            def post(l):
                f, vec = SPEC[l]["f"], SPEC[l]["vec"]
                top = 64 if l == 3 else 96
                out_s = SPEC[l]["out_s"]
                if l:
                    for k in range(QK):
                        pe.wait_ge(s.row_in0, 16)
                        pe.sem_inc(s.row_in0, -16)
                        nc.tensor.matmul(bank[0:QT, 4, 0:f], sel2[:, k, :], Nv.c2in[0:QT, 0:f], start=True, stop=True).then_inc(s.c2nd_mm, 1)

                def turns(j, b, first, half):
                    pe.wait_ge(s.sum_ready, 1)
                    pe.sem_inc(s.sum_ready, -1)
                    turn(l, Nv.sum, j, b, [(0, 1, top)] + [(top + vec * i, 1, vec) for i in range(3)])

                def products(j, b, first, half):
                    pe.wait_ge(s.node_tsb, 1)
                    pe.sem_inc(s.node_tsb, -1)
                    if not first:
                        pe.wait_ge(s.node_free, 1)
                        pe.sem_inc(s.node_free, -1)
                    o = bank[:, 2 + b, :]
                    last = nc.tensor.matmul(o[:, 0:out_s], Nv.hT[0:top, b, 0, :], wt[f"out_s{l}"][:], start=True, stop=True)
                    for i in range(3):
                        last = nc.tensor.matmul(o[:, out_s + V * i:out_s + V * (i + 1)], Nv.hT[0:vec, b, 1 + i, :], wt[f"out_v{l}"][:],
                                                start=True, stop=True)
                    if l in (1, 2):
                        last = nc.tensor.matmul(o[:, 160:161], Nv.hT[0:96, b, 0, :], wt[f"out_a{l}"][:], start=True, stop=True)
                    last.then_inc(s.node_mm, 1)
                pipelined(pe, SLOTS, [(0, turns), (1, products)])
                pe.wait_ge(s.node_free, 2)
                pe.sem_inc(s.node_free, -2)

            for l in (0, 1, 2):
                if l not in layers:
                    continue
                prep(l)
                barrier(pe, "pe")
                summing = (1, sums(l, E.sel, E.msg))
                pipelined(pe, GROUPS, [summing, (-2, edge_weights(l)), (-3, hidden(l))] if l else
                          [(-2, hidden(l)), summing, (-1, edge_weights(l))], unroll=2 * RUN_BANKS[l])
                pe.wait_ge(s.run_free, RUN_BANKS[l])
                pe.sem_inc(s.run_free, -RUN_BANKS[l])
                if l == 0:
                    pe.wait_ge(s.w_free, 2)
                    pe.sem_inc(s.w_free, -2)
                barrier(pe, "pe")
                post(l)
                barrier(pe, "pe")
            if 3 in layers:
                prep(3)
                barrier(pe, "pe")

                def edge_w3(g, b, first, half):
                    pe.wait_ge(s.attr_in0 if b == 0 else s.attr_in1, 16)
                    pe.sem_inc(s.attr_in0 if b == 0 else s.attr_in1, -16)
                    if not among_first(g, 1):
                        pe.wait_ge(s.w_free, 1)
                        pe.sem_inc(s.w_free, -1)
                    for t in range(2):
                        last = nc.tensor.matmul(bank[:, 0, t * 256:t * 256 + 224], T.rb[0:16, b, t * P:(t + 1) * P], wt["rbf"][:],
                                                start=True, stop=True)
                    last.then_inc(s.w_ready, 1)

                def turn3(f, b, at, signal):
                    for t in range(2):
                        nc.tensor.transpose(bank[0:96, at + t, 0:128], f[:, b, t, 0:96], ident[:])
                        nc.tensor.transpose(bank[:, at + t, 128:256], f[:, b, t, 96:224], ident[:])
                        last = nc.tensor.transpose(bank[:, at + t, 256:384], f[:, b, t, 224:352], ident[:])
                    last.then_inc(signal, 1)

                def turn_m1(g, b, first, half):
                    pe.wait_ge(s.f_ready, 1)
                    pe.sem_inc(s.f_ready, -1)
                    turn3(T.f, b, 1, s.t1_mm)

                def values(g, b, first, half):
                    pe.wait_ge(s.t1_ready, 1)
                    pe.sem_inc(s.t1_ready, -1)
                    for t in range(2):
                        o = bank[:, 6 + t, :]
                        nc.tensor.matmul(o[:, 0:160], T.t1[0:96, b, t, 0:128], wt["val_s"][:], start=True, stop=True)
                        nc.tensor.matmul(o[:, 160:288], T.t1[:, b, t, 128:256], wt["val_x"][:], start=True, stop=False)
                        last = nc.tensor.matmul(o[:, 160:288], T.t1[:, b, t, 256:384], wt["val_yz"][:], start=False, stop=True)
                    last.then_inc(s.c1_mm, 1)

                def turn_m2(g, b, first, half):
                    pe.wait_ge(s.f2_ready, 1)
                    pe.sem_inc(s.f2_ready, -1)
                    turn3(T.f2, b, 4, s.t2_mm)

                def linear(g, b, first, half):
                    pe.wait_ge(s.t2_ready, 1)
                    pe.sem_inc(s.t2_ready, -1)
                    if not (isinstance(g, int) and g == 0):
                        pe.wait_ge(s.c2_free, 1)
                        pe.sem_inc(s.c2_free, -1)
                    for t in range(2):
                        o = bank[:, 3, t * 192:(t + 1) * 192]
                        nc.tensor.matmul(o[:, 0:64], T.t2[0:96, b, t, 0:128], wt["lin_s"][:], start=True, stop=True)
                        nc.tensor.matmul(o[:, 64:192], T.t2[:, b, t, 128:256], wt["lin_x"][:], start=True, stop=False)
                        last = nc.tensor.matmul(o[:, 64:192], T.t2[:, b, t, 256:384], wt["lin_yz"][:], start=False, stop=True)
                    last.then_inc(s.c2_mm, 1)
                pipelined(pe, TILES // 2, [(-1, turn_m1), (1, linear), (-1, values), (0, turn_m2), (-3, edge_w3)])
                pe.wait_ge(s.c2_free, 1)
                pe.sem_inc(s.c2_free, -1)
                pe.wait_ge(s.w_free, 1)
                pe.sem_inc(s.w_free, -1)
                barrier(pe, "pe")
                for k in range(QK):
                    if k >= 2:
                        pe.wait_ge(s.scan_free, 1)
                        pe.sem_inc(s.scan_free, -1)
                    for h in range(4):
                        last = nc.tensor.transpose(bank[0:QT, k % 2, h * P:(h + 1) * P], aux[:, k * QT:(k + 1) * QT, h], ident[:])
                    last.then_inc(s.scan_t, 1)
                pe.wait_ge(s.scan_free, 2)
                pe.sem_inc(s.scan_free, -2)
                pe.wait_ge(s.scan_mm, 1)
                pe.sem_inc(s.scan_mm, -1)
                for e in range(2):
                    for k in range(QK):
                        last = nc.tensor.transpose(bank[0:4, 2 + 2 * e + k // 4, (k % 4) * QT:(k % 4 + 1) * QT], C.edge[0:QT, k, :, e],
                                                   ident[0:QT, 0:QT])
                last.then_inc(s.vt_mm, 1)
                pe.wait_ge(s.scan_mm, 1)
                pe.sem_inc(s.scan_mm, -1)
                for k in range(QK):
                    for e in range(2):
                        last = nc.tensor.transpose(bank[0:QT, 6, (2 * k + e) * 4:(2 * k + e) * 4 + 4], C.c[0:4, e, k * QT:(k + 1) * QT],
                                                   ident[0:4, 0:4])
                last.then_inc(s.vt_mm, 1)
                for k in range(QK):
                    pe.wait_ge(s.scan_mm, 1)
                    pe.sem_inc(s.scan_mm, -1)
                    if k >= 2:
                        pe.wait_ge(s.scan_free, 1)
                        pe.sem_inc(s.scan_free, -1)
                    for h in range(4):
                        last = nc.tensor.transpose(bank[:, k % 2, h * QT:(h + 1) * QT], C.fw[0:QT, k, h, :], ident[0:QT, 0:QT])
                    last.then_inc(s.vt_mm, 1)
                pe.wait_ge(s.scan_free, 2)
                pe.sem_inc(s.scan_free, -2)
                barrier(pe, "pe")
                pipelined(pe, GROUPS, [(1, sums(3, P2.sel, P2.msg))], unroll=2 * RUN_BANKS[3])
                pe.wait_ge(s.run_free, RUN_BANKS[3])
                pe.sem_inc(s.run_free, -RUN_BANKS[3])
                barrier(pe, "pe")
                post(3)
                barrier(pe, "pe")

        @block.vector
        def _(dve):
            V_ = nc.vector
            c = Steps()

            def tt(o, p, q, op):
                return V_.tensor_tensor(o, p, q, op)

            def bc(ap, axis, n):
                v = ap.unsqueeze(axis)
                shape = list(v.shape)
                shape[axis] = n
                return v.broadcast_to(shape)

            def inverse_root(v, width, eps, t, r):
                V_.tensor_scalar(v, v, 1.0 / width, eps, ALU.mult, ALU.add).then_inc(dve_own, c.step())
                dve.wait_ge(dve_own, c.n)
                dve.sem_inc(s.root_asked, 1)
                dve.wait_ge(s.root_done, 1)
                dve.sem_inc(s.root_done, -1)
                V_.reciprocal(r, t).then_inc(dve_own, c.step())
                dve.wait_ge(dve_own, c.n)
                tt(t, r, r, ALU.mult).then_inc(dve_own, c.step())
                dve.wait_ge(dve_own, c.n)
                tt(t, t, v, ALU.mult).then_inc(dve_own, c.step())
                dve.wait_ge(dve_own, c.n)
                V_.tensor_scalar(t, t, -0.5, 1.5, ALU.mult, ALU.add).then_inc(dve_own, c.step())
                dve.wait_ge(dve_own, c.n)
                tt(v, r, t, ALU.mult).then_inc(dve_own, c.step())
                dve.wait_ge(dve_own, c.n)

            V_.memset(wt["val_x"][:], 0.0).then_inc(dve_own, c.step())
            dve.wait_ge(dve_own, c.n)
            V_.memset(wt["lin_x"][:], 0.0).then_inc(dve_own, c.step())
            dve.wait_ge(dve_own, c.n)
            V_.memset(wt["val_yz"][:], 0.0).then_inc(dve_own, c.step())
            dve.wait_ge(dve_own, c.n)
            V_.memset(wt["lin_yz"][:], 0.0).then_inc(dve_own, c.step())
            dve.wait_ge(dve_own, c.n)
            dve.sem_inc(s.hid_ready, 2)
            dve.wait_ge(zero_made, 2)
            V_.tensor_copy(U.node, U.node_i).then_inc(dve_own, c.step())
            V_.tensor_copy(U.t, U.lk.bitcast(I32)).then_inc(dve_own, c.step())
            V_.tensor_copy(U.tc, U.cc.bitcast(I32)).then_inc(dve_own, c.step())
            V_.tensor_copy(U.prev[:, 0:QK], U.kc.bitcast(I32)).then_inc(dve_own, c.step())
            dve.wait_ge(dve_own, c.n)
            V_.tensor_copy(spare[:], U.prev[:, 0:1]).then_inc(dve_own, c.step())
            dve.wait_ge(dve_own, c.n)
            dve.wait_ge(loaded, LOADS)
            V_.tensor_copy(src_f[:], src_i[:]).then_inc(dve_own, c.step())
            V_.tensor_copy(dst_f[:], dst_i[:]).then_inc(dve_own, c.step())
            V_.tensor_copy(U.lk, U.lkI).then_inc(dve_own, c.step())
            V_.tensor_copy(U.nf, U.nfI).then_inc(dve_own, c.step())
            V_.tensor_copy(U.lkc[0:QT], U.lkc_i[0:QT]).then_inc(dve_own, c.step())
            V_.tensor_copy(U.nfc[0:QT], U.nfc_i[0:QT]).then_inc(dve_own, c.step())
            V_.tensor_copy(y[:, :, 0:4], aux[:, :, 0:4]).then_inc(dve_own, c.step())
            V_.tensor_copy(y[:, :, 4:6], aux[:, :, 1:3]).then_inc(dve_own, c.step())
            dve.wait_ge(dve_own, c.n)
            e3 = U.e3.rearrange("p (t i) -> p t i", i=3)
            tt(aux[:, :, 0:3], e3, e3, ALU.mult).then_inc(dve_own, c.step())
            dve.wait_ge(dve_own, c.n)
            V_.tensor_reduce(U.n2, aux[:, :, 0:3], AX, ALU.add).then_inc(dve_own, c.step())
            dve.wait_ge(dve_own, c.n)
            inverse_root(U.n2, 3.0, 0.0, U.j, U.one)
            tt(aux[:, :, 0:3], e3, bc(U.n2, 2, 3), ALU.mult).then_inc(dve_own, c.step())
            dve.wait_ge(dve_own, c.n)
            V_.tensor_copy(aux[:, :, 3:5], aux[:, :, 0:2]).then_inc(dve_own, c.step())
            dve.wait_ge(dve_own, c.n)
            V_.memset(U.one, 1.0).then_inc(dve_own, c.step())
            dve.wait_ge(dve_own, c.n)
            for j in range(SLOTS):
                V_.scalar_tensor_tensor(U.j, U.lk, U.node[:, j:j + 1], U.one, ALU.is_le, ALU.mult, accum_out=U.tiles[:, j:j + 1]).then_inc(dve_own, c.step())
                dve.wait_ge(dve_own, c.n)
            V_.tensor_copy(U.tile_i, U.tiles).then_inc(dve_own, c.step())
            dve.wait_ge(dve_own, c.n)
            dve.sem_inc(s.w_ready, 1)
            for j in range(SLOTS):
                dve.wait_ge(keys_got[j % 2], 16 * (j // 2 + 1))
                V_.scalar_tensor_tensor(U.j[:, 0:P], U.rowI[:, j % 2, :], U.node[:, j:j + 1], U.one[:, 0:P], ALU.is_le, ALU.mult,
                                               accum_out=U.in_tile[:, j:j + 1]).then_inc(dve_own, c.step())
                dve.wait_ge(dve_own, c.n)
                dve.sem_inc(s.got_free, 1)
            V_.scalar_tensor_tensor(U.end, U.tiles, float(P), U.in_tile, ALU.mult, ALU.add).then_inc(dve_own, c.step())
            dve.wait_ge(dve_own, c.n)
            dve.sem_inc(s.table_in, 1)
            V_.tensor_scalar(U.in_tile, U.end, -1.0, 0.0, ALU.add, ALU.max).then_inc(dve_own, c.step())
            dve.wait_ge(dve_own, c.n)
            V_.tensor_copy(last_i[:], U.in_tile).then_inc(dve_own, c.step())
            dve.wait_ge(dve_own, c.n)
            def second_keys(key, last, following, number):
                tt(key, last, following, ALU.is_equal).then_inc(dve_own, c.step())
                dve.wait_ge(dve_own, c.n)
                tt(U.j[0:last.shape[0], 0:last.shape[1]], last, number, ALU.subtract).then_inc(dve_own, c.step())
                dve.wait_ge(dve_own, c.n)
                tt(U.j[0:last.shape[0], 0:last.shape[1]], U.j[0:last.shape[0], 0:last.shape[1]], key, ALU.mult).then_inc(dve_own, c.step())
                dve.wait_ge(dve_own, c.n)
                return U.j[0:last.shape[0], 0:last.shape[1]]
            t_ = second_keys(U.one, U.lk, U.nf, U.t)
            tt(U.lk, t_, U.t, ALU.add).then_inc(dve_own, c.step())
            dve.wait_ge(dve_own, c.n)
            t_ = second_keys(U.cc[0:QT], U.lkc[0:QT], U.nfc[0:QT], U.tc[0:QT])
            tt(U.kc[0:QT], t_, U.tc[0:QT], ALU.add).then_inc(dve_own, c.step())
            dve.wait_ge(dve_own, c.n)
            for k in range(QK):
                V_.tensor_scalar(sel2[:, k, :], U.lk[0:QT, k * QT:(k + 1) * QT], U.kc[0:QT, k:k + 1], None, ALU.is_equal).then_inc(dve_own, c.step())
                dve.wait_ge(dve_own, c.n)
                V_.scalar_tensor_tensor(U.j[0:QT, 0:QT], U.lk[0:QT, k * QT:(k + 1) * QT], U.kc[0:QT, k:k + 1], lower[0:QT, 0:QT],
                                               ALU.is_equal, ALU.mult, accum_out=U.nfc[0:QT, k:k + 1]).then_inc(dve_own, c.step())
                dve.wait_ge(dve_own, c.n)
            V_.tensor_scalar(U.nfc[0:QT], U.nfc[0:QT], 1.0, None, ALU.is_lt).then_inc(dve_own, c.step())
            dve.wait_ge(dve_own, c.n)
            tt(U.cc[0:QT], U.cc[0:QT], U.nfc[0:QT], ALU.mult).then_inc(dve_own, c.step())
            dve.wait_ge(dve_own, c.n)
            tt(U.lkc[0:QT], U.lkc[0:QT], spare[0:QT, 0:1].broadcast_to([QT, QK]), ALU.subtract).then_inc(dve_own, c.step())
            dve.wait_ge(dve_own, c.n)
            tt(U.lkc[0:QT], U.lkc[0:QT], U.cc[0:QT], ALU.mult).then_inc(dve_own, c.step())
            dve.wait_ge(dve_own, c.n)
            tt(U.lkc[0:QT], U.lkc[0:QT], spare[0:QT, 0:1].broadcast_to([QT, QK]), ALU.add).then_inc(dve_own, c.step())
            dve.wait_ge(dve_own, c.n)
            V_.tensor_copy(put2_i[:], U.lkc[0:QT]).then_inc(dve_own, c.step())
            dve.wait_ge(dve_own, c.n)
            dve.wait_ge(moved, 48)
            tt(U.in_tile, U.end, U.prev, ALU.subtract).then_inc(dve_own, c.step())
            dve.wait_ge(dve_own, c.n)
            V_.tensor_scalar(has[:], U.in_tile, 1.0, None, ALU.min).then_inc(dve_own, c.step())
            dve.wait_ge(dve_own, c.n)
            V_.tensor_scalar(rcnt[:], U.in_tile, 1.0, None, ALU.max).then_inc(dve_own, c.step())
            dve.wait_ge(dve_own, c.n)
            V_.reciprocal(rcnt[:], rcnt[:]).then_inc(dve_own, c.step())
            dve.wait_ge(dve_own, c.n)
            dve.wait_ge(s.hid_free, 1)
            dve.sem_inc(s.hid_free, -1)

            def scale(name, by, c0=0, c1=None):
                w = wt[name]
                V_.tensor_scalar(w[:, c0:c1 or w.shape[1]], w[:, c0:c1 or w.shape[1]], by, None, ALU.mult).then_inc(dve_own, c.step())
                dve.wait_ge(dve_own, c.n)
            r3, r2 = 3 ** -0.5, 2 ** -0.5
            scale("fc2_0", r3, 160, 192)
            scale("fc2_0", r2, 192, 224)
            for l in (1, 2):
                scale(f"fc2_{l}", 0.125)
                scale(f"fc2_{l}", r3, 160, 192)
                for w in ("f_s", "k_s"):
                    scale(f"{w}{l}", 0.125)
                for w in ("f_v", "k_v"):
                    scale(f"{w}{l}", 32 ** -0.5)
                down = 96 ** -0.5 * (10 ** -0.5 if l == 1 else 1.0)
                for w in ("out_s", "out_v"):
                    scale(f"{w}{l}", down)
                scale(f"out_a{l}", down * (0.1 if l == 1 else 1.0))
            scale("rbf", r3, 160, 192)
            scale("rbf", r2, 192, 224)
            for at, rows, col, by in ((64, 32, 0, r3), (96, 32, 1, r2), (32, 32, 2, r2), (96, 32, 2, r2)):
                V_.tensor_scalar(w2[at:at + rows, col:col + 1], w2[at:at + rows, col:col + 1], by, None, ALU.mult).then_inc(dve_own, c.step())
                dve.wait_ge(dve_own, c.n)
            V_.tensor_scalar(wt["lin_s"][:], wt["lin_s"][:], w2[0:96, 0:1], None, ALU.mult).then_inc(dve_own, c.step())
            dve.wait_ge(dve_own, c.n)
            V_.tensor_scalar(wt["lin_x"][:], wt["lin_x"][:], w2[:, 1:2], None, ALU.mult).then_inc(dve_own, c.step())
            dve.wait_ge(dve_own, c.n)
            V_.tensor_scalar(wt["lin_yz"][:], wt["lin_yz"][:], w2[:, 2:3], None, ALU.mult).then_inc(dve_own, c.step())
            dve.wait_ge(dve_own, c.n)
            dve.wait_ge(dve_own, c.n)
            dve.sem_inc(dve_own, c.reset())
            barrier(dve, "dve")

            big = Nv.big.rearrange("p (j c) -> p j c", c=DIM)

            def mean_var(src, width, mean, rstd, eps, scratch):
                V_.tensor_reduce(stats[:, mean, :], src, AX, ALU.add).then_inc(dve_own, c.step())
                dve.wait_ge(dve_own, c.n)
                V_.tensor_scalar(stats[:, mean, :], stats[:, mean, :], 1.0 / width, None, ALU.mult).then_inc(dve_own, c.step())
                dve.wait_ge(dve_own, c.n)
                tt(scratch, src, bc(stats[:, mean, :], 2, width), ALU.subtract).then_inc(dve_own, c.step())
                dve.wait_ge(dve_own, c.n)
                tt(scratch, scratch, scratch, ALU.mult).then_inc(dve_own, c.step())
                dve.wait_ge(dve_own, c.n)
                V_.tensor_reduce(stats[:, rstd, :], scratch, AX, ALU.add).then_inc(dve_own, c.step())
                dve.wait_ge(dve_own, c.n)
                inverse_root(stats[:, rstd, :], width, eps, stats[:, 8, :], stats[:, 9, :])

            def prep(l):
                mean_var(x[:], DIM, 1, 0, 1e-5, big)
                tt(stats[:, 1, :], stats[:, 1, :], stats[:, 0, :], ALU.mult).then_inc(dve_own, c.step())
                dve.wait_ge(dve_own, c.n)
                V_.tensor_scalar(stats[:, 1, :], stats[:, 1, :], -1.0, None, ALU.mult).then_inc(dve_own, c.step())
                dve.wait_ge(dve_own, c.n)
                if l == 3:
                    tt(big, x[:], bc(stats[:, 0, :], 2, DIM), ALU.mult).then_inc(dve_own, c.step())
                    dve.wait_ge(dve_own, c.n)
                    tt(big, big, bc(stats[:, 1, :], 2, DIM), ALU.add).then_inc(dve_own, c.step())
                    dve.wait_ge(dve_own, c.n)
                    V_.tensor_scalar(big, big, 0.0, None, ALU.max).then_inc(dve_own, c.step())
                    dve.wait_ge(dve_own, c.n)
                    tt(x[:], x[:], big, ALU.add).then_inc(dve_own, c.step())
                    dve.wait_ge(dve_own, c.n)
                    normed = fore[:, 0:SLOTS * DIM].rearrange("p (j c) -> p j c", c=DIM)
                    hs = big[:, :, 0:S]
                    mean_var(hs, S, 3, 2, 1e-5, normed[:, :, 0:S])
                    tt(normed[:, :, 0:S], hs, bc(stats[:, 3, :], 2, S), ALU.subtract).then_inc(dve_own, c.step())
                    dve.wait_ge(dve_own, c.n)
                    tt(normed[:, :, 0:S], normed[:, :, 0:S], bc(stats[:, 2, :], 2, S), ALU.mult).then_inc(dve_own, c.step())
                    dve.wait_ge(dve_own, c.n)
                    hv = big[:, :, S:DIM]
                    nv = normed[:, :, S:DIM]
                    tt(nv, hv, hv, ALU.mult).then_inc(dve_own, c.step())
                    dve.wait_ge(dve_own, c.n)
                    V_.tensor_reduce(stats[:, 4, :], nv, AX, ALU.add).then_inc(dve_own, c.step())
                    dve.wait_ge(dve_own, c.n)
                    inverse_root(stats[:, 4, :], V, 1e-5, stats[:, 8, :], stats[:, 9, :])
                    for i in range(3):
                        tt(nv[:, :, V * i:V * (i + 1)], hv[:, :, i:3 * V:3], bc(stats[:, 4, :], 2, V), ALU.mult).then_inc(dve_own, c.step())
                        dve.wait_ge(dve_own, c.n)
                dve.wait_ge(dve_own, c.n)
                dve.sem_inc(dve_own, c.reset())
                dve.sem_inc(s.node_in, SLOTS)
                width = SPEC[l]["table"]
                ks = SPEC[l]["skip"]
                def stage(j, b, first, half):
                    dve.wait_ge(s.node_mm, 1)
                    dve.sem_inc(s.node_mm, -1)
                    o = bank[:, 2 + b, :]
                    t0 = fore[:, bass.ds(j * width, 160)]
                    k0 = skip[:, bass.ds(j, 1), 0:ks].rearrange("p o c -> p (o c)")
                    if l in (1, 2):
                        V_.tensor_scalar(t0, o[:, 0:160], attr[:, bass.ds(j, 1)], None, ALU.mult).then_inc(dve_own, c.step())
                        V_.tensor_scalar(k0, o[:, 160:160 + ks], attr[:, bass.ds(j, 1)], None, ALU.mult).then_inc(dve_own, c.step())
                    else:
                        V_.tensor_copy(t0, o[:, 0:160]).then_inc(dve_own, c.step())
                        V_.tensor_copy(k0, o[:, 160:160 + ks]).then_inc(dve_own, c.step())
                    if l == 0:
                        V_.tensor_copy(fore[:, bass.ds(j * width + 160, 64)], o[:, 64:128]).then_inc(dve_own, c.step())
                    dve.wait_ge(dve_own, c.n)
                    dve.sem_inc(dve_own, c.reset())
                    dve.sem_inc(s.node_free, 1)
                pipelined(dve, SLOTS, [(0, stage)])
                dve.sem_inc(s.table_in, 1)

            def select(g, b, keys, sel, scalar):
                for t in range(GROUP):
                    V_.tensor_scalar(sel[:, b, t, :], keys[:, b, t * P:(t + 1) * P],
                                       scalar[:, bass.ds(g * GROUP + t, 1)], None, ALU.is_equal).then_inc(dve_own, c.step())

            def edges(l):
                def stage(g, part, first, half):
                    f = SPEC[l]["f"]
                    b = part % 2
                    if l == 0:
                        dve.wait_ge(s.w_ready, 1)
                        dve.sem_inc(s.w_ready, -1)
                        dve.sem_inc(s.hid_free, 1)
                    dve.wait_ge(s.key_in0 if b == 0 else s.key_in1, 16)
                    dve.sem_inc(s.key_in0 if b == 0 else s.key_in1, -16)
                    if not first:
                        dve.wait_ge(s.msg_free, 1)
                        dve.sem_inc(s.msg_free, -1)
                    select(g, b, E.keys, E.sel, src_f if l == 0 else dst_f)
                    if l == 0:
                        for t in range(GROUP):
                            V_.scalar_tensor_tensor(E.first[:, t, :], E.keys[:, b, t * P:(t + 1) * P], src_f[:, bass.ds(g * GROUP + t, 1)],
                                                    lower[:], ALU.is_equal, ALU.mult, accum_out=E.cnt[:, t:t + 1]).then_inc(dve_own, c.step())
                    dve.wait_ge(got[l][part], (half + 1) * (16 * GROUP))
                    if l:
                        dve.wait_ge(s.wy_ready, 1)
                        dve.sem_inc(s.wy_ready, -1)
                    w = E.w[:, b] if l else wmm(b)
                    width = SPEC[l]["table"]
                    rows = E.got[:, part, 0:GROUP * width].rearrange("p (t c) -> p t c", c=width)
                    xs = rows[:, :, 0:S]
                    msg = E.msg[:, b, 0:GROUP * f].rearrange("p (t c) -> p t c", c=f)
                    vec = SPEC[l]["vec"]
                    blocks = msg[:, :, 96:96 + 3 * vec].rearrange("p t (i c) -> p t i c", c=vec)
                    t0 = E.t0[:, 0:GROUP * S].rearrange("p (t c) -> p t c", c=S)
                    t1 = E.t1.rearrange("p (t i c) -> p t i c", i=3, c=V)
                    t2 = E.t2.rearrange("p (t i c) -> p t i c", i=3, c=V)

                    def wv(c0):
                        return bc(w[:, :, c0:c0 + V], 2, 3)
                    if l == 0:
                        xv = rows[:, :, S:224].rearrange("p t (i c) -> p t i c", c=V)
                        sh = aux[:, bass.ds(g * GROUP, GROUP), :]
                        keys4 = src_f[:, bass.ds(g * GROUP, GROUP)]
                        u1, u2 = E.u1, E.u2
                        counted = c.n
                        tt(t0, w[:, :, 64:128], xs, ALU.mult).then_inc(dve_own, c.step())
                        tt(t1, xv[:, :, 0:3, :], bc(sh[:, :, 0:3], 3, V), ALU.mult).then_inc(dve_own, c.step())
                        tt(u1, xv[:, :, 1:4, :], bc(sh[:, :, 2:5], 3, V), ALU.mult).then_inc(dve_own, c.step())
                        tt(u2, xv[:, :, 2:5, :], bc(sh[:, :, 1:4], 3, V), ALU.mult).then_inc(dve_own, c.step())
                        dve.wait_ge(dve_own, counted + 1)
                        V_.tensor_scalar(E.cnt, E.cnt, 1.0, None, ALU.is_lt).then_inc(dve_own, c.step())
                        tt(blocks[:, :, :, 0:S], bc(t0, 2, 3), bc(sh[:, :, 0:3], 3, S), ALU.mult).then_inc(dve_own, c.step())
                        dve.wait_ge(dve_own, counted + 5)
                        V_.scalar_tensor_tensor(E.pos, keys4, spare[:], E.cnt, ALU.subtract, ALU.mult).then_inc(dve_own, c.step())
                        tt(t2[:, :, 0, :], t1[:, :, 0, :], t1[:, :, 1, :], ALU.add).then_inc(dve_own, c.step())
                        tt(u1, u1, u2, ALU.subtract).then_inc(dve_own, c.step())
                        dve.wait_ge(dve_own, counted + 7)
                        V_.tensor_scalar(put_i[:, bass.ds(g * GROUP, GROUP)], E.pos, spare[:], None, ALU.add).then_inc(dve_own, c.step())
                        dve.wait_ge(dve_own, counted + 8)
                        tt(t2[:, :, 0, :], t2[:, :, 0, :], t1[:, :, 2, :], ALU.add).then_inc(dve_own, c.step())
                        tt(msg[:, :, 0:S], w[:, :, 0:64], xs, ALU.mult).then_inc(dve_own, c.step())
                        dve.wait_ge(dve_own, counted + 9)
                        tt(blocks[:, :, :, 96:128], u1, wv(192), ALU.mult).then_inc(dve_own, c.step())
                        dve.wait_ge(dve_own, counted + 11)
                        tt(msg[:, :, S:96], t2[:, :, 0, :], w[:, :, 160:192], ALU.mult).then_inc(dve_own, c.step())
                        tt(blocks[:, :, :, S:96], wv(128), xv[:, :, 0:3, :], ALU.mult).then_inc(dve_own, c.step())
                    else:
                        yy = y[:, bass.ds(g * GROUP, GROUP), :]
                        xv = rows[:, :, S:DIM].rearrange("p t (i c) -> p t i c", c=V)
                        wb = t0
                        tt(t1, xv, bc(yy[:, :, 1:4], 3, V), ALU.mult).then_inc(dve_own, c.step())
                        parts = c.n
                        tt(wb, w[:, :, 96:160], xs, ALU.mult).then_inc(dve_own, c.step())
                        dve.wait_ge(dve_own, parts)
                        tt(t2[:, :, 0, :], t1[:, :, 0, :], t1[:, :, 1, :], ALU.add).then_inc(dve_own, c.step())
                        dve.wait_ge(dve_own, parts + 1)
                        tt(blocks[:, :, :, 0:S], bc(wb, 2, 3), bc(yy[:, :, 1:4], 3, S), ALU.mult).then_inc(dve_own, c.step())
                        dve.wait_ge(dve_own, parts + 2)
                        tt(t2[:, :, 0, :], t2[:, :, 0, :], t1[:, :, 2, :], ALU.add).then_inc(dve_own, c.step())
                        dot = c.n
                        tt(msg[:, :, 0:S], w[:, :, 0:S], xs, ALU.mult).then_inc(dve_own, c.step())
                        tt(blocks[:, :, :, S:96], bc(w[:, :, S:96], 2, 3), xv, ALU.mult).then_inc(dve_own, c.step())
                        dve.wait_ge(dve_own, dot)
                        tt(msg[:, :, S:96], t2[:, :, 0, :], w[:, :, 160:192], ALU.mult).then_inc(dve_own, c.step())
                    dve.wait_ge(dve_own, c.n)
                    dve.sem_inc(dve_own, c.reset())
                    dve.sem_inc(s.msg_ready, 1)
                    dve.sem_inc(s.w_free, 1)
                    dve.sem_inc(s.got_free, 1)
                    dve.sem_inc(s.key_free, 1)
                pipelined(dve, GROUPS, [(0, stage)], unroll=DEPTH)
                dve.wait_ge(s.msg_free, 2)
                dve.sem_inc(s.msg_free, -2)

            def post(l):
                f = SPEC[l]["f"]
                out_w = {0: 192, 1: 161, 2: 161, 3: 160}[l]
                conv = fore[:, 0:SLOTS * out_w].rearrange("p (j c) -> p j c", c=out_w)

                def sums(j, b, first, half):
                    dve.wait_ge(s.carry_in0 if b == 0 else s.carry_in1, 16 * (1 if l else CHAINS))
                    dve.sem_inc(s.carry_in0 if b == 0 else s.carry_in1, -(16 * (1 if l else CHAINS)))
                    car = Nv.car[:, b, :]
                    o = Nv.sum[:, b, 0:f]
                    if l:
                        dve.wait_ge(rows_got[l][b], (half + 1) * 16)
                        V_.scalar_tensor_tensor(o, Nv.row[:, b, 0:f], has[:, bass.ds(j, 1)], car[:, 0:f], ALU.mult, ALU.add).then_inc(dve_own, c.step())
                        dve.wait_ge(dve_own, c.n)
                    else:
                        tt(o, car[:, 0:f], car[:, f:2 * f], ALU.add).then_inc(dve_own, c.step())
                        tt(car[:, 2 * f:3 * f], car[:, 2 * f:3 * f], car[:, 3 * f:4 * f], ALU.add).then_inc(dve_own, c.step())
                        dve.wait_ge(dve_own, c.n)
                        tt(o, o, car[:, 2 * f:3 * f], ALU.add).then_inc(dve_own, c.step())
                        dve.wait_ge(dve_own, c.n)
                    if l == 3:
                        V_.tensor_scalar(Nv.rden[:, 0:4], o[:, 160:164], 1e-16, None, ALU.add).then_inc(dve_own, c.step())
                        dve.wait_ge(dve_own, c.n)
                        V_.reciprocal(Nv.rden[:, 0:4], Nv.rden[:, 0:4]).then_inc(dve_own, c.step())
                        dve.wait_ge(dve_own, c.n)
                        hs = o[:, 0:64].rearrange("p (h c) -> p h c", h=4)
                        hv = o[:, 64:160].rearrange("p (i h c) -> p i h c", i=3, h=4)
                        tt(hs, hs, bc(Nv.rden[:, 0:4], 2, 16), ALU.mult).then_inc(dve_own, c.step())
                        tt(hv, hv, bc(bc(Nv.rden[:, 0:4], 1, 3), 3, 8), ALU.mult).then_inc(dve_own, c.step())
                    dve.wait_ge(dve_own, c.n)
                    dve.sem_inc(dve_own, c.reset())
                    dve.sem_inc(s.sum_ready, 1)
                    dve.sem_inc(s.sum_free, 1)
                    if l:
                        dve.sem_inc(s.got_free, 1)

                def products(j, b, first, half):
                    dve.wait_ge(s.node_mm, 1)
                    dve.sem_inc(s.node_mm, -1)
                    o = bank[:, 2 + b, 0:out_w]
                    to = fore[:, bass.ds(j * out_w, out_w)]
                    if l == 1:
                        V_.tensor_scalar(to, o, attr[:, bass.ds(j, 1)], None, ALU.mult).then_inc(dve_own, c.step())
                    elif l == 2:
                        V_.tensor_scalar(to, o, attr[:, bass.ds(j, 1)], rcnt[:, bass.ds(j, 1)], ALU.mult, ALU.mult).then_inc(dve_own, c.step())
                    else:
                        V_.tensor_copy(to, o).then_inc(dve_own, c.step())
                    dve.wait_ge(dve_own, c.n)
                    dve.sem_inc(dve_own, c.reset())
                    dve.sem_inc(s.node_free, 1)
                pipelined(dve, SLOTS, [(2, products), (0, sums)])

                def add_to_x(res):
                    tt(x[:, :, 0:S], x[:, :, 0:S], res[:, :, 0:S], ALU.add).then_inc(dve_own, c.step())
                    for i in range(3):
                        tt(x[:, :, S + i:DIM:3], x[:, :, S + i:DIM:3], res[:, :, S + V * i:S + V * (i + 1)], ALU.add).then_inc(dve_own, c.step())
                    dve.wait_ge(dve_own, c.n)
                if l == 0:
                    V_.scalar_tensor_tensor(conv, conv, 1.0 / 32.0, skip[:], ALU.mult, ALU.add).then_inc(dve_own, c.step())
                    dve.wait_ge(dve_own, c.n)
                    dve.wait_ge(dve_own, c.n)
                    dve.sem_inc(dve_own, c.reset())
                    dve.sem_inc(s.vt_ready, 1)
                    dve.wait_ge(s.gate_ready, 1)
                    dve.sem_inc(s.gate_ready, -1)
                    tt(big[:, :, 0:S], conv[:, :, 0:S], skip[:, :, 0:S], ALU.mult).then_inc(dve_own, c.step())
                    for i in range(3):
                        tt(big[:, :, S + V * i:S + V * (i + 1)], conv[:, :, 96 + V * i:128 + V * i], skip[:, :, S:96], ALU.mult).then_inc(dve_own, c.step())
                    dve.wait_ge(dve_own, c.n)
                    add_to_x(big)
                elif l == 1:
                    turns = Nv.small
                    V_.tensor_scalar(turns[:, 0, :], conv[:, :, 160], 1.0 / (2 * math.pi), None, ALU.mult).then_inc(dve_own, c.step())
                    dve.wait_ge(dve_own, c.n)
                    V_.tensor_copy(Nv.smi, turns[:, 0, :]).then_inc(dve_own, c.step())
                    dve.wait_ge(dve_own, c.n)
                    V_.tensor_copy(turns[:, 1, :], Nv.smi).then_inc(dve_own, c.step())
                    dve.wait_ge(dve_own, c.n)
                    tt(turns[:, 2, :], turns[:, 0, :], turns[:, 1, :], ALU.subtract).then_inc(dve_own, c.step())
                    dve.wait_ge(dve_own, c.n)
                    V_.tensor_scalar(turns[:, 3, :], turns[:, 2, :], 0.25, None, ALU.add).then_inc(dve_own, c.step())
                    dve.wait_ge(dve_own, c.n)
                    for _ in range(2):
                        V_.tensor_scalar(turns[:, 6:8, :], turns[:, 2:4, :], 0.5, None, ALU.is_gt).then_inc(dve_own, c.step())
                        dve.wait_ge(dve_own, c.n)
                        tt(turns[:, 2:4, :], turns[:, 2:4, :], turns[:, 6:8, :], ALU.subtract).then_inc(dve_own, c.step())
                        dve.wait_ge(dve_own, c.n)
                        V_.tensor_scalar(turns[:, 6:8, :], turns[:, 2:4, :], -0.5, None, ALU.is_lt).then_inc(dve_own, c.step())
                        dve.wait_ge(dve_own, c.n)
                        tt(turns[:, 2:4, :], turns[:, 2:4, :], turns[:, 6:8, :], ALU.add).then_inc(dve_own, c.step())
                        dve.wait_ge(dve_own, c.n)
                    dve.wait_ge(dve_own, c.n)
                    dve.sem_inc(dve_own, c.reset())
                    dve.sem_inc(s.vt_ready, 1)
                    dve.wait_ge(s.gate_ready, 1)
                    dve.sem_inc(s.gate_ready, -1)
                    tt(big, skip[:, :, 0:DIM], bc(turns[:, 5, :], 2, DIM), ALU.mult).then_inc(dve_own, c.step())
                    tt(conv[:, :, 0:DIM], conv[:, :, 0:DIM], bc(turns[:, 4, :], 2, DIM), ALU.mult).then_inc(dve_own, c.step())
                    dve.wait_ge(dve_own, c.n)
                    tt(big, big, conv[:, :, 0:DIM], ALU.add).then_inc(dve_own, c.step())
                    dve.wait_ge(dve_own, c.n)
                    add_to_x(big)
                elif l == 2:
                    tt(big, conv[:, :, 0:DIM], conv[:, :, 160:161].broadcast_to([P, SLOTS, DIM]), ALU.mult).then_inc(dve_own, c.step())
                    dve.wait_ge(dve_own, c.n)
                    tt(big, big, skip[:, :, 0:DIM], ALU.add).then_inc(dve_own, c.step())
                    dve.wait_ge(dve_own, c.n)
                    add_to_x(big)
                else:
                    add_to_x(conv)
                dve.wait_ge(dve_own, c.n)
                dve.sem_inc(dve_own, c.reset())

            for l in (0, 1, 2):
                if l not in layers:
                    continue
                prep(l)
                barrier(dve, "dve")
                edges(l)
                barrier(dve, "dve")
                post(l)
                barrier(dve, "dve")

            if 3 in layers:
                prep(3)
                barrier(dve, "dve")

                def planes(ap):
                    return ap.rearrange("p t (i c) -> p t i c", i=3)

                q, u1, u2 = planes(T.q), planes(T.u1), planes(T.u2)

                def cross_parts(v, ys):
                    tt(u1[:, :, 0:2, :], v[:, :, 1:3, :], bc(ys[:, :, 2:4], 3, V), ALU.mult).then_inc(dve_own, c.step())
                    tt(u1[:, :, 2:3, :], v[:, :, 0:1, :], bc(ys[:, :, 4:5], 3, V), ALU.mult).then_inc(dve_own, c.step())
                    tt(u2[:, :, 0:1, :], v[:, :, 2:3, :], bc(ys[:, :, 1:2], 3, V), ALU.mult).then_inc(dve_own, c.step())
                    tt(u2[:, :, 1:3, :], v[:, :, 0:2, :], bc(ys[:, :, 2:4], 3, V), ALU.mult).then_inc(dve_own, c.step())
                    dve.wait_ge(dve_own, c.n - 1)

                def m1(g, part, first, half):
                    b = part % 2
                    ys = y[:, bass.ds(g * 2, 2), 1:6]
                    m, d = T.m[:, b], T.dot
                    w = T.w[:, b]
                    f = T.f[:, b]
                    vsl = f[:, :, 160:352].rearrange("p t (i c) -> p t i c", c=64)
                    mv = planes(m[:, :, S:DIM])
                    dve.wait_ge(s.m_ready, 1)
                    dve.sem_inc(s.m_ready, -1)
                    dve.wait_ge(s.wy_ready, 1)
                    dve.sem_inc(s.wy_ready, -1)
                    tt(q, mv, bc(ys[:, :, 0:3], 3, V), ALU.mult).then_inc(dve_own, c.step())
                    cross_parts(mv, ys)
                    tt(d, q[:, :, 0, :], q[:, :, 1, :], ALU.add).then_inc(dve_own, c.step())
                    half_dot = c.n
                    tt(f[:, :, 0:64], m[:, :, 0:S], w[:, :, 0:64], ALU.mult).then_inc(dve_own, c.step())
                    dve.wait_ge(dve_own, half_dot)
                    tt(d, d, q[:, :, 2, :], ALU.add).then_inc(dve_own, c.step())
                    tt(u1, u1, u2, ALU.subtract).then_inc(dve_own, c.step())
                    crossed = c.n
                    tt(f[:, :, 96:160], m[:, :, 0:S], w[:, :, 96:160], ALU.mult).then_inc(dve_own, c.step())
                    tt(vsl[:, :, :, 0:V], mv, bc(w[:, :, 64:96], 2, 3), ALU.mult).then_inc(dve_own, c.step())
                    dve.wait_ge(dve_own, crossed)
                    tt(f[:, :, 64:96], d, w[:, :, 160:192], ALU.mult).then_inc(dve_own, c.step())
                    tt(vsl[:, :, :, V:64], u1, bc(w[:, :, 192:224], 2, 3), ALU.mult).then_inc(dve_own, c.step())
                    dve.wait_ge(dve_own, c.n)
                    dve.sem_inc(dve_own, c.reset())
                    dve.sem_inc(s.f_ready, 1)
                    dve.sem_inc(s.got_free, 1)

                def m2(g, part, first, half):
                    b = part % 2
                    dve.wait_ge(s.gate_ready, 1)
                    dve.sem_inc(s.gate_ready, -1)
                    yy = y[:, bass.ds(g * 2, 2), :]
                    ys = yy[:, :, 1:6]
                    f, cv = T.f2[:, b], T.cv[:, b]
                    vsl = f[:, :, 160:352].rearrange("p t (i c) -> p t i c", c=64)
                    tt(vv, bc(cv[:, :, 64:96], 2, 3), bc(ys[:, :, 0:3], 3, V), ALU.mult).then_inc(dve_own, c.step())
                    V_.scalar_tensor_tensor(T.al2, cv[:, :, 0:64], 0.2, cv[:, :, 0:64], ALU.mult, ALU.max).then_inc(dve_own, c.step())
                    dve.wait_ge(dve_own, c.n - 1)
                    tt(vv, vv, planes(cv[:, :, 96:192]), ALU.add).then_inc(dve_own, c.step())
                    dve.wait_ge(dve_own, c.n - 1)
                    tt(T.al2, T.al2, bc(alpha_dot[:], 1, 2), ALU.mult).then_inc(dve_own, c.step())
                    dve.wait_ge(dve_own, c.n - 1)
                    tt(vv, vv, bc(f[:, :, 64:96], 2, 3), ALU.mult).then_inc(dve_own, c.step())
                    dve.wait_ge(dve_own, c.n - 1)
                    V_.tensor_reduce(aux[:, bass.ds(g * 2, 2), 0:4], T.al2.rearrange("p t (h c) -> p t h c", h=4), AX,
                                     ALU.add).then_inc(dve_own, c.step())
                    dve.wait_ge(dve_own, c.n - 1)
                    tt(q, vv, bc(ys[:, :, 0:3], 3, V), ALU.mult).then_inc(dve_own, c.step())
                    cross_parts(vv, ys)
                    tt(f[:, :, 64:96], q[:, :, 0, :], q[:, :, 1, :], ALU.add).then_inc(dve_own, c.step())
                    tt(vsl[:, :, :, 0:V], vv, y0_planes(yy), ALU.mult).then_inc(dve_own, c.step())
                    dve.wait_ge(dve_own, c.n - 1)
                    tt(f[:, :, 64:96], f[:, :, 64:96], q[:, :, 2, :], ALU.add).then_inc(dve_own, c.step())
                    tt(vsl[:, :, :, V:64], u1, u2, ALU.subtract).then_inc(dve_own, c.step())
                    dve.wait_ge(dve_own, c.n)
                    dve.sem_inc(dve_own, c.reset())
                    dve.sem_inc(s.f2_ready, 1)

                vv = T.vv

                def y0_planes(yy):
                    return bc(yy[:, :, 0:1].broadcast_to([P, 2, 3]), 3, V)

                def edge_out(g, part, first, half):
                    b = part % 2
                    dve.wait_ge(s.hs_ready, 1)
                    dve.sem_inc(s.hs_ready, -1)
                    ys = y[:, bass.ds(g * 2, 2), 1:4]
                    c2 = bank[:, 3, 0:384].rearrange("p (t c) -> p t c", t=2)
                    hv = planes(T.h[:, b, :, S:DIM])
                    tt(q, bc(c2[:, :, 64:96], 2, 3), bc(ys, 3, V), ALU.mult).then_inc(dve_own, c.step())
                    dve.wait_ge(dve_own, c.n)
                    tt(hv, q, c2[:, :, 96:192].rearrange("p t (i c) -> p t i c", i=3), ALU.add).then_inc(dve_own, c.step())
                    dve.wait_ge(dve_own, c.n)
                    dve.sem_inc(dve_own, c.reset())
                    dve.sem_inc(s.c2_free, 1)
                    dve.sem_inc(s.h_ready, 1)
                pipelined(dve, TILES // 2, [(-1, m1), (2, edge_out), (0, m2)], unroll=DEPTH)
                barrier(dve, "dve")

                dve.wait_ge(s.key_in0, 48)
                dve.sem_inc(s.key_in0, -48)
                V_.tensor_copy(C.k[0:QT], C.kI[0:QT]).then_inc(dve_own, c.step())
                V_.tensor_copy(C.lk, C.lkI).then_inc(dve_own, c.step())
                V_.tensor_copy(C.fk, C.fkI).then_inc(dve_own, c.step())
                dve.wait_ge(dve_own, c.n)

                def same(o, p_, q_):
                    tt(o, p_, q_, ALU.is_equal).then_inc(dve_own, c.step())
                    dve.wait_ge(dve_own, c.n)
                    V_.tensor_scalar(o, o, -1.0, BIG, ALU.add, ALU.mult).then_inc(dve_own, c.step())
                    dve.wait_ge(dve_own, c.n)

                V_.memset(C.b, -BIG).then_inc(dve_own, c.step())
                dve.wait_ge(dve_own, c.n)
                V_.memset(C.b2, -BIG).then_inc(dve_own, c.step())
                dve.wait_ge(dve_own, c.n)
                for k in range(QK):
                    kk = C.k[0:QT, k, :]
                    same(C.b[0:QT, 1:P], kk[:, 1:P], kk[:, 0:P - 1])
                    V_.tensor_copy(C.b2[0:QT, 0:P - 1], C.b[0:QT, 1:P]).then_inc(dve_own, c.step())
                    dve.wait_ge(dve_own, c.n)
                    dve.wait_ge(s.scan_sb, 1)
                    dve.sem_inc(s.scan_sb, -1)
                    dve.sem_inc(s.scan_free, 1)
                    for h in range(4):
                        fw, bw, at = C.fw[0:QT, k, h, :], C.bw[0:QT, h, :], C.aT[0:QT, k, h, :]
                        V_.tensor_tensor_scan(fw, C.b[0:QT], at, 0.0, ALU.add, ALU.max).then_inc(dve_own, c.step())
                        V_.tensor_tensor_scan(bw[:, ::-1], C.b2[0:QT, ::-1], at[:, ::-1], 0.0, ALU.add, ALU.max).then_inc(dve_own, c.step())
                    dve.wait_ge(dve_own, c.n)
                    V_.tensor_copy(C.edge[0:QT, k, :, 0], C.fw[0:QT, k, :, P - 1]).then_inc(dve_own, c.step())
                    V_.tensor_copy(C.edge[0:QT, k, :, 1], C.bw[0:QT, :, 0]).then_inc(dve_own, c.step())
                    dve.wait_ge(dve_own, c.n)
                    tt(C.fw[0:QT, k], C.fw[0:QT, k], C.bw[0:QT], ALU.max).then_inc(dve_own, c.step())
                    dve.wait_ge(dve_own, c.n)
                dve.sem_inc(s.scan_mm, 1)
                dve.wait_ge(s.vt_mm, 1)
                dve.sem_inc(s.vt_mm, -1)
                for e in range(2):
                    V_.tensor_copy(C.m[0:4, e, 0:4 * QT], bank[0:4, 2 + 2 * e, 0:4 * QT]).then_inc(dve_own, c.step())
                    V_.tensor_copy(C.m[0:4, e, 4 * QT:TILES], bank[0:4, 3 + 2 * e, 0:3 * QT]).then_inc(dve_own, c.step())
                V_.memset(C.j[0:4], -BIG).then_inc(dve_own, c.step())
                dve.wait_ge(dve_own, c.n)
                V_.memset(C.c[0:4], -BIG).then_inc(dve_own, c.step())
                dve.wait_ge(dve_own, c.n)
                lk, fk = C.lk[0:4], C.fk[0:4]
                same(C.j[0:4, 0, 1:TILES], lk[:, 1:TILES], lk[:, 0:TILES - 1])
                same(C.j[0:4, 1, 0:TILES - 1], fk[:, 1:TILES], fk[:, 0:TILES - 1])
                V_.tensor_tensor_scan(C.c[0:4, 0, :], C.j[0:4, 0, :], C.m[0:4, 0, :], 0.0, ALU.add, ALU.max).then_inc(dve_own, c.step())
                dve.wait_ge(dve_own, c.n)
                V_.tensor_tensor_scan(C.c[0:4, 1, ::-1], C.j[0:4, 1, ::-1], C.m[0:4, 1, ::-1], 0.0, ALU.add, ALU.max).then_inc(dve_own, c.step())
                dve.wait_ge(dve_own, c.n)
                same(C.j[0:4, 0, 1:TILES], fk[:, 1:TILES], lk[:, 0:TILES - 1])
                V_.tensor_copy(C.m[0:4, 0, 1:TILES], C.c[0:4, 0, 0:TILES - 1]).then_inc(dve_own, c.step())
                dve.wait_ge(dve_own, c.n)
                V_.tensor_copy(C.m[0:4, 1, 0:TILES - 1], C.c[0:4, 1, 1:TILES]).then_inc(dve_own, c.step())
                dve.wait_ge(dve_own, c.n)
                V_.memset(C.c[0:4], -BIG).then_inc(dve_own, c.step())
                dve.wait_ge(dve_own, c.n)
                tt(C.c[0:4, 0, 1:TILES], C.m[0:4, 0, 1:TILES], C.j[0:4, 0, 1:TILES], ALU.add).then_inc(dve_own, c.step())
                dve.wait_ge(dve_own, c.n)
                tt(C.c[0:4, 1, 0:TILES - 1], C.m[0:4, 1, 0:TILES - 1], C.j[0:4, 0, 1:TILES], ALU.add).then_inc(dve_own, c.step())
                dve.wait_ge(dve_own, c.n)
                dve.sem_inc(s.scan_mm, 1)
                dve.wait_ge(s.vt_mm, 1)
                dve.sem_inc(s.vt_mm, -1)
                V_.tensor_copy(C.cT[0:QT].rearrange("p k e h -> p (k e h)"), bank[0:QT, 6, 0:QK * 8]).then_inc(dve_own, c.step())
                dve.wait_ge(dve_own, c.n)
                for k in range(QK):
                    kk = C.k[0:QT, k, :]
                    for e, at in ((0, 0), (1, P - 1)):
                        V_.tensor_scalar(C.b[0:QT], kk, kk[:, at:at + 1], None, ALU.is_equal).then_inc(dve_own, c.step())
                        dve.wait_ge(dve_own, c.n)
                        V_.tensor_scalar(C.b[0:QT], C.b[0:QT], -1.0, BIG, ALU.add, ALU.mult).then_inc(dve_own, c.step())
                        dve.wait_ge(dve_own, c.n)
                        for h in range(4):
                            V_.scalar_tensor_tensor(C.fw[0:QT, k, h, :], C.b[0:QT], C.cT[0:QT, k, e, h:h + 1], C.fw[0:QT, k, h, :],
                                                      ALU.add, ALU.max).then_inc(dve_own, c.step())
                        dve.wait_ge(dve_own, c.n)
                    dve.sem_inc(s.scan_mm, 1)
                    dve.wait_ge(s.vt_mm, 1)
                    dve.sem_inc(s.vt_mm, -1)
                    sc = aux[:, k * QT:(k + 1) * QT, 0:4]
                    tt(sc, sc, bank[:, k % 2, 0:4 * QT].rearrange("p (h t) -> p t h", h=4), ALU.subtract).then_inc(dve_own, c.step())
                    dve.wait_ge(dve_own, c.n)
                    dve.sem_inc(s.scan_free, 1)
                dve.sem_inc(s.hid_ready, 1)
                dve.wait_ge(dve_own, c.n)
                dve.sem_inc(dve_own, c.reset())
                barrier(dve, "dve")

                def weigh(g, b, first, half):
                    f = SPEC[3]["f"]
                    dve.wait_ge(s.key_in0 if b == 0 else s.key_in1, 16)
                    dve.sem_inc(s.key_in0 if b == 0 else s.key_in1, -16)
                    if not first:
                        dve.wait_ge(s.msg_free, 1)
                        dve.sem_inc(s.msg_free, -1)
                    select(g, b, P2.keys, P2.sel, dst_f)
                    dve.wait_ge(s.attr_in0 if b == 0 else s.attr_in1, 16)
                    dve.sem_inc(s.attr_in0 if b == 0 else s.attr_in1, -16)
                    pp = aux[:, bass.ds(g * GROUP, GROUP), 0:4]
                    msg = P2.msg[:, b, :].rearrange("p (t c) -> p t c", c=f)
                    hh = P2.h[:, b, :].rearrange("p (t c) -> p t c", c=DIM)
                    V_.tensor_copy(msg[:, :, 160:164], pp).then_inc(dve_own, c.step())
                    tt(msg[:, :, 0:S].rearrange("p t (h c) -> p t h c", h=4), hh[:, :, 0:S].rearrange("p t (h c) -> p t h c", h=4),
                         bc(pp, 3, 16), ALU.mult).then_inc(dve_own, c.step())
                    for i in range(3):
                        lo = S + V * i
                        tt(msg[:, :, lo:lo + V].rearrange("p t (h c) -> p t h c", h=4),
                             hh[:, :, lo:lo + V].rearrange("p t (h c) -> p t h c", h=4), bc(pp, 3, 8), ALU.mult).then_inc(dve_own, c.step())
                    dve.wait_ge(dve_own, c.n)
                    dve.sem_inc(dve_own, c.reset())
                    dve.sem_inc(s.msg_ready, 1)
                    dve.sem_inc(s.attr_free, 1)
                    dve.sem_inc(s.key_free, 1)
                pipelined(dve, GROUPS, [(0, weigh)])
                dve.wait_ge(s.msg_free, 2)
                dve.sem_inc(s.msg_free, -2)
                barrier(dve, "dve")
                post(3)
                barrier(dve, "dve")


LOADS = 16 * 10
WEIGHTS = [
    "L0_gnn_W_skip0", "L0_gnn_W_skip1", "L0_gnn_W_nl0", "L0_gnn_W_nl1", "L0_gnn_W_fc1", "L0_gnn_W_fc2",
    "L0_gnn_W_out_s", "L0_gnn_W_out_v", "L1_gnn_W_sc_s", "L1_gnn_W_sc_v", "L1_gnn_W1_s", "L1_gnn_W1_v",
    "L1_gnn_W2_s", "L1_gnn_W2_v", "L1_gnn_W3", "L1_gnn_fcW1", "L1_gnn_fcW2", "L2_gnn_Wfc1", "L2_gnn_Wfc2",
    "L2_gnn_Wsc0", "L2_gnn_Wsc1", "L2_gnn_Wl1_0", "L2_gnn_Wl1_1", "L2_gnn_Wl2_s", "L2_gnn_Wl2_v", "L2_gnn_Wa",
    "L3_gnn_Ws_src", "L3_gnn_Wv_src", "L3_gnn_Ws_dst", "L3_gnn_Wv_dst", "L3_gnn_W_rbf", "L3_gnn_W_alpha",
    "L3_gnn_Ws_val", "L3_gnn_Wv_val", "L3_gnn_Wg", "L3_gnn_Ws_vlin", "L3_gnn_Wv_vlin", "L3_gnn_Wps", "L3_gnn_Wpv",
]
COLUMNS = ["L3_gnn_gamma_s", "L3_gnn_beta_s", "L3_gnn_gamma_v", "L3_gnn_w2_ss", "L3_gnn_w2_sv", "L3_gnn_w2_vs",
           "L3_gnn_w2_vv0", "L3_gnn_w2_vv1"]


def laid_out(inputs):
    import numpy as np

    more = TILES * P - EDGES
    d = {}

    def edges_first(v, fill=0.0):
        v = np.concatenate([v, np.full((more, v.shape[1]), fill, v.dtype)])
        return v.reshape(TILES, P, -1).transpose(1, 0, 2).reshape(P, -1)

    def features_first(v):
        return np.concatenate([v, np.zeros((more, v.shape[1]), v.dtype)]).T

    d["x"] = np.concatenate([inputs["x"], np.zeros((ROWS - NODES, DIM), np.float32)])
    d["node_vec1"] = np.concatenate([inputs["node_vec1"][:, 0], np.zeros(ROWS - NODES, np.float32)]).reshape(P, SLOTS)
    for name in ("src", "dst"):
        v = np.concatenate([inputs[name], np.full(more, PAD_NODE, np.int32)])
        d[name + "_row"] = v
        d[name] = v.reshape(TILES, P).T
    keys = d["dst_row"].reshape(TILES, P)
    d["dst_tiles"] = np.concatenate([keys, np.full((1, P), ROWS, np.int32)])
    d["tile_last"], d["tile_first"] = keys[:, -1], keys[:, 0]
    d["next_first"] = np.concatenate([keys[1:, 0], np.full(1, ROWS, np.int32)])
    d["last_col"] = d["tile_last"].reshape(QK, QT).T
    d["next_col"] = d["next_first"].reshape(QK, QT).T
    d["edge_attr_3"] = edges_first(inputs["edge_attr_3"], 1.0)
    d["edge_attr_4"] = edges_first(inputs["edge_attr_4"]).reshape(P, TILES, 4)
    for k in (8, 16, 64):
        d[f"edge_attr_{k}"] = features_first(inputs[f"edge_attr_{k}"])
    d["Ws_val_T"] = inputs["L3_gnn_Ws_val"].T
    for name in WEIGHTS:
        d[name] = inputs[name]
    for name in COLUMNS:
        d[name] = inputs[name].reshape(-1, 1)
    d["L3_gnn_alpha_dot"] = inputs["L3_gnn_alpha_dot"].reshape(-1)
    return {k: np.ascontiguousarray(v) for k, v in d.items()}


def kernel(**inputs):
    import numpy as np
    import concourse.bacc as bacc
    from concourse.bass_utils import run_bass_kernel_spmd

    nc = bacc.Bacc("TRN2", target_bir_lowering=False, num_devices=1)
    arrays, args = {}, {}
    for name, v in laid_out({k: np.asarray(v) for k, v in inputs.items()}).items():
        arrays["in_" + name] = v
        args[name] = nc.dram_tensor("in_" + name, v.shape, mybir.dt.from_np(v.dtype), kind="ExternalInput").ap()
    out = nc.dram_tensor("out_x", (NODES, DIM), F32, kind="ExternalOutput").ap()
    build(nc, args, out, LAYERS)
    return run_bass_kernel_spmd(nc, [arrays], core_ids=[0]).results[0]["out_x"]


LAYERS = (0, 1, 2, 3)
```

```python
import math
from contextlib import ExitStack

import concourse.bass as bass
from concourse import mybir

ALU = mybir.AluOpType
ACT = mybir.ActivationFunctionType
AX = mybir.AxisListType.X
F32 = mybir.dt.float32
I32 = mybir.dt.int32
I16 = mybir.dt.int16

P = 128
NODES, DIM = 3125, 160
SLOTS = 25
ROWS = P * SLOTS
TABLE_ROWS = ROWS + P
EDGES = 100000
TILES = 784
GROUP = 4
GROUPS = TILES // GROUP
QT, QK = 112, 7
PAD_NODE = ROWS - 1
S, V = 64, 32
CHAINS = 4
DEPTH = 4
RUN_BANKS = (2, 3, 3, 3)
BIG = 1.0e38

SPEC = {
    0: dict(k=64, w=224, f=480, vec=128, table=224, out_s=96, skip=192),
    1: dict(k=8, w=192, f=384, vec=96, table=160, out_s=64, skip=160),
    2: dict(k=16, w=192, f=384, vec=96, table=160, out_s=64, skip=160),
    3: dict(k=16, w=224, f=164, vec=32, table=160, out_s=64, skip=160),
}


class Steps:

    def __init__(self):
        self.n = 0

    def step(self):
        self.n += 1
        return 1

    def reset(self):
        n, self.n = self.n, 0
        return -n


def pipelined(eng, count, stages, unroll=2):
    ahead, behind = min(lag for lag, _ in stages), max(lag for lag, _ in stages)
    lo = -(-(behind + unroll) // unroll) * unroll
    hi = (count + ahead) // unroll * unroll

    def step(i, part):
        for lag, stage in stages:
            if part is None:
                if 0 <= i - lag < count:
                    stage(i - lag, (i - lag) % unroll, i - lag < 2, (i - lag) // unroll)
            else:
                stage(i * unroll + (part - lag), (part - lag) % unroll, False, i + (part - lag) // unroll)

    for i in range(ahead, lo):
        step(i, None)
    with eng.Fori(lo // unroll, hi // unroll) as it:
        for part in range(unroll):
            step(it, part)
    for i in range(hi, count + behind):
        step(i, None)


def among_first(g, n):
    return isinstance(g, int) and g < n


def build(nc, a, out, layers=(0, 1, 2, 3)):
    with ExitStack() as ctx:
        def sb(name, shape, dt=F32):
            return ctx.enter_context(nc.sbuf_tensor(name, shape, dt))

        def sem(name):
            return ctx.enter_context(nc.semaphore(name))

        def dram(name, shape, dt=F32):
            return nc.dram_tensor(name, shape, dt, kind="Internal").ap()

        node_table = {l: dram(f"node_table{l}", (ROWS, SPEC[l]["table"])) for l in (0, 1, 2)}
        src_table = dram("src_table", (ROWS, DIM))
        dst_table = dram("dst_table", (ROWS, DIM))
        src_sum = [dram(f"src_sum{c}", (TABLE_ROWS, SPEC[0]["f"])) for c in range(CHAINS)]
        run_rows = {l: dram(f"run_rows{l}", (TILES * P, SPEC[l]["f"])) for l in (1, 2, 3)}
        carry = {l: dram(f"carry{l}", (TABLE_ROWS, SPEC[l]["f"])) for l in (1, 2, 3)}
        edge_h = dram("edge_h", (TILES * P, DIM))
        ends = dram("ends", (ROWS + 1, 1))
        keys16 = {name: dram(name + "_keys16", (TILES * P,), I16) for name in ("src", "dst")}

        x = sb("x", [P, SLOTS, DIM])
        skip = sb("skip", [P, SLOTS, 192])
        fore = sb("fore", [P, SLOTS * 224])
        attr = sb("attr", [P, SLOTS])
        y = sb("y", [P, TILES, 6])
        aux = sb("aux", [P, TILES, 5])
        src_i = sb("src_i", [P, TILES], I32)
        dst_i = sb("dst_i", [P, TILES], I32)
        src_f = sb("src_f", [P, TILES])
        dst_f = sb("dst_f", [P, TILES])
        put_i = sb("put_i", [P, TILES], I32)
        ident = sb("ident", [P, P])
        lower = sb("lower", [P, P])
        spare = sb("spare", [P, 1])
        stats = sb("stats", [P, 12, SLOTS])
        last_i = sb("last_i", [P, SLOTS], I32)
        rcnt = sb("rcnt", [P, SLOTS])
        has = sb("has", [P, SLOTS])
        sel2 = sb("sel2", [QT, QK, QT])
        put2_i = sb("put2_i", [QT, QK], I32)
        work = sb("work", [P, 18432])

        def carve():
            at = [0]

            def get(*dims, dt=F32):
                n = math.prod(dims)
                n += n % 2
                assert at[0] + n <= 18432, (at[0], n)
                v = work[:, at[0]:at[0] + n]
                at[0] += n
                v = v[:, 0:math.prod(dims)]
                if dt != F32:
                    v = v.bitcast(dt)
                if len(dims) == 1:
                    return v
                names = " ".join(f"d{i}" for i in range(len(dims)))
                return v.rearrange(f"p ({names}) -> p {names}", **{f"d{i}": d for i, d in enumerate(dims)})

            return get

        bank = ctx.enter_context(nc.psum_tensor("bank", [P, 8, 512], F32))

        wt = {}

        def weight(name, rows, cols):
            wt[name] = sb("w_" + name, [rows, cols])

        weight("fc1_0", 64, 64)
        weight("fc2_0", 64, 224)
        weight("fc1_1", 8, 64)
        weight("fc2_1", 64, 192)
        weight("fc1_2", 16, 64)
        weight("fc2_2", 64, 192)
        weight("rbf", 16, 224)
        for l in range(4):
            weight(f"in_s{l}", 64, 160 if l == 0 else 128)
            weight(f"in_v{l}", 96, 192)
        weight("out_s0", 96, 96)
        weight("out_v0", 128, 32)
        for l in (1, 2):
            weight(f"out_s{l}", 96, 64)
            weight(f"out_v{l}", 96, 32)
            weight(f"out_a{l}", 96, 1)
        weight("out_s3", 64, 64)
        weight("out_v3", 32, 32)
        weight("val_s", 96, 160)
        weight("val_x", 128, 128)
        weight("val_yz", 128, 128)
        weight("gate", 64, 32)
        weight("lin_s", 96, 64)
        weight("lin_x", 128, 128)
        weight("lin_yz", 128, 128)
        val_sT = sb("val_sT", [64, 96])
        gamma_s = sb("gamma_s", [64, 1])
        beta_s = sb("beta_s", [64, 1])
        gamma_v = sb("gamma_v", [96, 1])
        alpha_dot = sb("alpha_dot", [P, 64])
        w2 = sb("w2", [P, 3])

        phase = sem("phase")
        dve_own, act_own, pool_own = sem("dve_own"), sem("act_own"), sem("pool_own")
        loaded, zero_made, zeroed = sem("loaded"), sem("zero_made"), sem("zeroed")
        moved = sem("moved")
        weights_in = sem("weights_in")
        one = {n: sem(n) for n in (
            "blocks_zeroed", "weights_ready", "gate_weights_mm", "weights_whole", "end_tile_ready", "end_keys_free",
            "keys_narrowed", "root_asked", "root_done", "table_in",
            "node_in", "h_ready", "node_turned", "node_in_sbuf", "node_mm", "node_free", "carry_in0", "carry_in1",
            "sum_ready", "sum_free", "row_in0", "second_mm", "second_ready", "second_added", "function_asked",
            "function_done",
            "attr_in0", "attr_in1", "attr_free", "key_in0", "key_in1", "key_free", "got_free", "hid_mm", "hid_ready",
            "hid_free", "w_ready", "w_free", "weights_scaled", "msg_ready", "msg_free", "run_mm", "run_free",
            "run_ready", "store0", "store1",
            "m_ready", "m1_ready", "m1_turned", "m1_in_sbuf", "values_mm", "values_ready", "m2_ready", "m2_turned",
            "m2_in_sbuf", "linear_mm", "linear_free", "scalars_out",
            "scores_turned", "scores_in_sbuf", "scan_ready", "scan_turned", "scan_free", "scores_shifted")}
        keys_got = [sem(f"keys_got{b}") for b in range(2)]
        got = {l: [sem(f"got{l}_{b}") for b in range(DEPTH)] for l in range(4)}
        rows_got = {l: [sem(f"rows_got{l}_{b}") for b in range(2)] for l in (1, 2, 3)}
        carried = {l: sem(f"carried{l}") for l in (1, 2, 3)}
        put = [sem(f"put{c}") for c in range(CHAINS)]
        s = type("Signals", (), one)

        block = ctx.enter_context(nc.Block())
        phases = {"n": {}}

        def barrier(eng, name):
            n = phases["n"][name] = phases["n"].get(name, 0) + 1
            eng.drain().then_inc(phase, 1)
            eng.wait_ge(phase, 5 * n)

        def edge_views():
            g = carve()
            v = type("Edge", (), {})
            v.attr = g(2, 512)
            v.keys = g(512).bitcast(I16).rearrange("p (b n) -> p b n", b=2)
            v.hid = g(2, 512)
            v.got = fore[:, 0:DEPTH * GROUP * 224].rearrange("p (b c) -> p b c", b=DEPTH)
            v.w = g(2, GROUP, 192)
            v.msg = g(2, GROUP * 480)
            v.sel = g(2, GROUP, P)
            v.run = g(2, GROUP * 480)
            v.t0, v.t1, v.t2 = g(GROUP * 160), g(GROUP * 96), g(GROUP * 96)
            v.first = g(GROUP, P)
            v.u1, v.u2 = g(GROUP, 3, V), g(GROUP, 3, V)
            v.idx = g(DEPTH, GROUP, dt=I32)
            v.pidx = g(2, GROUP, dt=I32)
            v.cnt = g(GROUP)
            v.pos = g(GROUP)
            return v

        E = edge_views()

        def node_views():
            g = carve()
            v = type("Node", (), {})
            v.h = g(2, DIM)
            v.hT = g(2, 4, P)
            v.big = g(SLOTS * DIM)
            v.row = g(2, 480)
            v.car = g(2, 4 * 480)
            v.sum = g(2, 480)
            v.c2 = g(480)
            v.c2in = g(480)
            v.idx = g(2, 2, dt=I32)
            v.small = g(8, SLOTS)
            v.smi = g(SLOTS, dt=I32)
            v.rden = g(8)
            return v

        Nv = node_views()

        def l3_views():
            g = carve()
            v = type("L3", (), {})
            v.rb = g(2, 256)
            rows = fore[:, 0:DEPTH * 4 * DIM].rearrange("p (b k t c) -> p b k t c", b=DEPTH, k=2, c=DIM)
            v.gs, v.gd = rows[:, :, 0], rows[:, :, 1]
            v.m = g(2, 2, DIM)
            v.w = g(2, 2, 224)
            v.cv = g(2, 2, 192)
            v.f, v.f2 = g(2, 2, 352), g(2, 2, 352)
            v.t1, v.t2 = g(2, 2, 384), g(2, 2, 384)
            v.al2 = g(2, 64)
            v.dot = g(2, V)
            v.vv = g(2, 3, V)
            v.q, v.u1, v.u2 = g(2, 96), g(2, 96), g(2, 96)
            v.h = g(2, 2, DIM)
            v.idx = g(DEPTH, 2, 2, dt=I32)
            return v

        T = l3_views()

        def pass2_views():
            g = carve()
            v = type("Pass2", (), {})
            v.keys = g(512).bitcast(I16).rearrange("p (b n) -> p b n", b=2)
            v.h = g(2, GROUP * DIM)
            v.msg = g(2, GROUP * 164)
            v.sel = g(2, GROUP, P)
            v.run = g(2, GROUP * 164)
            return v

        P2 = pass2_views()

        def scan_views():
            g = carve()
            v = type("Scan", (), {})
            v.aT = g(QK, 4, P)
            v.bw = g(4, P)
            v.fw = g(QK, 4, P)
            v.kI = g(QK, P, dt=I32)
            v.k = g(QK, P)
            v.b = g(P)
            v.b2 = g(P)
            v.edge = g(QK, 4, 2)
            v.lk, v.fk = g(TILES), g(TILES)
            v.lkI, v.fkI = g(TILES, dt=I32), g(TILES, dt=I32)
            v.m = g(2, TILES)
            v.j = g(2, TILES)
            v.c = g(2, TILES)
            v.cT = g(QK, 2, 4)
            return v

        C = scan_views()

        def setup_views():
            g = carve()
            v = type("Setup", (), {})
            v.lkI, v.nfI = g(TILES, dt=I32), g(TILES, dt=I32)
            v.lk, v.nf, v.t, v.j, v.one = g(TILES), g(TILES), g(TILES), g(TILES), g(TILES)
            v.e3 = g(TILES * 3)
            v.e4 = g(TILES * 4)
            v.wide = {name: g(QK, P, dt=I32) for name in ("src", "dst")}
            v.narrow = {name: g(QK * P // 2).bitcast(I16).rearrange("p (k n) -> p k n", k=QK) for name in ("src", "dst")}
            v.n2 = g(TILES)
            v.rowI = g(2, P, dt=I32)
            v.tile_i = g(SLOTS, dt=I32)
            v.node = g(SLOTS)
            v.node_i = g(SLOTS, dt=I32)
            v.tiles = g(SLOTS)
            v.in_tile = g(SLOTS)
            v.end = g(SLOTS)
            v.prev = g(SLOTS)
            v.lkc_i, v.nfc_i = g(QK, dt=I32), g(QK, dt=I32)
            v.lkc, v.nfc, v.tc, v.cc, v.kc = g(QK), g(QK), g(QK), g(QK), g(QK)
            v.zero = g(480)
            return v

        U = setup_views()

        def group_rows(d, width, per):
            return d.rearrange("(g t p) f -> g p t f", t=per, p=P)

        def wmm(k):
            return bank[:, 1 + 2 * k:3 + 2 * k, :].rearrange("p b (t c) -> p (b t) c", c=256)

        @block.sync
        def _(sp):
            n = 0

            def load(dst, src):
                nonlocal n
                sp.dma_start(dst, src).then_inc(loaded, 16)
                n += 16

            load(x[:], a["x"].rearrange("(p j) c -> p j c", j=SLOTS))
            load(attr[:], a["node_vec1"])
            load(src_i[:], a["src"])
            load(dst_i[:], a["dst"])
            load(U.lkI, a["tile_last"].partition_broadcast(P))
            load(U.nfI, a["next_first"].partition_broadcast(P))
            load(U.lkc_i[0:QT], a["last_col"])
            load(U.nfc_i[0:QT], a["next_col"])
            load(U.e3, a["edge_attr_3"])
            load(U.e4, a["edge_attr_4"].rearrange("p t c -> p (t c)"))
            for name in ("src", "dst"):
                load(U.wide[name][0:QT], a[name + "_row"].rearrange("(k q n) -> q k n", q=QT, n=P))
            assert n == LOADS
            sp.wait_ge(zero_made, 1)
            for table in ([*src_sum] if 0 in layers else []) + [carry[l] for l in (1, 2, 3) if l in layers]:
                width = table.shape[1]
                sp.dma_start(table.rearrange("(p r) f -> p r f", p=P),
                             U.zero[:, 0:width].unsqueeze(1).broadcast_to([P, TABLE_ROWS // P, width])).then_inc(zeroed, 16)
            sp.wait_ge(zeroed, 16 * ((CHAINS if 0 in layers else 0) + len([l for l in layers if l])))
            sp.wait_ge(s.keys_narrowed, 1)
            sp.sem_inc(s.keys_narrowed, -1)
            for name in ("src", "dst"):
                sp.dma_start(keys16[name].rearrange("(k q n) -> q k n", q=QT, n=P), U.narrow[name][0:QT]).then_inc(moved, 16)
            sp.wait_ge(s.table_in, 1)
            sp.sem_inc(s.table_in, -1)
            sp.dma_start(ends[1:ROWS + 1].rearrange("(p j) o -> p (j o)", j=SLOTS), U.end).then_inc(moved, 16)
            sp.dma_start(ends[0:1], U.zero[0:1, 0:1]).then_inc(moved, 16)
            sp.wait_ge(moved, 64)
            sp.dma_start(U.prev, ends[0:ROWS].rearrange("(p j) o -> p (j o)", j=SLOTS)).then_inc(moved, 16)
            barrier(sp, "sp")

            def table_out(l):
                sp.wait_ge(s.table_in, 1)
                sp.sem_inc(s.table_in, -1)
                if l < 3:
                    sp.dma_start(node_table[l].rearrange("(p j) c -> p (j c)", j=SLOTS),
                                 fore[:, 0:SLOTS * SPEC[l]["table"]]).then_inc(s.carry_in0, 16)
                    sp.wait_ge(s.carry_in0, 16)
                    sp.sem_inc(s.carry_in0, -16)
                else:
                    sp.dma_start(src_table.rearrange("(p j) c -> p (j c)", j=SLOTS),
                                 fore[:, 0:SLOTS * DIM]).then_inc(s.carry_in0, 16)
                    sp.dma_start(dst_table.rearrange("(p j) c -> p j c", j=SLOTS),
                                 skip[:, :, 0:DIM]).then_inc(s.carry_in0, 16)
                    sp.wait_ge(s.carry_in0, 32)
                    sp.sem_inc(s.carry_in0, -32)

            def load_attr(attr_name, k):
                def stage(g, b, first, half):
                    if not first:
                        sp.wait_ge(s.attr_free, 1)
                        sp.sem_inc(s.attr_free, -1)
                    sp.dma_start(E.attr[0:k, b, :],
                                 a[attr_name].rearrange("k (g n) -> k g n", n=512)[:, bass.ds(g, 1), :]
                                 .rearrange("k o n -> k (o n)")).then_inc(s.attr_in0 if b == 0 else s.attr_in1, 16)
                return stage

            def load_keys(name, keys):
                def stage(g, b, first, half):
                    if not first:
                        sp.wait_ge(s.key_free, 1)
                        sp.sem_inc(s.key_free, -1)
                    sp.dma_start(keys[:, b, :],
                                 keys16[name].rearrange("(g n) -> g n", n=512)[bass.ds(g, 1), :]
                                 .rearrange("o n -> (o n)").partition_broadcast(P)).then_inc(s.key_in0 if b == 0 else s.key_in1, 16)
                return stage

            def stores(l, run, f):
                def stage(g, b, first, half):
                    sp.wait_ge(s.run_ready, GROUP)
                    sp.sem_inc(s.run_ready, -GROUP)
                    sp.dma_start(group_rows(run_rows[l], f, GROUP)[bass.ds(g, 1)].rearrange("o p t f -> (o p) t f"),
                                 run[:, b, 0:GROUP * f].rearrange("p (t f) -> p t f", f=f)).then_inc(
                        s.store0 if b == 0 else s.store1, 16)
                return stage

            def post(l):
                f = SPEC[l]["f"]
                if l:
                    for k in range(QK):
                        if k:
                            sp.wait_ge(s.second_added, 1)
                            sp.sem_inc(s.second_added, -1)
                        sp.dma_start(Nv.c2in[0:QT, 0:f],
                                     run_rows[l].rearrange("(k q p) f -> q k p f", q=QT, p=P)[:, k, P - 1, :]).then_inc(s.row_in0, 16)
                    sp.wait_ge(s.second_added, 1)
                    sp.sem_inc(s.second_added, -1)

                def stage(j, b, first, half):
                    if not first:
                        sp.wait_ge(s.sum_free, 1)
                        sp.sem_inc(s.sum_free, -1)
                    for c in range(1 if l else CHAINS):
                        table = carry[l] if l else src_sum[c]
                        sp.dma_start(Nv.car[:, b, c * f:(c + 1) * f],
                                     table[0:ROWS].rearrange("(p j) f -> j p f", j=SLOTS)[bass.ds(j, 1)]
                                     .rearrange("o p f -> (o p) f")).then_inc(s.carry_in0 if b == 0 else s.carry_in1, 16)
                pipelined(sp, SLOTS, [(0, stage)])
                sp.wait_ge(s.sum_free, 2)
                sp.sem_inc(s.sum_free, -2)

            for l in (0, 1, 2):
                if l not in layers:
                    continue
                table_out(l)
                barrier(sp, "sp")
                stages = [(-3 if l else -2, load_attr(("edge_attr_64", "edge_attr_8", "edge_attr_16")[l], SPEC[l]["k"])),
                          (0, load_keys("src" if l == 0 else "dst", E.keys))]
                if l:
                    stages.append((2, stores(l, E.run, SPEC[l]["f"])))
                pipelined(sp, GROUPS, stages)
                sp.wait_ge(s.attr_free, 2)
                sp.sem_inc(s.attr_free, -2)
                sp.wait_ge(s.key_free, 2)
                sp.sem_inc(s.key_free, -2)
                barrier(sp, "sp")
                post(l)
                barrier(sp, "sp")
            if 3 in layers:
                table_out(3)
                barrier(sp, "sp")

                def rbf(g, b, first, half):
                    if not first:
                        sp.wait_ge(s.attr_free, 1)
                        sp.sem_inc(s.attr_free, -1)
                    sp.dma_start(T.rb[0:16, b, :],
                                 a["edge_attr_16"].rearrange("k (g n) -> k g n", n=256)[:, bass.ds(g, 1), :]
                                 .rearrange("k o n -> k (o n)")).then_inc(s.attr_in0 if b == 0 else s.attr_in1, 16)

                def keep_h(g, b, first, half):
                    sp.wait_ge(s.h_ready, 1)
                    sp.sem_inc(s.h_ready, -1)
                    sp.dma_start(edge_h.rearrange("(g t p) f -> g p t f", t=2, p=P)[bass.ds(g, 1)]
                                 .rearrange("o p t f -> (o p) t f"), T.h[:, b]).then_inc(s.store0 if b == 0 else s.store1, 16)
                pipelined(sp, TILES // 2, [(0, rbf), (5, keep_h)])
                sp.wait_ge(s.attr_free, 2)
                sp.sem_inc(s.attr_free, -2)
                barrier(sp, "sp")
                sp.dma_start(C.kI[0:QT], a["dst_row"].rearrange("(k q n) -> q k n", q=QT, n=P)).then_inc(s.key_in0, 16)
                sp.dma_start(C.lkI, a["tile_last"].partition_broadcast(P)).then_inc(s.key_in0, 16)
                sp.dma_start(C.fkI, a["tile_first"].partition_broadcast(P)).then_inc(s.key_in0, 16)
                barrier(sp, "sp")

                def load_h(g, b, first, half):
                    if not first:
                        sp.wait_ge(s.attr_free, 1)
                        sp.sem_inc(s.attr_free, -1)
                    sp.dma_start(P2.h[:, b, :].rearrange("p (t f) -> p t f", f=DIM),
                                 group_rows(edge_h, DIM, GROUP)[bass.ds(g, 1)].rearrange("o p t f -> (o p) t f")).then_inc(
                        s.attr_in0 if b == 0 else s.attr_in1, 16)
                pipelined(sp, GROUPS, [(0, load_h), (0, load_keys("dst", P2.keys)),
                                       (2, stores(3, P2.run, SPEC[3]["f"]))])
                sp.wait_ge(s.attr_free, 2)
                sp.sem_inc(s.attr_free, -2)
                sp.wait_ge(s.key_free, 2)
                sp.sem_inc(s.key_free, -2)
                barrier(sp, "sp")
                post(3)
                barrier(sp, "sp")
            sp.dma_start(out.rearrange("(p j) c -> p j c", j=SLOTS), x[0:NODES // SLOTS]).then_inc(moved, 16)
            sp.wait_ge(moved, 96)

        @block.gpsimd
        def _(pool):
            own = Steps()
            last_row = pool.to_reg(ROWS - 1)
            last_table_row = pool.to_reg(TABLE_ROWS - 1)
            last_tile = pool.to_reg(TILES)

            def gather(dst, table, idx, bound):
                return pool.indirect_dma_start(dst, None, table, bass.IndirectOffsetOnAxis(ap=idx, axis=0),
                                               bounds_check=bound, oob_is_err=True)

            nc.gpsimd.memset(U.zero, 0.0).then_inc(pool_own, own.step())
            nc.gpsimd.memset(ident[:], 0.0).then_inc(pool_own, own.step())
            nc.gpsimd.memset(lower[:], 1.0).then_inc(pool_own, own.step())
            nc.gpsimd.iota(U.node_i, pattern=[[1, SLOTS]], base=0, channel_multiplier=SLOTS).then_inc(pool_own, own.step())
            nc.gpsimd.iota(U.lk.bitcast(I32), pattern=[[1, TILES]], base=4000, channel_multiplier=0).then_inc(pool_own, own.step())
            nc.gpsimd.iota(U.cc.bitcast(I32), pattern=[[QT, QK]], base=4000, channel_multiplier=1).then_inc(pool_own, own.step())
            nc.gpsimd.iota(U.kc.bitcast(I32), pattern=[[0, QK]], base=ROWS, channel_multiplier=1).then_inc(pool_own, own.step())
            pool.wait_ge(pool_own, own.n)
            nc.gpsimd.affine_select(out=ident[:], in_=ident[:], compare_op=ALU.not_equal, fill=1.0, base=0,
                                        pattern=[[-1, P]], channel_multiplier=1).then_inc(pool_own, own.step())
            nc.gpsimd.affine_select(out=lower[:], in_=lower[:], compare_op=ALU.is_gt, fill=0.0, base=0,
                                        pattern=[[-1, P]], channel_multiplier=1).then_inc(pool_own, own.step())
            pool.wait_ge(pool_own, own.n)
            pool.sem_inc(pool_own, own.reset())
            pool.sem_inc(zero_made, 2)
            pool.wait_ge(s.end_tile_ready, 1)
            pool.sem_inc(s.end_tile_ready, -1)
            for j in range(SLOTS):
                if j >= 2:
                    pool.wait_ge(s.end_keys_free, 1)
                    pool.sem_inc(s.end_keys_free, -1)
                nc.gpsimd.tensor_copy(put_i[:, j:j + 1], U.tile_i[:, j:j + 1]).then_inc(pool_own, own.step())
                pool.wait_ge(pool_own, own.n)
                pool.sem_inc(pool_own, own.reset())
                gather(U.rowI[:, j % 2, :], a["dst_tiles"], put_i[:, j:j + 1], last_tile).then_inc(
                    keys_got[j % 2], 16)
            pool.wait_ge(s.end_keys_free, 2)
            pool.sem_inc(s.end_keys_free, -2)
            barrier(pool, "pool")

            def gathers(l, table, indices, buf, width):
                def stage(g, b, first, half):
                    if not among_first(g, DEPTH):
                        pool.wait_ge(s.got_free, 1)
                        pool.sem_inc(s.got_free, -1)
                    nc.gpsimd.tensor_copy(E.idx[:, b, :], indices[:, bass.ds(g * GROUP, GROUP)]).then_inc(pool_own, own.step())
                    pool.wait_ge(pool_own, own.n)
                    pool.sem_inc(pool_own, own.reset())
                    for t in range(GROUP):
                        gather(buf[:, b, t * width:(t + 1) * width], table, E.idx[:, b, t:t + 1], last_row).then_inc(
                            got[l][b], 16)
                return stage

            def scatter(g, b, first, half):
                for t in range(GROUP):
                    if not (isinstance(g, int) and g == 0):
                        pool.wait_ge(put[t], g * 16)
                    pool.wait_ge(s.run_ready, 1)
                    pool.sem_inc(s.run_ready, -1)
                    if t == 0:
                        nc.gpsimd.tensor_copy(E.pidx[:, b % 2, :], put_i[:, bass.ds(g * GROUP, GROUP)]).then_inc(pool_own, own.step())
                        pool.wait_ge(pool_own, own.n)
                        pool.sem_inc(pool_own, own.reset())
                    pool.indirect_dma_start(
                        src_sum[t], bass.IndirectOffsetOnAxis(ap=E.pidx[:, b % 2, t:t + 1], axis=0),
                        E.run[:, b % 2, t * 480:(t + 1) * 480], None, compute_op=ALU.add,
                        bounds_check=last_table_row, oob_is_err=True).then_inc(put[t], 16)

            def post(l):
                f = SPEC[l]["f"]
                if not l:
                    return
                for k in range(QK):
                    pool.wait_ge(s.second_ready, 1)
                    pool.sem_inc(s.second_ready, -1)
                    pool.indirect_dma_start(
                        carry[l], bass.IndirectOffsetOnAxis(ap=put2_i[:, k:k + 1], axis=0),
                        Nv.c2[0:QT, 0:f], None, compute_op=ALU.add,
                        bounds_check=last_table_row, oob_is_err=True).then_inc(carried[l], 16)
                    pool.wait_ge(carried[l], 16 * (k + 1))
                    pool.sem_inc(s.second_added, 1)

                def stage(j, b, first, half):
                    if not first:
                        pool.wait_ge(s.got_free, 1)
                        pool.sem_inc(s.got_free, -1)
                    nc.gpsimd.tensor_copy(Nv.idx[:, b, 0:1], last_i[:, bass.ds(j, 1)]).then_inc(pool_own, own.step())
                    pool.wait_ge(pool_own, own.n)
                    pool.sem_inc(pool_own, own.reset())
                    gather(Nv.row[:, b, 0:f], run_rows[l], Nv.idx[:, b, 0:1], last_edge).then_inc(
                        rows_got[l][b], 16)
                pipelined(pool, SLOTS, [(0, stage)])
                pool.wait_ge(s.got_free, 2)
                pool.sem_inc(s.got_free, -2)

            last_edge = pool.to_reg(TILES * P - 1)
            for l in (0, 1, 2):
                if l not in layers:
                    continue
                barrier(pool, "pool")
                stages = [(0, gathers(l, node_table[l], src_i if l else dst_i, E.got, SPEC[l]["table"]))]
                if l == 0:
                    stages.append((2, scatter))
                pipelined(pool, GROUPS, stages, unroll=DEPTH)
                pool.wait_ge(s.got_free, DEPTH)
                pool.sem_inc(s.got_free, -DEPTH)
                barrier(pool, "pool")
                post(l)
                barrier(pool, "pool")
            if 3 in layers:
                barrier(pool, "pool")

                def gather_both(g, b, first, half):
                    nc.gpsimd.tensor_copy(T.idx[:, b, 0, :], src_i[:, bass.ds(g * 2, 2)]).then_inc(pool_own, own.step())
                    nc.gpsimd.tensor_copy(T.idx[:, b, 1, :], dst_i[:, bass.ds(g * 2, 2)]).then_inc(pool_own, own.step())
                    pool.wait_ge(pool_own, own.n)
                    pool.sem_inc(pool_own, own.reset())
                    for t in range(2):
                        gather(T.gs[:, b, t, :], src_table, T.idx[:, b, 0, t:t + 1], last_row).then_inc(
                            got[3][b], 16)
                        gather(T.gd[:, b, t, :], dst_table, T.idx[:, b, 1, t:t + 1], last_row).then_inc(
                            got[3][b], 16)

                def add_both(g, b, first, half):
                    pool.wait_ge(got[3][b], (half + 1) * 64)
                    if not among_first(g, 2):
                        pool.wait_ge(s.got_free, 1)
                        pool.sem_inc(s.got_free, -1)
                    nc.gpsimd.tensor_tensor(T.m[:, b % 2], T.gs[:, b], T.gd[:, b], ALU.add).then_inc(s.m_ready, 1)
                pipelined(pool, TILES // 2, [(2, add_both), (0, gather_both)], unroll=DEPTH)
                pool.wait_ge(s.got_free, 2)
                pool.sem_inc(s.got_free, -2)
                barrier(pool, "pool")
                barrier(pool, "pool")
                barrier(pool, "pool")
                post(3)
                barrier(pool, "pool")

        INPUT_MAPS = (
            ("L0_gnn_W_nl0", "L0_gnn_W_skip0", "L0_gnn_W_nl1", "L0_gnn_W_skip1"),
            ("L1_gnn_W1_s", "L1_gnn_W_sc_s", "L1_gnn_W1_v", "L1_gnn_W_sc_v"),
            ("L2_gnn_Wl1_0", "L2_gnn_Wsc0", "L2_gnn_Wl1_1", "L2_gnn_Wsc1"),
            ("L3_gnn_Ws_src", "L3_gnn_Ws_dst", "L3_gnn_Wv_src", "L3_gnn_Wv_dst"),
        )
        BY_Y0 = ((0, 0, 64), (64, 128, 32), (96, 64, 64), (160, 160, 64))

        @block.scalar
        def _(act):
            own = Steps()

            def wload(dst, src):
                act.dma_start(dst, src).then_inc(weights_in, 16)
                wload.n += 16
            wload.n = 0
            for name, key in (("fc1_0", "L0_gnn_W_fc1"), ("fc2_0", "L0_gnn_W_fc2"), ("fc1_1", "L1_gnn_fcW1"),
                              ("fc1_2", "L2_gnn_Wfc1"),
                              ("out_s0", "L0_gnn_W_out_s"), ("out_v0", "L0_gnn_W_out_v"),
                              ("out_s1", "L1_gnn_W2_s"), ("out_v1", "L1_gnn_W2_v"), ("out_a1", "L1_gnn_W3"),
                              ("out_s2", "L2_gnn_Wl2_s"), ("out_v2", "L2_gnn_Wl2_v"), ("out_a2", "L2_gnn_Wa"),
                              ("out_s3", "L3_gnn_Wps"), ("out_v3", "L3_gnn_Wpv"), ("gate", "L3_gnn_Wg"), ("lin_s", "L3_gnn_Ws_vlin")):
                wload(wt[name][:], a[key])
            for l, (f_s, k_s, _, _) in enumerate(INPUT_MAPS):
                wload(wt[f"in_s{l}"][:, 0:64], a[f_s])
                wload(wt[f"in_s{l}"][:, 64:], a[k_s])
            for name, key in (("fc2_1", "L1_gnn_fcW2"), ("fc2_2", "L2_gnn_Wfc2"), ("rbf", "L3_gnn_W_rbf")):
                for to, at, n in BY_Y0:
                    n = min(n, wt[name].shape[1] - to)
                    wload(wt[name][:, to:to + n], a[key][:, at:at + n])
            wload(wt["val_s"][:, 32:96], a["L3_gnn_Ws_val"])
            wload(wt["val_s"][:, 96:160], a["L3_gnn_W_alpha"])
            wload(val_sT[:], a["Ws_val_T"])
            wload(gamma_s[:], a["L3_gnn_gamma_s"])
            wload(beta_s[:], a["L3_gnn_beta_s"])
            for i in range(3):
                wload(gamma_v[V * i:V * (i + 1)], a["L3_gnn_gamma_v"])
            wload(alpha_dot[:], a["L3_gnn_alpha_dot"].partition_broadcast(P))
            wload(w2[0:64, 0:1], a["L3_gnn_w2_ss"])
            wload(w2[64:96, 0:1], a["L3_gnn_w2_vv0"])
            wload(w2[0:64, 1:2], a["L3_gnn_w2_sv"])
            for at, col, key in ((64, 1, "w2_vs"), (96, 1, "w2_vv1"), (0, 2, "w2_vs"), (32, 2, "w2_vv1"),
                                 (64, 2, "w2_vs"), (96, 2, "w2_vv1")):
                wload(w2[at:at + 32, col:col + 1], a["L3_gnn_" + key])
            act.wait_ge(weights_in, wload.n)
            act.wait_ge(s.blocks_zeroed, 1)
            act.sem_inc(s.blocks_zeroed, -1)
            for l, (_, _, f_v, k_v) in enumerate(INPUT_MAPS):
                for i in range(3):
                    for k, key in enumerate((f_v, k_v)):
                        c0 = 96 * k + V * i
                        wload(wt[f"in_v{l}"][V * i:V * (i + 1), c0:c0 + V], a[key])
            for name, key in (("val", "L3_gnn_Wv_val"), ("lin", "L3_gnn_Wv_vlin")):
                wload(wt[name + "_x"][0:64, 0:32], a[key][0:64])
                wload(wt[name + "_x"][64:128, 32:64], a[key][64:128])
                wload(wt[name + "_yz"][0:64, 64:96], a[key][64:128])
                wload(wt[name + "_yz"][64:128, 96:128], a[key][64:128])
            act.wait_ge(weights_in, wload.n)
            act.sem_inc(s.weights_ready, 1)
            act.wait_ge(s.gate_weights_mm, 1)
            act.sem_inc(s.gate_weights_mm, -1)
            act.activation(wt["val_s"][:, 0:32], bank[0:96, 0, 0:32], ACT.Copy).then_inc(act_own, own.step())
            act.wait_ge(act_own, own.n)
            act.sem_inc(act_own, own.reset())
            act.sem_inc(s.weights_whole, 1)

            def root(t, v):
                act.wait_ge(s.root_asked, 1)
                act.sem_inc(s.root_asked, -1)
                act.activation(t, v, ACT.Sqrt).then_inc(s.root_done, 1)
            root(U.j, U.n2)
            barrier(act, "act")

            def prep(l):
                for row in (0,) if l < 3 else (0, 2, 4):
                    root(stats[:, 8, :], stats[:, row, :])

                def features(j, b, first, half):
                    act.wait_ge(s.node_in, 1)
                    act.sem_inc(s.node_in, -1)
                    if l < 3:
                        row = x[:, bass.ds(j, 1), :].rearrange("p o c -> p (o c)")
                        act.activation(Nv.h[:, b, 0:S], row[:, 0:S], ACT.Relu, bias=stats[:, 1, bass.ds(j, 1)],
                                       scale=stats[:, 0, bass.ds(j, 1)]).then_inc(act_own, own.step())
                        act.activation(Nv.h[:, b, S:DIM].rearrange("p (i m) -> p m i", i=3),
                                       row[:, S:DIM].rearrange("p (m i) -> p m i", i=3), ACT.Relu,
                                       bias=stats[:, 1, bass.ds(j, 1)], scale=stats[:, 0, bass.ds(j, 1)]).then_inc(s.h_ready, 1)
                    else:
                        act.activation(Nv.h[:, b, :], fore[:, bass.ds(j * DIM, DIM)], ACT.Copy).then_inc(s.h_ready, 1)

                def turned(j, b, first, half):
                    act.wait_ge(s.node_turned, 1)
                    act.sem_inc(s.node_turned, -1)
                    scalars, vectors = bank[0:64, b, 0:128], bank[0:96, b, 128:256]
                    if l < 3:
                        act.activation(Nv.hT[0:64, b, 0, :], scalars, ACT.Copy).then_inc(act_own, own.step())
                        act.activation(Nv.hT[0:96, b, 1, :], vectors, ACT.Copy).then_inc(s.node_in_sbuf, 1)
                    else:
                        act.activation(Nv.hT[0:64, b, 0, :], scalars, ACT.Identity,
                                       bias=beta_s[:], scale=gamma_s[:]).then_inc(act_own, own.step())
                        act.activation(Nv.hT[0:96, b, 1, :], vectors, ACT.Copy, scale=gamma_v[:]).then_inc(s.node_in_sbuf, 1)
                    act.wait_ge(act_own, own.n)
                    act.sem_inc(act_own, own.reset())
                pipelined(act, SLOTS, [(0, features), (1, turned)])

            def hidden(l):
                def stage(g, part, first, half):
                    b = part % 2
                    act.wait_ge(s.hid_mm, 1)
                    act.sem_inc(s.hid_mm, -1)
                    act.sem_inc(s.attr_free, 1)
                    if l == 0 and not first:
                        act.wait_ge(s.hid_free, 1)
                        act.sem_inc(s.hid_free, -1)
                    act.activation(E.hid[0:64, b, :], bank[0:64, 0 if l else 7 * b, :], ACT.Relu if l == 0 else ACT.Silu,
                                   scale=(1.0, 8 ** -0.5, 0.25)[l]).then_inc(s.hid_ready, 1)
                return stage

            def weights_out(g, part, first, half):
                b = part % 2
                act.wait_ge(s.w_ready, 1)
                act.sem_inc(s.w_ready, -1)
                if not first:
                    act.wait_ge(s.w_free, 1)
                    act.sem_inc(s.w_free, -1)
                for t in range(GROUP):
                    act.activation(E.w[:, b, t, 0:96], wmm(b)[:, t, 0:96], ACT.Copy,
                                   scale=y[:, bass.ds(g * GROUP + t, 1), 0]).then_inc(act_own, own.step())
                act.activation(E.w[:, b, :, 96:192], wmm(b)[:, :, 96:192], ACT.Copy).then_inc(act_own, own.step())
                act.wait_ge(act_own, own.n)
                act.sem_inc(act_own, own.reset())
                act.sem_inc(s.weights_scaled, 1)

            def evacuate(l, run):
                f, store = SPEC[l]["f"], l > 0

                def stage(g, part, first, half):
                    b = part % 2
                    if store and not first:
                        act.wait_ge(s.store0 if b == 0 else s.store1, 16)
                        act.sem_inc(s.store0 if b == 0 else s.store1, -16)
                    for t in range(GROUP):
                        if not store and not first:
                            act.wait_ge(put[t], (g - 1) * 16)
                        act.wait_ge(s.run_mm, 1)
                        act.sem_inc(s.run_mm, -1)
                        if t == GROUP - 1:
                            act.sem_inc(s.msg_free, 1)
                        act.activation(run[:, b, t * f:(t + 1) * f], bank[:, 5 + (part * GROUP + t) % RUN_BANKS[l], 0:f], ACT.Copy).then_inc(act_own, own.step())
                        act.wait_ge(act_own, own.n)
                        act.sem_inc(act_own, own.reset())
                        act.sem_inc(s.run_free, 1)
                        act.sem_inc(s.run_ready, 1)
                return stage

            def post(l):
                f, vec = SPEC[l]["f"], SPEC[l]["vec"]
                top = 64 if l == 3 else 96
                if l:
                    for k in range(QK):
                        act.wait_ge(s.second_mm, 1)
                        act.sem_inc(s.second_mm, -1)
                        act.activation(Nv.c2[0:QT, 0:f], bank[0:QT, 4, 0:f], ACT.Copy).then_inc(s.second_ready, 1)

                def turned(j, b, first, half):
                    act.wait_ge(s.node_turned, 1)
                    act.sem_inc(s.node_turned, -1)
                    act.activation(Nv.hT[0:top, b, 0, :], bank[0:top, b, 0:128], ACT.Copy).then_inc(act_own, own.step())
                    act.activation(Nv.hT[0:vec, b, 1:4, :], bank[0:vec, b, 128:512].rearrange("p (i n) -> p i n", i=3),
                                   ACT.Copy).then_inc(s.node_in_sbuf, 1)
                    act.wait_ge(act_own, own.n)
                    act.sem_inc(act_own, own.reset())
                pipelined(act, SLOTS, [(0, turned)])
                if l == 0:
                    o = fore[:, 0:SLOTS * 192].rearrange("p (j c) -> p j c", c=192)
                    act.wait_ge(s.function_asked, 1)
                    act.sem_inc(s.function_asked, -1)
                    act.activation(skip[:, :, 0:96], o[:, :, 0:96], ACT.Sigmoid).then_inc(act_own, own.step())
                    act.wait_ge(act_own, own.n)
                    act.sem_inc(act_own, own.reset())
                    act.sem_inc(s.function_done, 1)
                if l == 1:
                    act.wait_ge(s.function_asked, 1)
                    act.sem_inc(s.function_asked, -1)
                    act.activation(Nv.small[:, 4:6, :], Nv.small[:, 2:4, :], ACT.Sin, scale=2 * math.pi).then_inc(act_own, own.step())
                    act.wait_ge(act_own, own.n)
                    act.sem_inc(act_own, own.reset())
                    act.sem_inc(s.function_done, 1)

            for l in (0, 1, 2):
                if l not in layers:
                    continue
                prep(l)
                barrier(act, "act")
                evacuating = (1, evacuate(l, E.run))
                pipelined(act, GROUPS, [evacuating, (-2, weights_out), (-3, hidden(l))] if l else [(-2, hidden(l)), evacuating],
                          unroll=2 * RUN_BANKS[l])
                if l == 0:
                    for t in range(GROUP):
                        act.wait_ge(put[t], GROUPS * 16)
                else:
                    act.wait_ge(s.store0, 16)
                    act.sem_inc(s.store0, -16)
                    act.wait_ge(s.store1, 16)
                    act.sem_inc(s.store1, -16)
                if l == 0:
                    act.wait_ge(s.hid_free, 2)
                    act.sem_inc(s.hid_free, -2)
                else:
                    act.wait_ge(s.w_free, 2)
                    act.sem_inc(s.w_free, -2)
                barrier(act, "act")
                post(l)
                barrier(act, "act")
            if 3 in layers:
                prep(3)
                barrier(act, "act")

                def m1_turned(g, b, first, half):
                    act.wait_ge(s.m1_turned, 1)
                    act.sem_inc(s.m1_turned, -1)
                    act.activation(T.t1[0:96, b, :, 0:128], bank[0:96, 1:3, 0:128], ACT.Copy).then_inc(act_own, own.step())
                    act.activation(T.t1[:, b, :, 128:384], bank[:, 1:3, 128:384], ACT.Copy).then_inc(act_own, own.step())
                    act.wait_ge(act_own, own.n)
                    act.sem_inc(act_own, own.reset())
                    act.sem_inc(s.m1_in_sbuf, 1)

                def weights_by_y0_3(g, b, first, half):
                    act.wait_ge(s.w_ready, 1)
                    act.sem_inc(s.w_ready, -1)
                    act.sem_inc(s.attr_free, 1)
                    for t in range(2):
                        act.activation(T.w[:, b, t, 0:96], bank[:, 0, t * 256:t * 256 + 96], ACT.Copy,
                                       scale=y[:, bass.ds(g * 2 + t, 1), 0]).then_inc(act_own, own.step())
                    act.activation(T.w[:, b, :, 96:224], bank[:, 0, :].rearrange("p (t c) -> p t c", t=2)[:, :, 96:224],
                                   ACT.Copy).then_inc(act_own, own.step())
                    act.wait_ge(act_own, own.n)
                    act.sem_inc(act_own, own.reset())
                    act.sem_inc(s.weights_scaled, 1)
                    act.sem_inc(s.w_free, 1)

                def values_out(g, b, first, half):
                    act.wait_ge(s.values_mm, 1)
                    act.sem_inc(s.values_mm, -1)
                    c1 = bank[:, 6:8, 0:288]
                    act.activation(T.f2[:, b, :, 64:160], c1[:, :, 0:96], ACT.Sigmoid).then_inc(act_own, own.step())
                    act.activation(T.cv[:, b], c1[:, :, 96:288], ACT.Copy).then_inc(act_own, own.step())
                    act.wait_ge(act_own, own.n)
                    for t in range(2):
                        act.activation(T.f2[:, b, t, 0:64], T.f2[:, b, t, 96:160], ACT.Copy,
                                       scale=y[:, bass.ds(g * 2 + t, 1), 0]).then_inc(act_own, own.step())
                    act.wait_ge(act_own, own.n)
                    act.sem_inc(act_own, own.reset())
                    act.sem_inc(s.values_ready, 1)

                def m2_turned(g, b, first, half):
                    act.wait_ge(s.m2_turned, 1)
                    act.sem_inc(s.m2_turned, -1)
                    act.activation(T.t2[0:96, b, :, 0:128], bank[0:96, 4:6, 0:128], ACT.Copy).then_inc(act_own, own.step())
                    act.activation(T.t2[:, b, :, 128:384], bank[:, 4:6, 128:384], ACT.Copy).then_inc(act_own, own.step())
                    act.wait_ge(act_own, own.n)
                    act.sem_inc(act_own, own.reset())
                    act.sem_inc(s.m2_in_sbuf, 1)

                def scalars_out(g, b, first, half):
                    if not first:
                        act.wait_ge(s.store0 if b == 0 else s.store1, 16)
                        act.sem_inc(s.store0 if b == 0 else s.store1, -16)
                    act.wait_ge(s.linear_mm, 1)
                    act.sem_inc(s.linear_mm, -1)
                    act.activation(T.h[:, b, :, 0:64], bank[:, 3, 0:384].rearrange("p (t c) -> p t c", t=2)[:, :, 0:64],
                                   ACT.Copy).then_inc(s.scalars_out, 1)
                pipelined(act, TILES // 2, [(-1, m1_turned), (1, scalars_out), (-1, values_out), (0, m2_turned), (-3, weights_by_y0_3)])
                act.wait_ge(s.store0, 16)
                act.sem_inc(s.store0, -16)
                act.wait_ge(s.store1, 16)
                act.sem_inc(s.store1, -16)
                barrier(act, "act")
                for k in range(QK):
                    act.wait_ge(s.scores_turned, 1)
                    act.sem_inc(s.scores_turned, -1)
                    act.activation(C.aT[0:QT, k], bank[0:QT, k % 2, :].rearrange("p (h n) -> p h n", h=4), ACT.Copy).then_inc(s.scores_in_sbuf, 1)
                act.wait_ge(s.scores_shifted, 1)
                act.sem_inc(s.scores_shifted, -1)
                act.activation(aux[:, :, 0:4], aux[:, :, 0:4], ACT.Exp).then_inc(act_own, own.step())
                act.wait_ge(act_own, own.n)
                act.sem_inc(act_own, own.reset())
                barrier(act, "act")
                pipelined(act, GROUPS, [(1, evacuate(3, P2.run))], unroll=2 * RUN_BANKS[3])
                act.wait_ge(s.store0, 16)
                act.sem_inc(s.store0, -16)
                act.wait_ge(s.store1, 16)
                act.sem_inc(s.store1, -16)
                barrier(act, "act")
                post(3)
                barrier(act, "act")

        @block.tensor
        def _(pe):
            pe.wait_ge(s.weights_ready, 1)
            pe.sem_inc(s.weights_ready, -1)
            nc.tensor.matmul(bank[0:96, 0, 0:32], val_sT[:], wt["gate"][:], start=True, stop=True).then_inc(s.gate_weights_mm, 1)
            barrier(pe, "pe")

            def turn(l, what, j, b, blocks):
                for i, (c0, w) in enumerate(blocks):
                    last = nc.tensor.transpose(bank[0:w, b, i * P:(i + 1) * P], what[:, b, c0:c0 + w], ident[:])
                last.then_inc(s.node_turned, 1)

            def prep(l):
                blocks = [(0, 64), (64, 96)]

                def turns(j, b, first, half):
                    pe.wait_ge(s.h_ready, 1)
                    pe.sem_inc(s.h_ready, -1)
                    turn(l, Nv.h, j, b, blocks)

                def products(j, b, first, half):
                    pe.wait_ge(s.node_in_sbuf, 1)
                    pe.sem_inc(s.node_in_sbuf, -1)
                    if not first:
                        pe.wait_ge(s.node_free, 1)
                        pe.sem_inc(s.node_free, -1)
                    o = bank[:, 2 + b, :]
                    ks = 96 if l == 0 else 64
                    nc.tensor.matmul(o[:, 0:64 + ks], Nv.hT[0:64, b, 0, :], wt[f"in_s{l}"][:], start=True, stop=True)
                    last = nc.tensor.matmul(o[:, 160:352], Nv.hT[0:96, b, 1, :], wt[f"in_v{l}"][:], start=True, stop=True)
                    last.then_inc(s.node_mm, 1)
                pipelined(pe, SLOTS, [(0, turns), (1, products)])
                pe.wait_ge(s.node_free, 2)
                pe.sem_inc(s.node_free, -2)

            def hidden(l):
                def stage(g, part, first, half):
                    b = part % 2
                    pe.wait_ge(s.attr_in0 if b == 0 else s.attr_in1, 16)
                    pe.sem_inc(s.attr_in0 if b == 0 else s.attr_in1, -16)
                    k = SPEC[l]["k"]
                    nc.tensor.matmul(bank[0:64, 0 if l else 7 * b, :], wt[f"fc1_{l}"][:], E.attr[0:k, b, :], start=True, stop=True).then_inc(s.hid_mm, 1)
                return stage

            def edge_weights(l):
                def stage(g, part, first, half):
                    b = part % 2
                    pe.wait_ge(s.hid_ready, 1)
                    pe.sem_inc(s.hid_ready, -1)
                    if l == 0 and not first:
                        pe.wait_ge(s.w_free, 1)
                        pe.sem_inc(s.w_free, -1)
                    for t in range(GROUP):
                        last = nc.tensor.matmul(wmm(b)[:, t, 0:SPEC[l]["w"]], E.hid[0:64, b, t * P:(t + 1) * P], wt[f"fc2_{l}"][:],
                                                start=True, stop=True)
                    last.then_inc(s.w_ready, 1)
                return stage

            def sums(l, sel, msg):
                f = SPEC[l]["f"]

                def stage(g, part, first, half):
                    b = part % 2
                    pe.wait_ge(s.msg_ready, 1)
                    pe.sem_inc(s.msg_ready, -1)
                    for t in range(GROUP):
                        if not (among_first(g, 1) and t < RUN_BANKS[l]):
                            pe.wait_ge(s.run_free, 1)
                            pe.sem_inc(s.run_free, -1)
                        nc.tensor.matmul(bank[:, 5 + (part * GROUP + t) % RUN_BANKS[l], 0:f], sel[:, b, t, :], msg[:, b, t * f:(t + 1) * f],
                                         start=True, stop=True).then_inc(s.run_mm, 1)
                return stage

            def post(l):
                f, vec = SPEC[l]["f"], SPEC[l]["vec"]
                top = 64 if l == 3 else 96
                out_s = SPEC[l]["out_s"]
                if l:
                    for k in range(QK):
                        pe.wait_ge(s.row_in0, 16)
                        pe.sem_inc(s.row_in0, -16)
                        nc.tensor.matmul(bank[0:QT, 4, 0:f], sel2[:, k, :], Nv.c2in[0:QT, 0:f], start=True, stop=True).then_inc(s.second_mm, 1)

                def turns(j, b, first, half):
                    pe.wait_ge(s.sum_ready, 1)
                    pe.sem_inc(s.sum_ready, -1)
                    turn(l, Nv.sum, j, b, [(0, top)] + [(top + vec * i, vec) for i in range(3)])

                def products(j, b, first, half):
                    pe.wait_ge(s.node_in_sbuf, 1)
                    pe.sem_inc(s.node_in_sbuf, -1)
                    if not first:
                        pe.wait_ge(s.node_free, 1)
                        pe.sem_inc(s.node_free, -1)
                    o = bank[:, 2 + b, :]
                    last = nc.tensor.matmul(o[:, 0:out_s], Nv.hT[0:top, b, 0, :], wt[f"out_s{l}"][:], start=True, stop=True)
                    for i in range(3):
                        last = nc.tensor.matmul(o[:, out_s + V * i:out_s + V * (i + 1)], Nv.hT[0:vec, b, 1 + i, :], wt[f"out_v{l}"][:],
                                                start=True, stop=True)
                    if l in (1, 2):
                        last = nc.tensor.matmul(o[:, 160:161], Nv.hT[0:96, b, 0, :], wt[f"out_a{l}"][:], start=True, stop=True)
                    last.then_inc(s.node_mm, 1)
                pipelined(pe, SLOTS, [(0, turns), (1, products)])
                pe.wait_ge(s.node_free, 2)
                pe.sem_inc(s.node_free, -2)

            for l in (0, 1, 2):
                if l not in layers:
                    continue
                prep(l)
                barrier(pe, "pe")
                summing = (1, sums(l, E.sel, E.msg))
                pipelined(pe, GROUPS, [summing, (-2, edge_weights(l)), (-3, hidden(l))] if l else
                          [(-2, hidden(l)), summing, (-1, edge_weights(l))], unroll=2 * RUN_BANKS[l])
                pe.wait_ge(s.run_free, RUN_BANKS[l])
                pe.sem_inc(s.run_free, -RUN_BANKS[l])
                if l == 0:
                    pe.wait_ge(s.w_free, 2)
                    pe.sem_inc(s.w_free, -2)
                barrier(pe, "pe")
                post(l)
                barrier(pe, "pe")
            if 3 in layers:
                prep(3)
                barrier(pe, "pe")

                def edge_w3(g, b, first, half):
                    pe.wait_ge(s.attr_in0 if b == 0 else s.attr_in1, 16)
                    pe.sem_inc(s.attr_in0 if b == 0 else s.attr_in1, -16)
                    if not among_first(g, 1):
                        pe.wait_ge(s.w_free, 1)
                        pe.sem_inc(s.w_free, -1)
                    for t in range(2):
                        last = nc.tensor.matmul(bank[:, 0, t * 256:t * 256 + 224], T.rb[0:16, b, t * P:(t + 1) * P], wt["rbf"][:],
                                                start=True, stop=True)
                    last.then_inc(s.w_ready, 1)

                def turn3(f, b, at, signal):
                    for t in range(2):
                        nc.tensor.transpose(bank[0:96, at + t, 0:128], f[:, b, t, 0:96], ident[:])
                        nc.tensor.transpose(bank[:, at + t, 128:256], f[:, b, t, 96:224], ident[:])
                        last = nc.tensor.transpose(bank[:, at + t, 256:384], f[:, b, t, 224:352], ident[:])
                    last.then_inc(signal, 1)

                def turn_m1(g, b, first, half):
                    pe.wait_ge(s.m1_ready, 1)
                    pe.sem_inc(s.m1_ready, -1)
                    turn3(T.f, b, 1, s.m1_turned)

                def values(g, b, first, half):
                    pe.wait_ge(s.m1_in_sbuf, 1)
                    pe.sem_inc(s.m1_in_sbuf, -1)
                    for t in range(2):
                        o = bank[:, 6 + t, :]
                        nc.tensor.matmul(o[:, 0:160], T.t1[0:96, b, t, 0:128], wt["val_s"][:], start=True, stop=True)
                        nc.tensor.matmul(o[:, 160:288], T.t1[:, b, t, 128:256], wt["val_x"][:], start=True, stop=False)
                        last = nc.tensor.matmul(o[:, 160:288], T.t1[:, b, t, 256:384], wt["val_yz"][:], start=False, stop=True)
                    last.then_inc(s.values_mm, 1)

                def turn_m2(g, b, first, half):
                    pe.wait_ge(s.m2_ready, 1)
                    pe.sem_inc(s.m2_ready, -1)
                    turn3(T.f2, b, 4, s.m2_turned)

                def linear(g, b, first, half):
                    pe.wait_ge(s.m2_in_sbuf, 1)
                    pe.sem_inc(s.m2_in_sbuf, -1)
                    if not (isinstance(g, int) and g == 0):
                        pe.wait_ge(s.linear_free, 1)
                        pe.sem_inc(s.linear_free, -1)
                    for t in range(2):
                        o = bank[:, 3, t * 192:(t + 1) * 192]
                        nc.tensor.matmul(o[:, 0:64], T.t2[0:96, b, t, 0:128], wt["lin_s"][:], start=True, stop=True)
                        nc.tensor.matmul(o[:, 64:192], T.t2[:, b, t, 128:256], wt["lin_x"][:], start=True, stop=False)
                        last = nc.tensor.matmul(o[:, 64:192], T.t2[:, b, t, 256:384], wt["lin_yz"][:], start=False, stop=True)
                    last.then_inc(s.linear_mm, 1)
                pipelined(pe, TILES // 2, [(-1, turn_m1), (1, linear), (-1, values), (0, turn_m2), (-3, edge_w3)])
                pe.wait_ge(s.linear_free, 1)
                pe.sem_inc(s.linear_free, -1)
                pe.wait_ge(s.w_free, 1)
                pe.sem_inc(s.w_free, -1)
                barrier(pe, "pe")
                for k in range(QK):
                    if k >= 2:
                        pe.wait_ge(s.scan_free, 1)
                        pe.sem_inc(s.scan_free, -1)
                    for h in range(4):
                        last = nc.tensor.transpose(bank[0:QT, k % 2, h * P:(h + 1) * P], aux[:, k * QT:(k + 1) * QT, h], ident[:])
                    last.then_inc(s.scores_turned, 1)
                pe.wait_ge(s.scan_free, 2)
                pe.sem_inc(s.scan_free, -2)
                pe.wait_ge(s.scan_ready, 1)
                pe.sem_inc(s.scan_ready, -1)
                for e in range(2):
                    for k in range(QK):
                        last = nc.tensor.transpose(bank[0:4, 2 + 2 * e + k // 4, (k % 4) * QT:(k % 4 + 1) * QT], C.edge[0:QT, k, :, e],
                                                   ident[0:QT, 0:QT])
                last.then_inc(s.scan_turned, 1)
                pe.wait_ge(s.scan_ready, 1)
                pe.sem_inc(s.scan_ready, -1)
                for k in range(QK):
                    for e in range(2):
                        last = nc.tensor.transpose(bank[0:QT, 6, (2 * k + e) * 4:(2 * k + e) * 4 + 4], C.c[0:4, e, k * QT:(k + 1) * QT],
                                                   ident[0:4, 0:4])
                last.then_inc(s.scan_turned, 1)
                for k in range(QK):
                    pe.wait_ge(s.scan_ready, 1)
                    pe.sem_inc(s.scan_ready, -1)
                    if k >= 2:
                        pe.wait_ge(s.scan_free, 1)
                        pe.sem_inc(s.scan_free, -1)
                    for h in range(4):
                        last = nc.tensor.transpose(bank[:, k % 2, h * QT:(h + 1) * QT], C.fw[0:QT, k, h, :], ident[0:QT, 0:QT])
                    last.then_inc(s.scan_turned, 1)
                pe.wait_ge(s.scan_free, 2)
                pe.sem_inc(s.scan_free, -2)
                barrier(pe, "pe")
                pipelined(pe, GROUPS, [(1, sums(3, P2.sel, P2.msg))], unroll=2 * RUN_BANKS[3])
                pe.wait_ge(s.run_free, RUN_BANKS[3])
                pe.sem_inc(s.run_free, -RUN_BANKS[3])
                barrier(pe, "pe")
                post(3)
                barrier(pe, "pe")

        @block.vector
        def _(dve):
            V_ = nc.vector
            c = Steps()

            def tt(o, p, q, op):
                return V_.tensor_tensor(o, p, q, op)

            def bc(ap, axis, n):
                v = ap.unsqueeze(axis)
                shape = list(v.shape)
                shape[axis] = n
                return v.broadcast_to(shape)

            def inverse_root(v, width, eps, t, r):
                V_.tensor_scalar(v, v, 1.0 / width, eps, ALU.mult, ALU.add).then_inc(dve_own, c.step())
                dve.wait_ge(dve_own, c.n)
                dve.sem_inc(s.root_asked, 1)
                dve.wait_ge(s.root_done, 1)
                dve.sem_inc(s.root_done, -1)
                V_.reciprocal(r, t).then_inc(dve_own, c.step())
                dve.wait_ge(dve_own, c.n)
                tt(t, r, r, ALU.mult).then_inc(dve_own, c.step())
                dve.wait_ge(dve_own, c.n)
                tt(t, t, v, ALU.mult).then_inc(dve_own, c.step())
                dve.wait_ge(dve_own, c.n)
                V_.tensor_scalar(t, t, -0.5, 1.5, ALU.mult, ALU.add).then_inc(dve_own, c.step())
                dve.wait_ge(dve_own, c.n)
                tt(v, r, t, ALU.mult).then_inc(dve_own, c.step())
                dve.wait_ge(dve_own, c.n)

            V_.memset(wt["val_x"][:], 0.0).then_inc(dve_own, c.step())
            dve.wait_ge(dve_own, c.n)
            V_.memset(wt["lin_x"][:], 0.0).then_inc(dve_own, c.step())
            dve.wait_ge(dve_own, c.n)
            for l in range(4):
                V_.memset(wt[f"in_v{l}"][:], 0.0).then_inc(dve_own, c.step())
            V_.memset(wt["val_yz"][:], 0.0).then_inc(dve_own, c.step())
            dve.wait_ge(dve_own, c.n)
            V_.memset(wt["lin_yz"][:], 0.0).then_inc(dve_own, c.step())
            dve.wait_ge(dve_own, c.n)
            dve.sem_inc(s.blocks_zeroed, 1)
            dve.wait_ge(zero_made, 2)
            V_.tensor_copy(U.node, U.node_i).then_inc(dve_own, c.step())
            V_.tensor_copy(U.t, U.lk.bitcast(I32)).then_inc(dve_own, c.step())
            V_.tensor_copy(U.tc, U.cc.bitcast(I32)).then_inc(dve_own, c.step())
            V_.tensor_copy(U.prev[:, 0:QK], U.kc.bitcast(I32)).then_inc(dve_own, c.step())
            dve.wait_ge(dve_own, c.n)
            V_.tensor_copy(spare[:], U.prev[:, 0:1]).then_inc(dve_own, c.step())
            dve.wait_ge(dve_own, c.n)
            dve.wait_ge(loaded, LOADS)
            for name in ("src", "dst"):
                V_.tensor_copy(U.narrow[name][0:QT], U.wide[name][0:QT]).then_inc(dve_own, c.step())
            dve.wait_ge(dve_own, c.n)
            dve.sem_inc(s.keys_narrowed, 1)
            V_.tensor_copy(src_f[:], src_i[:]).then_inc(dve_own, c.step())
            V_.tensor_copy(dst_f[:], dst_i[:]).then_inc(dve_own, c.step())
            V_.tensor_copy(U.lk, U.lkI).then_inc(dve_own, c.step())
            V_.tensor_copy(U.nf, U.nfI).then_inc(dve_own, c.step())
            V_.tensor_copy(U.lkc[0:QT], U.lkc_i[0:QT]).then_inc(dve_own, c.step())
            V_.tensor_copy(U.nfc[0:QT], U.nfc_i[0:QT]).then_inc(dve_own, c.step())
            V_.tensor_copy(y[:, :, 0:4], U.e4.rearrange("p (t c) -> p t c", c=4)).then_inc(dve_own, c.step())
            V_.tensor_copy(y[:, :, 4:6], U.e4.rearrange("p (t c) -> p t c", c=4)[:, :, 1:3]).then_inc(dve_own, c.step())
            dve.wait_ge(dve_own, c.n)
            e3 = U.e3.rearrange("p (t i) -> p t i", i=3)
            tt(aux[:, :, 0:3], e3, e3, ALU.mult).then_inc(dve_own, c.step())
            dve.wait_ge(dve_own, c.n)
            V_.tensor_reduce(U.n2, aux[:, :, 0:3], AX, ALU.add).then_inc(dve_own, c.step())
            dve.wait_ge(dve_own, c.n)
            inverse_root(U.n2, 3.0, 0.0, U.j, U.one)
            tt(aux[:, :, 0:3], e3, bc(U.n2, 2, 3), ALU.mult).then_inc(dve_own, c.step())
            dve.wait_ge(dve_own, c.n)
            V_.tensor_copy(aux[:, :, 3:5], aux[:, :, 0:2]).then_inc(dve_own, c.step())
            dve.wait_ge(dve_own, c.n)
            V_.memset(U.one, 1.0).then_inc(dve_own, c.step())
            dve.wait_ge(dve_own, c.n)
            for j in range(SLOTS):
                V_.scalar_tensor_tensor(U.j, U.lk, U.node[:, j:j + 1], U.one, ALU.is_le, ALU.mult, accum_out=U.tiles[:, j:j + 1]).then_inc(dve_own, c.step())
                dve.wait_ge(dve_own, c.n)
            V_.tensor_copy(U.tile_i, U.tiles).then_inc(dve_own, c.step())
            dve.wait_ge(dve_own, c.n)
            dve.sem_inc(s.end_tile_ready, 1)
            for j in range(SLOTS):
                dve.wait_ge(keys_got[j % 2], 16 * (j // 2 + 1))
                V_.scalar_tensor_tensor(U.j[:, 0:P], U.rowI[:, j % 2, :], U.node[:, j:j + 1], U.one[:, 0:P], ALU.is_le, ALU.mult,
                                               accum_out=U.in_tile[:, j:j + 1]).then_inc(dve_own, c.step())
                dve.wait_ge(dve_own, c.n)
                dve.sem_inc(s.end_keys_free, 1)
            V_.scalar_tensor_tensor(U.end, U.tiles, float(P), U.in_tile, ALU.mult, ALU.add).then_inc(dve_own, c.step())
            dve.wait_ge(dve_own, c.n)
            dve.sem_inc(s.table_in, 1)
            V_.tensor_scalar(U.in_tile, U.end, -1.0, 0.0, ALU.add, ALU.max).then_inc(dve_own, c.step())
            dve.wait_ge(dve_own, c.n)
            V_.tensor_copy(last_i[:], U.in_tile).then_inc(dve_own, c.step())
            dve.wait_ge(dve_own, c.n)
            def second_keys(key, last, following, number):
                tt(key, last, following, ALU.is_equal).then_inc(dve_own, c.step())
                dve.wait_ge(dve_own, c.n)
                tt(U.j[0:last.shape[0], 0:last.shape[1]], last, number, ALU.subtract).then_inc(dve_own, c.step())
                dve.wait_ge(dve_own, c.n)
                tt(U.j[0:last.shape[0], 0:last.shape[1]], U.j[0:last.shape[0], 0:last.shape[1]], key, ALU.mult).then_inc(dve_own, c.step())
                dve.wait_ge(dve_own, c.n)
                return U.j[0:last.shape[0], 0:last.shape[1]]
            t_ = second_keys(U.one, U.lk, U.nf, U.t)
            tt(U.lk, t_, U.t, ALU.add).then_inc(dve_own, c.step())
            dve.wait_ge(dve_own, c.n)
            t_ = second_keys(U.cc[0:QT], U.lkc[0:QT], U.nfc[0:QT], U.tc[0:QT])
            tt(U.kc[0:QT], t_, U.tc[0:QT], ALU.add).then_inc(dve_own, c.step())
            dve.wait_ge(dve_own, c.n)
            for k in range(QK):
                V_.tensor_scalar(sel2[:, k, :], U.lk[0:QT, k * QT:(k + 1) * QT], U.kc[0:QT, k:k + 1], None, ALU.is_equal).then_inc(dve_own, c.step())
                dve.wait_ge(dve_own, c.n)
                V_.scalar_tensor_tensor(U.j[0:QT, 0:QT], U.lk[0:QT, k * QT:(k + 1) * QT], U.kc[0:QT, k:k + 1], lower[0:QT, 0:QT],
                                               ALU.is_equal, ALU.mult, accum_out=U.nfc[0:QT, k:k + 1]).then_inc(dve_own, c.step())
                dve.wait_ge(dve_own, c.n)
            V_.tensor_scalar(U.nfc[0:QT], U.nfc[0:QT], 1.0, None, ALU.is_lt).then_inc(dve_own, c.step())
            dve.wait_ge(dve_own, c.n)
            tt(U.cc[0:QT], U.cc[0:QT], U.nfc[0:QT], ALU.mult).then_inc(dve_own, c.step())
            dve.wait_ge(dve_own, c.n)
            tt(U.lkc[0:QT], U.lkc[0:QT], spare[0:QT, 0:1].broadcast_to([QT, QK]), ALU.subtract).then_inc(dve_own, c.step())
            dve.wait_ge(dve_own, c.n)
            tt(U.lkc[0:QT], U.lkc[0:QT], U.cc[0:QT], ALU.mult).then_inc(dve_own, c.step())
            dve.wait_ge(dve_own, c.n)
            tt(U.lkc[0:QT], U.lkc[0:QT], spare[0:QT, 0:1].broadcast_to([QT, QK]), ALU.add).then_inc(dve_own, c.step())
            dve.wait_ge(dve_own, c.n)
            V_.tensor_copy(put2_i[:], U.lkc[0:QT]).then_inc(dve_own, c.step())
            dve.wait_ge(dve_own, c.n)
            dve.wait_ge(moved, 80)
            tt(U.in_tile, U.end, U.prev, ALU.subtract).then_inc(dve_own, c.step())
            dve.wait_ge(dve_own, c.n)
            V_.tensor_scalar(has[:], U.in_tile, 1.0, None, ALU.min).then_inc(dve_own, c.step())
            dve.wait_ge(dve_own, c.n)
            V_.tensor_scalar(rcnt[:], U.in_tile, 1.0, None, ALU.max).then_inc(dve_own, c.step())
            dve.wait_ge(dve_own, c.n)
            V_.reciprocal(rcnt[:], rcnt[:]).then_inc(dve_own, c.step())
            dve.wait_ge(dve_own, c.n)
            dve.wait_ge(s.weights_whole, 1)
            dve.sem_inc(s.weights_whole, -1)

            def scale(name, by, c0=0, c1=None):
                w = wt[name]
                V_.tensor_scalar(w[:, c0:c1 or w.shape[1]], w[:, c0:c1 or w.shape[1]], by, None, ALU.mult).then_inc(dve_own, c.step())
                dve.wait_ge(dve_own, c.n)
            r3, r2 = 3 ** -0.5, 2 ** -0.5
            scale("fc2_0", r3, 160, 192)
            scale("fc2_0", r2, 192, 224)
            for l in (1, 2):
                scale(f"fc2_{l}", 0.125)
                scale(f"fc2_{l}", r3, 160, 192)
                scale(f"in_s{l}", 0.125)
                scale(f"in_v{l}", 32 ** -0.5)
                down = 96 ** -0.5 * (10 ** -0.5 if l == 1 else 1.0)
                for w in ("out_s", "out_v"):
                    scale(f"{w}{l}", down)
                scale(f"out_a{l}", down * (0.1 if l == 1 else 1.0))
            scale("rbf", r3, 160, 192)
            scale("rbf", r2, 192, 224)
            for at, rows, col, by in ((64, 32, 0, r3), (96, 32, 1, r2), (32, 32, 2, r2), (96, 32, 2, r2)):
                V_.tensor_scalar(w2[at:at + rows, col:col + 1], w2[at:at + rows, col:col + 1], by, None, ALU.mult).then_inc(dve_own, c.step())
                dve.wait_ge(dve_own, c.n)
            V_.tensor_scalar(wt["lin_s"][:], wt["lin_s"][:], w2[0:96, 0:1], None, ALU.mult).then_inc(dve_own, c.step())
            dve.wait_ge(dve_own, c.n)
            V_.tensor_scalar(wt["lin_x"][:], wt["lin_x"][:], w2[:, 1:2], None, ALU.mult).then_inc(dve_own, c.step())
            dve.wait_ge(dve_own, c.n)
            V_.tensor_scalar(wt["lin_yz"][:], wt["lin_yz"][:], w2[:, 2:3], None, ALU.mult).then_inc(dve_own, c.step())
            dve.wait_ge(dve_own, c.n)
            dve.wait_ge(dve_own, c.n)
            dve.sem_inc(dve_own, c.reset())
            barrier(dve, "dve")

            big = Nv.big.rearrange("p (j c) -> p j c", c=DIM)

            def mean_var(src, width, mean, rstd, eps, scratch):
                V_.tensor_reduce(stats[:, mean, :], src, AX, ALU.add).then_inc(dve_own, c.step())
                dve.wait_ge(dve_own, c.n)
                V_.tensor_scalar(stats[:, mean, :], stats[:, mean, :], 1.0 / width, None, ALU.mult).then_inc(dve_own, c.step())
                dve.wait_ge(dve_own, c.n)
                tt(scratch, src, bc(stats[:, mean, :], 2, width), ALU.subtract).then_inc(dve_own, c.step())
                dve.wait_ge(dve_own, c.n)
                tt(scratch, scratch, scratch, ALU.mult).then_inc(dve_own, c.step())
                dve.wait_ge(dve_own, c.n)
                V_.tensor_reduce(stats[:, rstd, :], scratch, AX, ALU.add).then_inc(dve_own, c.step())
                dve.wait_ge(dve_own, c.n)
                inverse_root(stats[:, rstd, :], width, eps, stats[:, 8, :], stats[:, 9, :])

            def prep(l):
                mean_var(x[:], DIM, 1, 0, 1e-5, big)
                tt(stats[:, 1, :], stats[:, 1, :], stats[:, 0, :], ALU.mult).then_inc(dve_own, c.step())
                dve.wait_ge(dve_own, c.n)
                V_.tensor_scalar(stats[:, 1, :], stats[:, 1, :], -1.0, None, ALU.mult).then_inc(dve_own, c.step())
                dve.wait_ge(dve_own, c.n)
                if l == 3:
                    tt(big, x[:], bc(stats[:, 0, :], 2, DIM), ALU.mult).then_inc(dve_own, c.step())
                    dve.wait_ge(dve_own, c.n)
                    tt(big, big, bc(stats[:, 1, :], 2, DIM), ALU.add).then_inc(dve_own, c.step())
                    dve.wait_ge(dve_own, c.n)
                    V_.tensor_scalar(big, big, 0.0, None, ALU.max).then_inc(dve_own, c.step())
                    dve.wait_ge(dve_own, c.n)
                    tt(x[:], x[:], big, ALU.add).then_inc(dve_own, c.step())
                    dve.wait_ge(dve_own, c.n)
                    normed = fore[:, 0:SLOTS * DIM].rearrange("p (j c) -> p j c", c=DIM)
                    hs = big[:, :, 0:S]
                    mean_var(hs, S, 3, 2, 1e-5, normed[:, :, 0:S])
                    tt(normed[:, :, 0:S], hs, bc(stats[:, 3, :], 2, S), ALU.subtract).then_inc(dve_own, c.step())
                    dve.wait_ge(dve_own, c.n)
                    tt(normed[:, :, 0:S], normed[:, :, 0:S], bc(stats[:, 2, :], 2, S), ALU.mult).then_inc(dve_own, c.step())
                    dve.wait_ge(dve_own, c.n)
                    hv = big[:, :, S:DIM]
                    nv = normed[:, :, S:DIM]
                    tt(nv, hv, hv, ALU.mult).then_inc(dve_own, c.step())
                    dve.wait_ge(dve_own, c.n)
                    V_.tensor_reduce(stats[:, 4, :], nv, AX, ALU.add).then_inc(dve_own, c.step())
                    dve.wait_ge(dve_own, c.n)
                    inverse_root(stats[:, 4, :], V, 1e-5, stats[:, 8, :], stats[:, 9, :])
                    for i in range(3):
                        tt(nv[:, :, V * i:V * (i + 1)], hv[:, :, i:3 * V:3], bc(stats[:, 4, :], 2, V), ALU.mult).then_inc(dve_own, c.step())
                        dve.wait_ge(dve_own, c.n)
                dve.wait_ge(dve_own, c.n)
                dve.sem_inc(dve_own, c.reset())
                dve.sem_inc(s.node_in, SLOTS)
                width = SPEC[l]["table"]
                ks = SPEC[l]["skip"]
                def stage(j, b, first, half):
                    dve.wait_ge(s.node_mm, 1)
                    dve.sem_inc(s.node_mm, -1)
                    o = bank[:, 2 + b, :]
                    row = fore[:, bass.ds(j * width, width)]
                    k0 = skip[:, bass.ds(j, 1), 0:ks].rearrange("p o c -> p (o c)")
                    for to, c0, c1 in ((row[:, 0:S], 0, 64), (row[:, S:DIM], 160, 256), (k0[:, 0:ks - 96], 64, 64 + ks - 96),
                                       (k0[:, ks - 96:ks], 256, 352)):
                        if l in (1, 2):
                            V_.tensor_scalar(to, o[:, c0:c1], attr[:, bass.ds(j, 1)], None, ALU.mult).then_inc(dve_own, c.step())
                        else:
                            V_.tensor_copy(to, o[:, c0:c1]).then_inc(dve_own, c.step())
                    if l == 0:
                        V_.tensor_copy(row[:, DIM:224], o[:, 160:224]).then_inc(dve_own, c.step())
                    dve.wait_ge(dve_own, c.n)
                    dve.sem_inc(dve_own, c.reset())
                    dve.sem_inc(s.node_free, 1)
                pipelined(dve, SLOTS, [(0, stage)])
                dve.sem_inc(s.table_in, 1)

            def select(g, b, keys, sel, scalar):
                for t in range(GROUP):
                    V_.tensor_scalar(sel[:, b, t, :], keys[:, b, t * P:(t + 1) * P],
                                       scalar[:, bass.ds(g * GROUP + t, 1)], None, ALU.is_equal).then_inc(dve_own, c.step())

            def edges(l):
                def stage(g, part, first, half):
                    f = SPEC[l]["f"]
                    b = part % 2
                    if l == 0:
                        dve.wait_ge(s.w_ready, 1)
                        dve.sem_inc(s.w_ready, -1)
                        dve.sem_inc(s.hid_free, 1)
                    dve.wait_ge(s.key_in0 if b == 0 else s.key_in1, 16)
                    dve.sem_inc(s.key_in0 if b == 0 else s.key_in1, -16)
                    if not first:
                        dve.wait_ge(s.msg_free, 1)
                        dve.sem_inc(s.msg_free, -1)
                    select(g, b, E.keys, E.sel, src_f if l == 0 else dst_f)
                    if l == 0:
                        for t in range(GROUP):
                            V_.scalar_tensor_tensor(E.first[:, t, :], E.keys[:, b, t * P:(t + 1) * P], src_f[:, bass.ds(g * GROUP + t, 1)],
                                                    lower[:], ALU.is_equal, ALU.mult, accum_out=E.cnt[:, t:t + 1]).then_inc(dve_own, c.step())
                    dve.wait_ge(got[l][part], (half + 1) * (16 * GROUP))
                    if l:
                        dve.wait_ge(s.weights_scaled, 1)
                        dve.sem_inc(s.weights_scaled, -1)
                    w = E.w[:, b] if l else wmm(b)
                    width = SPEC[l]["table"]
                    rows = E.got[:, part, 0:GROUP * width].rearrange("p (t c) -> p t c", c=width)
                    xs = rows[:, :, 0:S]
                    msg = E.msg[:, b, 0:GROUP * f].rearrange("p (t c) -> p t c", c=f)
                    vec = SPEC[l]["vec"]
                    blocks = msg[:, :, 96:96 + 3 * vec].rearrange("p t (i c) -> p t i c", c=vec)
                    t0 = E.t0[:, 0:GROUP * S].rearrange("p (t c) -> p t c", c=S)
                    t1 = E.t1.rearrange("p (t i c) -> p t i c", i=3, c=V)
                    t2 = E.t2.rearrange("p (t i c) -> p t i c", i=3, c=V)

                    def wv(c0):
                        return bc(w[:, :, c0:c0 + V], 2, 3)
                    if l == 0:
                        xv = rows[:, :, S:224].rearrange("p t (i c) -> p t i c", c=V)
                        sh = aux[:, bass.ds(g * GROUP, GROUP), :]
                        keys4 = src_f[:, bass.ds(g * GROUP, GROUP)]
                        u1, u2 = E.u1, E.u2
                        counted = c.n
                        tt(t0, w[:, :, 64:128], xs, ALU.mult).then_inc(dve_own, c.step())
                        tt(t1, xv[:, :, 0:3, :], bc(sh[:, :, 0:3], 3, V), ALU.mult).then_inc(dve_own, c.step())
                        tt(u1, xv[:, :, 1:4, :], bc(sh[:, :, 2:5], 3, V), ALU.mult).then_inc(dve_own, c.step())
                        tt(u2, xv[:, :, 2:5, :], bc(sh[:, :, 1:4], 3, V), ALU.mult).then_inc(dve_own, c.step())
                        dve.wait_ge(dve_own, counted + 1)
                        V_.tensor_scalar(E.cnt, E.cnt, 1.0, None, ALU.is_lt).then_inc(dve_own, c.step())
                        tt(blocks[:, :, :, 0:S], bc(t0, 2, 3), bc(sh[:, :, 0:3], 3, S), ALU.mult).then_inc(dve_own, c.step())
                        dve.wait_ge(dve_own, counted + 5)
                        V_.scalar_tensor_tensor(E.pos, keys4, spare[:], E.cnt, ALU.subtract, ALU.mult).then_inc(dve_own, c.step())
                        tt(t2[:, :, 0, :], t1[:, :, 0, :], t1[:, :, 1, :], ALU.add).then_inc(dve_own, c.step())
                        tt(u1, u1, u2, ALU.subtract).then_inc(dve_own, c.step())
                        dve.wait_ge(dve_own, counted + 7)
                        V_.tensor_scalar(put_i[:, bass.ds(g * GROUP, GROUP)], E.pos, spare[:], None, ALU.add).then_inc(dve_own, c.step())
                        dve.wait_ge(dve_own, counted + 8)
                        tt(t2[:, :, 0, :], t2[:, :, 0, :], t1[:, :, 2, :], ALU.add).then_inc(dve_own, c.step())
                        tt(msg[:, :, 0:S], w[:, :, 0:64], xs, ALU.mult).then_inc(dve_own, c.step())
                        dve.wait_ge(dve_own, counted + 9)
                        tt(blocks[:, :, :, 96:128], u1, wv(192), ALU.mult).then_inc(dve_own, c.step())
                        dve.wait_ge(dve_own, counted + 11)
                        tt(msg[:, :, S:96], t2[:, :, 0, :], w[:, :, 160:192], ALU.mult).then_inc(dve_own, c.step())
                        tt(blocks[:, :, :, S:96], wv(128), xv[:, :, 0:3, :], ALU.mult).then_inc(dve_own, c.step())
                    else:
                        yy = y[:, bass.ds(g * GROUP, GROUP), :]
                        xv = rows[:, :, S:DIM].rearrange("p t (i c) -> p t i c", c=V)
                        wb = t0
                        tt(t1, xv, bc(yy[:, :, 1:4], 3, V), ALU.mult).then_inc(dve_own, c.step())
                        parts = c.n
                        tt(wb, w[:, :, 96:160], xs, ALU.mult).then_inc(dve_own, c.step())
                        dve.wait_ge(dve_own, parts)
                        tt(t2[:, :, 0, :], t1[:, :, 0, :], t1[:, :, 1, :], ALU.add).then_inc(dve_own, c.step())
                        dve.wait_ge(dve_own, parts + 1)
                        tt(blocks[:, :, :, 0:S], bc(wb, 2, 3), bc(yy[:, :, 1:4], 3, S), ALU.mult).then_inc(dve_own, c.step())
                        dve.wait_ge(dve_own, parts + 2)
                        tt(t2[:, :, 0, :], t2[:, :, 0, :], t1[:, :, 2, :], ALU.add).then_inc(dve_own, c.step())
                        dot = c.n
                        tt(msg[:, :, 0:S], w[:, :, 0:S], xs, ALU.mult).then_inc(dve_own, c.step())
                        tt(blocks[:, :, :, S:96], bc(w[:, :, S:96], 2, 3), xv, ALU.mult).then_inc(dve_own, c.step())
                        dve.wait_ge(dve_own, dot)
                        tt(msg[:, :, S:96], t2[:, :, 0, :], w[:, :, 160:192], ALU.mult).then_inc(dve_own, c.step())
                    dve.wait_ge(dve_own, c.n)
                    dve.sem_inc(dve_own, c.reset())
                    dve.sem_inc(s.msg_ready, 1)
                    dve.sem_inc(s.w_free, 1)
                    dve.sem_inc(s.got_free, 1)
                    dve.sem_inc(s.key_free, 1)
                pipelined(dve, GROUPS, [(0, stage)], unroll=DEPTH)
                dve.wait_ge(s.msg_free, 2)
                dve.sem_inc(s.msg_free, -2)

            def post(l):
                f = SPEC[l]["f"]
                out_w = {0: 192, 1: 161, 2: 161, 3: 160}[l]
                conv = fore[:, 0:SLOTS * out_w].rearrange("p (j c) -> p j c", c=out_w)

                def sums(j, b, first, half):
                    dve.wait_ge(s.carry_in0 if b == 0 else s.carry_in1, 16 * (1 if l else CHAINS))
                    dve.sem_inc(s.carry_in0 if b == 0 else s.carry_in1, -(16 * (1 if l else CHAINS)))
                    car = Nv.car[:, b, :]
                    o = Nv.sum[:, b, 0:f]
                    if l:
                        dve.wait_ge(rows_got[l][b], (half + 1) * 16)
                        V_.scalar_tensor_tensor(o, Nv.row[:, b, 0:f], has[:, bass.ds(j, 1)], car[:, 0:f], ALU.mult, ALU.add).then_inc(dve_own, c.step())
                        dve.wait_ge(dve_own, c.n)
                    else:
                        tt(o, car[:, 0:f], car[:, f:2 * f], ALU.add).then_inc(dve_own, c.step())
                        tt(car[:, 2 * f:3 * f], car[:, 2 * f:3 * f], car[:, 3 * f:4 * f], ALU.add).then_inc(dve_own, c.step())
                        dve.wait_ge(dve_own, c.n)
                        tt(o, o, car[:, 2 * f:3 * f], ALU.add).then_inc(dve_own, c.step())
                        dve.wait_ge(dve_own, c.n)
                    if l == 3:
                        V_.tensor_scalar(Nv.rden[:, 0:4], o[:, 160:164], 1e-16, None, ALU.add).then_inc(dve_own, c.step())
                        dve.wait_ge(dve_own, c.n)
                        V_.reciprocal(Nv.rden[:, 0:4], Nv.rden[:, 0:4]).then_inc(dve_own, c.step())
                        dve.wait_ge(dve_own, c.n)
                        hs = o[:, 0:64].rearrange("p (h c) -> p h c", h=4)
                        hv = o[:, 64:160].rearrange("p (i h c) -> p i h c", i=3, h=4)
                        tt(hs, hs, bc(Nv.rden[:, 0:4], 2, 16), ALU.mult).then_inc(dve_own, c.step())
                        tt(hv, hv, bc(bc(Nv.rden[:, 0:4], 1, 3), 3, 8), ALU.mult).then_inc(dve_own, c.step())
                    dve.wait_ge(dve_own, c.n)
                    dve.sem_inc(dve_own, c.reset())
                    dve.sem_inc(s.sum_ready, 1)
                    dve.sem_inc(s.sum_free, 1)
                    if l:
                        dve.sem_inc(s.got_free, 1)

                def products(j, b, first, half):
                    dve.wait_ge(s.node_mm, 1)
                    dve.sem_inc(s.node_mm, -1)
                    o = bank[:, 2 + b, 0:out_w]
                    to = fore[:, bass.ds(j * out_w, out_w)]
                    if l == 1:
                        V_.tensor_scalar(to, o, attr[:, bass.ds(j, 1)], None, ALU.mult).then_inc(dve_own, c.step())
                    elif l == 2:
                        V_.tensor_scalar(to, o, attr[:, bass.ds(j, 1)], rcnt[:, bass.ds(j, 1)], ALU.mult, ALU.mult).then_inc(dve_own, c.step())
                    else:
                        V_.tensor_copy(to, o).then_inc(dve_own, c.step())
                    dve.wait_ge(dve_own, c.n)
                    dve.sem_inc(dve_own, c.reset())
                    dve.sem_inc(s.node_free, 1)
                pipelined(dve, SLOTS, [(2, products), (0, sums)])

                def add_to_x(res):
                    tt(x[:, :, 0:S], x[:, :, 0:S], res[:, :, 0:S], ALU.add).then_inc(dve_own, c.step())
                    for i in range(3):
                        tt(x[:, :, S + i:DIM:3], x[:, :, S + i:DIM:3], res[:, :, S + V * i:S + V * (i + 1)], ALU.add).then_inc(dve_own, c.step())
                    dve.wait_ge(dve_own, c.n)
                if l == 0:
                    V_.scalar_tensor_tensor(conv, conv, 1.0 / 32.0, skip[:], ALU.mult, ALU.add).then_inc(dve_own, c.step())
                    dve.wait_ge(dve_own, c.n)
                    dve.wait_ge(dve_own, c.n)
                    dve.sem_inc(dve_own, c.reset())
                    dve.sem_inc(s.function_asked, 1)
                    dve.wait_ge(s.function_done, 1)
                    dve.sem_inc(s.function_done, -1)
                    tt(big[:, :, 0:S], conv[:, :, 0:S], skip[:, :, 0:S], ALU.mult).then_inc(dve_own, c.step())
                    for i in range(3):
                        tt(big[:, :, S + V * i:S + V * (i + 1)], conv[:, :, 96 + V * i:128 + V * i], skip[:, :, S:96], ALU.mult).then_inc(dve_own, c.step())
                    dve.wait_ge(dve_own, c.n)
                    add_to_x(big)
                elif l == 1:
                    turns = Nv.small
                    V_.tensor_scalar(turns[:, 0, :], conv[:, :, 160], 1.0 / (2 * math.pi), None, ALU.mult).then_inc(dve_own, c.step())
                    dve.wait_ge(dve_own, c.n)
                    V_.tensor_copy(Nv.smi, turns[:, 0, :]).then_inc(dve_own, c.step())
                    dve.wait_ge(dve_own, c.n)
                    V_.tensor_copy(turns[:, 1, :], Nv.smi).then_inc(dve_own, c.step())
                    dve.wait_ge(dve_own, c.n)
                    tt(turns[:, 2, :], turns[:, 0, :], turns[:, 1, :], ALU.subtract).then_inc(dve_own, c.step())
                    dve.wait_ge(dve_own, c.n)
                    V_.tensor_scalar(turns[:, 3, :], turns[:, 2, :], 0.25, None, ALU.add).then_inc(dve_own, c.step())
                    dve.wait_ge(dve_own, c.n)
                    for _ in range(2):
                        V_.tensor_scalar(turns[:, 6:8, :], turns[:, 2:4, :], 0.5, None, ALU.is_gt).then_inc(dve_own, c.step())
                        dve.wait_ge(dve_own, c.n)
                        tt(turns[:, 2:4, :], turns[:, 2:4, :], turns[:, 6:8, :], ALU.subtract).then_inc(dve_own, c.step())
                        dve.wait_ge(dve_own, c.n)
                        V_.tensor_scalar(turns[:, 6:8, :], turns[:, 2:4, :], -0.5, None, ALU.is_lt).then_inc(dve_own, c.step())
                        dve.wait_ge(dve_own, c.n)
                        tt(turns[:, 2:4, :], turns[:, 2:4, :], turns[:, 6:8, :], ALU.add).then_inc(dve_own, c.step())
                        dve.wait_ge(dve_own, c.n)
                    dve.wait_ge(dve_own, c.n)
                    dve.sem_inc(dve_own, c.reset())
                    dve.sem_inc(s.function_asked, 1)
                    dve.wait_ge(s.function_done, 1)
                    dve.sem_inc(s.function_done, -1)
                    tt(big, skip[:, :, 0:DIM], bc(turns[:, 5, :], 2, DIM), ALU.mult).then_inc(dve_own, c.step())
                    tt(conv[:, :, 0:DIM], conv[:, :, 0:DIM], bc(turns[:, 4, :], 2, DIM), ALU.mult).then_inc(dve_own, c.step())
                    dve.wait_ge(dve_own, c.n)
                    tt(big, big, conv[:, :, 0:DIM], ALU.add).then_inc(dve_own, c.step())
                    dve.wait_ge(dve_own, c.n)
                    add_to_x(big)
                elif l == 2:
                    tt(big, conv[:, :, 0:DIM], conv[:, :, 160:161].broadcast_to([P, SLOTS, DIM]), ALU.mult).then_inc(dve_own, c.step())
                    dve.wait_ge(dve_own, c.n)
                    tt(big, big, skip[:, :, 0:DIM], ALU.add).then_inc(dve_own, c.step())
                    dve.wait_ge(dve_own, c.n)
                    add_to_x(big)
                else:
                    add_to_x(conv)
                dve.wait_ge(dve_own, c.n)
                dve.sem_inc(dve_own, c.reset())

            for l in (0, 1, 2):
                if l not in layers:
                    continue
                prep(l)
                barrier(dve, "dve")
                edges(l)
                barrier(dve, "dve")
                post(l)
                barrier(dve, "dve")

            if 3 in layers:
                prep(3)
                barrier(dve, "dve")

                def planes(ap):
                    return ap.rearrange("p t (i c) -> p t i c", i=3)

                q, u1, u2 = planes(T.q), planes(T.u1), planes(T.u2)

                def cross_parts(v, ys):
                    tt(u1[:, :, 0:2, :], v[:, :, 1:3, :], bc(ys[:, :, 2:4], 3, V), ALU.mult).then_inc(dve_own, c.step())
                    tt(u1[:, :, 2:3, :], v[:, :, 0:1, :], bc(ys[:, :, 4:5], 3, V), ALU.mult).then_inc(dve_own, c.step())
                    tt(u2[:, :, 0:1, :], v[:, :, 2:3, :], bc(ys[:, :, 1:2], 3, V), ALU.mult).then_inc(dve_own, c.step())
                    tt(u2[:, :, 1:3, :], v[:, :, 0:2, :], bc(ys[:, :, 2:4], 3, V), ALU.mult).then_inc(dve_own, c.step())
                    dve.wait_ge(dve_own, c.n - 1)

                def m1(g, part, first, half):
                    b = part % 2
                    ys = y[:, bass.ds(g * 2, 2), 1:6]
                    m, d = T.m[:, b], T.dot
                    w = T.w[:, b]
                    f = T.f[:, b]
                    vsl = f[:, :, 160:352].rearrange("p t (i c) -> p t i c", c=64)
                    mv = planes(m[:, :, S:DIM])
                    dve.wait_ge(s.m_ready, 1)
                    dve.sem_inc(s.m_ready, -1)
                    dve.wait_ge(s.weights_scaled, 1)
                    dve.sem_inc(s.weights_scaled, -1)
                    tt(q, mv, bc(ys[:, :, 0:3], 3, V), ALU.mult).then_inc(dve_own, c.step())
                    cross_parts(mv, ys)
                    tt(d, q[:, :, 0, :], q[:, :, 1, :], ALU.add).then_inc(dve_own, c.step())
                    half_dot = c.n
                    tt(f[:, :, 0:64], m[:, :, 0:S], w[:, :, 0:64], ALU.mult).then_inc(dve_own, c.step())
                    dve.wait_ge(dve_own, half_dot)
                    tt(d, d, q[:, :, 2, :], ALU.add).then_inc(dve_own, c.step())
                    tt(u1, u1, u2, ALU.subtract).then_inc(dve_own, c.step())
                    crossed = c.n
                    tt(f[:, :, 96:160], m[:, :, 0:S], w[:, :, 96:160], ALU.mult).then_inc(dve_own, c.step())
                    tt(vsl[:, :, :, 0:V], mv, bc(w[:, :, 64:96], 2, 3), ALU.mult).then_inc(dve_own, c.step())
                    dve.wait_ge(dve_own, crossed)
                    tt(f[:, :, 64:96], d, w[:, :, 160:192], ALU.mult).then_inc(dve_own, c.step())
                    tt(vsl[:, :, :, V:64], u1, bc(w[:, :, 192:224], 2, 3), ALU.mult).then_inc(dve_own, c.step())
                    dve.wait_ge(dve_own, c.n)
                    dve.sem_inc(dve_own, c.reset())
                    dve.sem_inc(s.m1_ready, 1)
                    dve.sem_inc(s.got_free, 1)

                def m2(g, part, first, half):
                    b = part % 2
                    dve.wait_ge(s.values_ready, 1)
                    dve.sem_inc(s.values_ready, -1)
                    yy = y[:, bass.ds(g * 2, 2), :]
                    ys = yy[:, :, 1:6]
                    f, cv = T.f2[:, b], T.cv[:, b]
                    vsl = f[:, :, 160:352].rearrange("p t (i c) -> p t i c", c=64)
                    tt(vv, bc(cv[:, :, 64:96], 2, 3), bc(ys[:, :, 0:3], 3, V), ALU.mult).then_inc(dve_own, c.step())
                    V_.scalar_tensor_tensor(T.al2, cv[:, :, 0:64], 0.2, cv[:, :, 0:64], ALU.mult, ALU.max).then_inc(dve_own, c.step())
                    dve.wait_ge(dve_own, c.n - 1)
                    tt(vv, vv, planes(cv[:, :, 96:192]), ALU.add).then_inc(dve_own, c.step())
                    dve.wait_ge(dve_own, c.n - 1)
                    tt(T.al2, T.al2, bc(alpha_dot[:], 1, 2), ALU.mult).then_inc(dve_own, c.step())
                    dve.wait_ge(dve_own, c.n - 1)
                    tt(vv, vv, bc(f[:, :, 64:96], 2, 3), ALU.mult).then_inc(dve_own, c.step())
                    dve.wait_ge(dve_own, c.n - 1)
                    V_.tensor_reduce(aux[:, bass.ds(g * 2, 2), 0:4], T.al2.rearrange("p t (h c) -> p t h c", h=4), AX,
                                     ALU.add).then_inc(dve_own, c.step())
                    dve.wait_ge(dve_own, c.n - 1)
                    tt(q, vv, bc(ys[:, :, 0:3], 3, V), ALU.mult).then_inc(dve_own, c.step())
                    cross_parts(vv, ys)
                    tt(f[:, :, 64:96], q[:, :, 0, :], q[:, :, 1, :], ALU.add).then_inc(dve_own, c.step())
                    tt(vsl[:, :, :, 0:V], vv, y0_planes(yy), ALU.mult).then_inc(dve_own, c.step())
                    dve.wait_ge(dve_own, c.n - 1)
                    tt(f[:, :, 64:96], f[:, :, 64:96], q[:, :, 2, :], ALU.add).then_inc(dve_own, c.step())
                    tt(vsl[:, :, :, V:64], u1, u2, ALU.subtract).then_inc(dve_own, c.step())
                    dve.wait_ge(dve_own, c.n)
                    dve.sem_inc(dve_own, c.reset())
                    dve.sem_inc(s.m2_ready, 1)

                vv = T.vv

                def y0_planes(yy):
                    return bc(yy[:, :, 0:1].broadcast_to([P, 2, 3]), 3, V)

                def edge_out(g, part, first, half):
                    b = part % 2
                    dve.wait_ge(s.scalars_out, 1)
                    dve.sem_inc(s.scalars_out, -1)
                    ys = y[:, bass.ds(g * 2, 2), 1:4]
                    c2 = bank[:, 3, 0:384].rearrange("p (t c) -> p t c", t=2)
                    hv = planes(T.h[:, b, :, S:DIM])
                    tt(q, bc(c2[:, :, 64:96], 2, 3), bc(ys, 3, V), ALU.mult).then_inc(dve_own, c.step())
                    dve.wait_ge(dve_own, c.n)
                    tt(hv, q, c2[:, :, 96:192].rearrange("p t (i c) -> p t i c", i=3), ALU.add).then_inc(dve_own, c.step())
                    dve.wait_ge(dve_own, c.n)
                    dve.sem_inc(dve_own, c.reset())
                    dve.sem_inc(s.linear_free, 1)
                    dve.sem_inc(s.h_ready, 1)
                pipelined(dve, TILES // 2, [(-1, m1), (2, edge_out), (0, m2)], unroll=DEPTH)
                barrier(dve, "dve")

                dve.wait_ge(s.key_in0, 48)
                dve.sem_inc(s.key_in0, -48)
                V_.tensor_copy(C.k[0:QT], C.kI[0:QT]).then_inc(dve_own, c.step())
                V_.tensor_copy(C.lk, C.lkI).then_inc(dve_own, c.step())
                V_.tensor_copy(C.fk, C.fkI).then_inc(dve_own, c.step())
                dve.wait_ge(dve_own, c.n)

                def same(o, p_, q_):
                    tt(o, p_, q_, ALU.is_equal).then_inc(dve_own, c.step())
                    dve.wait_ge(dve_own, c.n)
                    V_.tensor_scalar(o, o, -1.0, BIG, ALU.add, ALU.mult).then_inc(dve_own, c.step())
                    dve.wait_ge(dve_own, c.n)

                V_.memset(C.b, -BIG).then_inc(dve_own, c.step())
                dve.wait_ge(dve_own, c.n)
                V_.memset(C.b2, -BIG).then_inc(dve_own, c.step())
                dve.wait_ge(dve_own, c.n)
                for k in range(QK):
                    kk = C.k[0:QT, k, :]
                    same(C.b[0:QT, 1:P], kk[:, 1:P], kk[:, 0:P - 1])
                    V_.tensor_copy(C.b2[0:QT, 0:P - 1], C.b[0:QT, 1:P]).then_inc(dve_own, c.step())
                    dve.wait_ge(dve_own, c.n)
                    dve.wait_ge(s.scores_in_sbuf, 1)
                    dve.sem_inc(s.scores_in_sbuf, -1)
                    dve.sem_inc(s.scan_free, 1)
                    for h in range(4):
                        fw, bw, at = C.fw[0:QT, k, h, :], C.bw[0:QT, h, :], C.aT[0:QT, k, h, :]
                        V_.tensor_tensor_scan(fw, C.b[0:QT], at, 0.0, ALU.add, ALU.max).then_inc(dve_own, c.step())
                        V_.tensor_tensor_scan(bw[:, ::-1], C.b2[0:QT, ::-1], at[:, ::-1], 0.0, ALU.add, ALU.max).then_inc(dve_own, c.step())
                    dve.wait_ge(dve_own, c.n)
                    V_.tensor_copy(C.edge[0:QT, k, :, 0], C.fw[0:QT, k, :, P - 1]).then_inc(dve_own, c.step())
                    V_.tensor_copy(C.edge[0:QT, k, :, 1], C.bw[0:QT, :, 0]).then_inc(dve_own, c.step())
                    dve.wait_ge(dve_own, c.n)
                    tt(C.fw[0:QT, k], C.fw[0:QT, k], C.bw[0:QT], ALU.max).then_inc(dve_own, c.step())
                    dve.wait_ge(dve_own, c.n)
                dve.sem_inc(s.scan_ready, 1)
                dve.wait_ge(s.scan_turned, 1)
                dve.sem_inc(s.scan_turned, -1)
                for e in range(2):
                    V_.tensor_copy(C.m[0:4, e, 0:4 * QT], bank[0:4, 2 + 2 * e, 0:4 * QT]).then_inc(dve_own, c.step())
                    V_.tensor_copy(C.m[0:4, e, 4 * QT:TILES], bank[0:4, 3 + 2 * e, 0:3 * QT]).then_inc(dve_own, c.step())
                V_.memset(C.j[0:4], -BIG).then_inc(dve_own, c.step())
                dve.wait_ge(dve_own, c.n)
                V_.memset(C.c[0:4], -BIG).then_inc(dve_own, c.step())
                dve.wait_ge(dve_own, c.n)
                lk, fk = C.lk[0:4], C.fk[0:4]
                same(C.j[0:4, 0, 1:TILES], lk[:, 1:TILES], lk[:, 0:TILES - 1])
                same(C.j[0:4, 1, 0:TILES - 1], fk[:, 1:TILES], fk[:, 0:TILES - 1])
                V_.tensor_tensor_scan(C.c[0:4, 0, :], C.j[0:4, 0, :], C.m[0:4, 0, :], 0.0, ALU.add, ALU.max).then_inc(dve_own, c.step())
                dve.wait_ge(dve_own, c.n)
                V_.tensor_tensor_scan(C.c[0:4, 1, ::-1], C.j[0:4, 1, ::-1], C.m[0:4, 1, ::-1], 0.0, ALU.add, ALU.max).then_inc(dve_own, c.step())
                dve.wait_ge(dve_own, c.n)
                same(C.j[0:4, 0, 1:TILES], fk[:, 1:TILES], lk[:, 0:TILES - 1])
                V_.tensor_copy(C.m[0:4, 0, 1:TILES], C.c[0:4, 0, 0:TILES - 1]).then_inc(dve_own, c.step())
                dve.wait_ge(dve_own, c.n)
                V_.tensor_copy(C.m[0:4, 1, 0:TILES - 1], C.c[0:4, 1, 1:TILES]).then_inc(dve_own, c.step())
                dve.wait_ge(dve_own, c.n)
                V_.memset(C.c[0:4], -BIG).then_inc(dve_own, c.step())
                dve.wait_ge(dve_own, c.n)
                tt(C.c[0:4, 0, 1:TILES], C.m[0:4, 0, 1:TILES], C.j[0:4, 0, 1:TILES], ALU.add).then_inc(dve_own, c.step())
                dve.wait_ge(dve_own, c.n)
                tt(C.c[0:4, 1, 0:TILES - 1], C.m[0:4, 1, 0:TILES - 1], C.j[0:4, 0, 1:TILES], ALU.add).then_inc(dve_own, c.step())
                dve.wait_ge(dve_own, c.n)
                dve.sem_inc(s.scan_ready, 1)
                dve.wait_ge(s.scan_turned, 1)
                dve.sem_inc(s.scan_turned, -1)
                V_.tensor_copy(C.cT[0:QT].rearrange("p k e h -> p (k e h)"), bank[0:QT, 6, 0:QK * 8]).then_inc(dve_own, c.step())
                dve.wait_ge(dve_own, c.n)
                for k in range(QK):
                    kk = C.k[0:QT, k, :]
                    for e, at in ((0, 0), (1, P - 1)):
                        V_.tensor_scalar(C.b[0:QT], kk, kk[:, at:at + 1], None, ALU.is_equal).then_inc(dve_own, c.step())
                        dve.wait_ge(dve_own, c.n)
                        V_.tensor_scalar(C.b[0:QT], C.b[0:QT], -1.0, BIG, ALU.add, ALU.mult).then_inc(dve_own, c.step())
                        dve.wait_ge(dve_own, c.n)
                        for h in range(4):
                            V_.scalar_tensor_tensor(C.fw[0:QT, k, h, :], C.b[0:QT], C.cT[0:QT, k, e, h:h + 1], C.fw[0:QT, k, h, :],
                                                      ALU.add, ALU.max).then_inc(dve_own, c.step())
                        dve.wait_ge(dve_own, c.n)
                    dve.sem_inc(s.scan_ready, 1)
                    dve.wait_ge(s.scan_turned, 1)
                    dve.sem_inc(s.scan_turned, -1)
                    sc = aux[:, k * QT:(k + 1) * QT, 0:4]
                    tt(sc, sc, bank[:, k % 2, 0:4 * QT].rearrange("p (h t) -> p t h", h=4), ALU.subtract).then_inc(dve_own, c.step())
                    dve.wait_ge(dve_own, c.n)
                    dve.sem_inc(s.scan_free, 1)
                dve.sem_inc(s.scores_shifted, 1)
                dve.wait_ge(dve_own, c.n)
                dve.sem_inc(dve_own, c.reset())
                barrier(dve, "dve")

                def weigh(g, b, first, half):
                    f = SPEC[3]["f"]
                    dve.wait_ge(s.key_in0 if b == 0 else s.key_in1, 16)
                    dve.sem_inc(s.key_in0 if b == 0 else s.key_in1, -16)
                    if not first:
                        dve.wait_ge(s.msg_free, 1)
                        dve.sem_inc(s.msg_free, -1)
                    select(g, b, P2.keys, P2.sel, dst_f)
                    dve.wait_ge(s.attr_in0 if b == 0 else s.attr_in1, 16)
                    dve.sem_inc(s.attr_in0 if b == 0 else s.attr_in1, -16)
                    pp = aux[:, bass.ds(g * GROUP, GROUP), 0:4]
                    msg = P2.msg[:, b, :].rearrange("p (t c) -> p t c", c=f)
                    hh = P2.h[:, b, :].rearrange("p (t c) -> p t c", c=DIM)
                    V_.tensor_copy(msg[:, :, 160:164], pp).then_inc(dve_own, c.step())
                    tt(msg[:, :, 0:S].rearrange("p t (h c) -> p t h c", h=4), hh[:, :, 0:S].rearrange("p t (h c) -> p t h c", h=4),
                         bc(pp, 3, 16), ALU.mult).then_inc(dve_own, c.step())
                    for i in range(3):
                        lo = S + V * i
                        tt(msg[:, :, lo:lo + V].rearrange("p t (h c) -> p t h c", h=4),
                             hh[:, :, lo:lo + V].rearrange("p t (h c) -> p t h c", h=4), bc(pp, 3, 8), ALU.mult).then_inc(dve_own, c.step())
                    dve.wait_ge(dve_own, c.n)
                    dve.sem_inc(dve_own, c.reset())
                    dve.sem_inc(s.msg_ready, 1)
                    dve.sem_inc(s.attr_free, 1)
                    dve.sem_inc(s.key_free, 1)
                pipelined(dve, GROUPS, [(0, weigh)])
                dve.wait_ge(s.msg_free, 2)
                dve.sem_inc(s.msg_free, -2)
                barrier(dve, "dve")
                post(3)
                barrier(dve, "dve")


LOADS = 16 * 12
WEIGHTS = [
    "L0_gnn_W_skip0", "L0_gnn_W_skip1", "L0_gnn_W_nl0", "L0_gnn_W_nl1", "L0_gnn_W_fc1", "L0_gnn_W_fc2",
    "L0_gnn_W_out_s", "L0_gnn_W_out_v", "L1_gnn_W_sc_s", "L1_gnn_W_sc_v", "L1_gnn_W1_s", "L1_gnn_W1_v",
    "L1_gnn_W2_s", "L1_gnn_W2_v", "L1_gnn_W3", "L1_gnn_fcW1", "L1_gnn_fcW2", "L2_gnn_Wfc1", "L2_gnn_Wfc2",
    "L2_gnn_Wsc0", "L2_gnn_Wsc1", "L2_gnn_Wl1_0", "L2_gnn_Wl1_1", "L2_gnn_Wl2_s", "L2_gnn_Wl2_v", "L2_gnn_Wa",
    "L3_gnn_Ws_src", "L3_gnn_Wv_src", "L3_gnn_Ws_dst", "L3_gnn_Wv_dst", "L3_gnn_W_rbf", "L3_gnn_W_alpha",
    "L3_gnn_Ws_val", "L3_gnn_Wv_val", "L3_gnn_Wg", "L3_gnn_Ws_vlin", "L3_gnn_Wv_vlin", "L3_gnn_Wps", "L3_gnn_Wpv",
]
COLUMNS = ["L3_gnn_gamma_s", "L3_gnn_beta_s", "L3_gnn_gamma_v", "L3_gnn_w2_ss", "L3_gnn_w2_sv", "L3_gnn_w2_vs",
           "L3_gnn_w2_vv0", "L3_gnn_w2_vv1"]


def laid_out(inputs):
    import numpy as np

    more = TILES * P - EDGES
    d = {}

    def edges_first(v, fill=0.0):
        v = np.concatenate([v, np.full((more, v.shape[1]), fill, v.dtype)])
        return v.reshape(TILES, P, -1).transpose(1, 0, 2).reshape(P, -1)

    def features_first(v):
        return np.concatenate([v, np.zeros((more, v.shape[1]), v.dtype)]).T

    d["x"] = np.concatenate([inputs["x"], np.zeros((ROWS - NODES, DIM), np.float32)])
    d["node_vec1"] = np.concatenate([inputs["node_vec1"][:, 0], np.zeros(ROWS - NODES, np.float32)]).reshape(P, SLOTS)
    for name in ("src", "dst"):
        v = np.concatenate([inputs[name], np.full(more, PAD_NODE, np.int32)])
        d[name + "_row"] = v
        d[name] = v.reshape(TILES, P).T
    keys = d["dst_row"].reshape(TILES, P)
    d["dst_tiles"] = np.concatenate([keys, np.full((1, P), ROWS, np.int32)])
    d["tile_last"], d["tile_first"] = keys[:, -1], keys[:, 0]
    d["next_first"] = np.concatenate([keys[1:, 0], np.full(1, ROWS, np.int32)])
    d["last_col"] = d["tile_last"].reshape(QK, QT).T
    d["next_col"] = d["next_first"].reshape(QK, QT).T
    d["edge_attr_3"] = edges_first(inputs["edge_attr_3"], 1.0)
    d["edge_attr_4"] = edges_first(inputs["edge_attr_4"]).reshape(P, TILES, 4)
    for k in (8, 16, 64):
        d[f"edge_attr_{k}"] = features_first(inputs[f"edge_attr_{k}"])
    d["Ws_val_T"] = inputs["L3_gnn_Ws_val"].T
    for name in WEIGHTS:
        d[name] = inputs[name]
    for name in COLUMNS:
        d[name] = inputs[name].reshape(-1, 1)
    d["L3_gnn_alpha_dot"] = inputs["L3_gnn_alpha_dot"].reshape(-1)
    return {k: np.ascontiguousarray(v) for k, v in d.items()}


def kernel(**inputs):
    import numpy as np
    import concourse.bacc as bacc
    from concourse.bass_utils import run_bass_kernel_spmd

    nc = bacc.Bacc("TRN2", target_bir_lowering=False, num_devices=1)
    arrays, args = {}, {}
    for name, v in laid_out({k: np.asarray(v) for k, v in inputs.items()}).items():
        arrays["in_" + name] = v
        args[name] = nc.dram_tensor("in_" + name, v.shape, mybir.dt.from_np(v.dtype), kind="ExternalInput").ap()
    out = nc.dram_tensor("out_x", (NODES, DIM), F32, kind="ExternalOutput").ap()
    build(nc, args, out, LAYERS)
    return run_bass_kernel_spmd(nc, [arrays], core_ids=[0]).results[0]["out_x"]


LAYERS = (0, 1, 2, 3)
```
